# Optimizing a Trainium2 kernel written in Bass

```python
import numpy as np
import jax
import jax.numpy as jnp

def _softmax(x, axis=-1):
    return jax.nn.softmax(x, axis=axis)

def _gelu(x):
    return jax.nn.gelu(x, approximate=True)

def _silu(x):
    return jax.nn.silu(x)

def _sigmoid(x):
    return jax.nn.sigmoid(x)

def _layernorm(x, axis=-1, eps=1e-05):
    m = jnp.mean(x, axis=axis, keepdims=True)
    v = jnp.var(x, axis=axis, keepdims=True)
    return (x - m) / jnp.sqrt(v + eps)

def _scatter_add(tgt, idx, src, axis=0):
    return tgt.at[idx].add(src)

def _segment_sum(src, seg, n):
    return jax.ops.segment_sum(src, seg, n)
kernel_name = 'mk_decoder_postln_d2_seqx_r8_49f7e9'

def setup_inputs(seed: int=0):
    np.random.seed(seed)
    _w = jnp.asarray

    def _rec_inputs():
        import jax
        import jax.numpy as jnp
        _rk = jax.random.key(seed)
        x = 7.22e-05 + 1 * jax.random.normal(jax.random.fold_in(_rk, 1), (8, 56, 256), jnp.float32)
        _lenS = 56 - jax.random.randint(jax.random.fold_in(_rk, 7), (8,), 0, max(1, 56 // 4) + 1, jnp.int32)
        _lenS2 = 1500 - jax.random.randint(jax.random.fold_in(_rk, 8), (8,), 0, max(1, 1500 // 4) + 1, jnp.int32)
        _ctx_2048P = jax.random.normal(jax.random.fold_in(_rk, 11), (8, 16, 256), jnp.float32)
        _ctx_2048c = jax.random.dirichlet(jax.random.fold_in(_rk, 511), 0.3 * jnp.ones((16,), jnp.float32), (8, 1500))
        _ctx_2048t = jnp.einsum('bsk,bkd->bsd', _ctx_2048c, _ctx_2048P)
        _ctx_2048t = _ctx_2048t * jax.lax.rsqrt(jnp.mean(jnp.square(_ctx_2048t)) + 1e-12) * 0.953939
        ctx_2048 = -0.000514642 + 1.00011 * (_ctx_2048t + 0.3 * jax.random.normal(jax.random.fold_in(_rk, 611), (8, 1500, 256), jnp.float32))
        _validS = jnp.arange(56)[None, :] < _lenS[:, None]
        _validS2 = jnp.arange(1500)[None, :] < _lenS2[:, None]
        _causal = jnp.tril(jnp.ones((56, 56), dtype=bool))
        mask_BxS2_ik0 = jnp.where(jnp.broadcast_to(_validS2[:, :], (8, 1500)), 0, 1).astype(jnp.int32)
        return (x, ctx_2048, mask_BxS2_ik0)
    x, ctx_2048, mask_BxS2_ik0 = _rec_inputs()

    def _L0_attn_setup():
        import jax, jax.numpy as jnp
        import numpy as np
        N_HEADS = 16
        D_HEAD = 128
        D_MODEL = 256
        MAXLEN = 256
        key = jax.random.key(seed)
        ks = jax.random.split(key, 9)
        b, t = (2, 256)
        hd = N_HEADS * D_HEAD
        init = 0.02
        return {'x': jax.random.normal(ks[0], (b, t, D_MODEL), dtype=jnp.float32), 'Wq': jax.random.normal(ks[1], (D_MODEL, hd), dtype=jnp.float32) * init, 'bq': jnp.zeros((hd,), dtype=jnp.float32), 'Wk': jax.random.normal(ks[2], (D_MODEL, hd), dtype=jnp.float32) * init, 'bk': jnp.zeros((hd,), dtype=jnp.float32), 'Wv': jax.random.normal(ks[3], (D_MODEL, hd), dtype=jnp.float32) * init, 'bv': jnp.zeros((hd,), dtype=jnp.float32), 'Wo': jax.random.normal(ks[4], (hd, D_MODEL), dtype=jnp.float32) * init, 'bo': jnp.zeros((D_MODEL,), dtype=jnp.float32)}
    _L0_attn_all = _L0_attn_setup()
    _L0_attn_in = {k: v for k, v in _L0_attn_all.items() if k in ('Wq', 'bq', 'Wk', 'bk', 'Wv', 'bv', 'Wo', 'bo')}
    del _L0_attn_all

    def _L0_xattn_setup():
        import jax, jax.numpy as jnp
        import numpy as np
        D_MODEL = 256
        NUM_HEADS = 16
        HEAD_DIM = D_MODEL // NUM_HEADS

        def _fq_sym(x, axis):
            s = jnp.max(jnp.abs(x), axis=axis, keepdims=True) / 127.0
            s = jnp.maximum(s, 1e-08)
            q = jnp.clip(jnp.round(x / s), -127.0, 127.0) * s
            return x + jax.lax.stop_gradient(q - x)

        def _fq_unsigned(x, axis):
            s = jnp.max(x, axis=axis, keepdims=True) / 255.0
            s = jnp.maximum(s, 1e-08)
            q = jnp.clip(jnp.round(x / s), 0.0, 255.0) * s
            return x + jax.lax.stop_gradient(q - x)
        key = jax.random.key(seed)
        ks = jax.random.split(key, 8)
        B, N, M, C = (2, 256, 64, D_MODEL)
        return {'x': jax.random.normal(ks[0], (B, N, C), jnp.float32), 'cond': jax.random.normal(ks[1], (B, M, C), jnp.float32), 'Wq': jax.random.normal(ks[2], (C, C), jnp.float32) * 0.02, 'bq': jnp.zeros((C,), jnp.float32), 'Wkv': jax.random.normal(ks[3], (C, 2 * C), jnp.float32) * 0.02, 'bkv': jnp.zeros((2 * C,), jnp.float32), 'Wp': jax.random.normal(ks[4], (C, C), jnp.float32) * 0.02, 'bp': jnp.zeros((C,), jnp.float32)}
    _L0_xattn_all = _L0_xattn_setup()
    _L0_xattn_in = {k: v for k, v in _L0_xattn_all.items() if k in ('Wq', 'bq', 'Wkv', 'bkv', 'Wp', 'bp')}
    del _L0_xattn_all

    def _L0_ffn_setup():
        import jax, jax.numpy as jnp
        import numpy as np
        TOP_K = 2
        key = jax.random.key(seed)
        ks = jax.random.split(key, 5)
        B, S, D, INTER, E = (4, 256, 256, 256, 8)
        x = jax.random.normal(ks[0], (B, S, D), dtype=jnp.float32)
        w1 = jax.random.normal(ks[1], (INTER, D), dtype=jnp.float32) * (1.0 / np.sqrt(D))
        w3 = jax.random.normal(ks[2], (INTER, INTER), dtype=jnp.float32) * (1.0 / np.sqrt(INTER))
        w2 = jax.random.normal(ks[3], (D, INTER), dtype=jnp.float32) * (1.0 / np.sqrt(INTER))
        wr = jax.random.normal(ks[4], (E, D), dtype=jnp.float32) * (1.0 / np.sqrt(D))
        return {'x': x, 'w1': w1, 'w3': w3, 'w2': w2, 'wr': wr}
    _L0_ffn_all = _L0_ffn_setup()
    _L0_ffn_in = {k: v for k, v in _L0_ffn_all.items() if k in ('w1', 'w3', 'w2', 'wr')}
    del _L0_ffn_all

    def _L1_attn_setup():
        import math
        import jax, jax.numpy as jnp
        import numpy as np
        NUM_HEAD = 16
        EMB = 256
        HEAD_DIM = EMB // NUM_HEAD
        B, T = (2, 256)

        def get_slopes(n):
            start = 2 ** (-2 ** (-(math.log2(n) - 3)))
            return np.array([start * start ** i for i in range(n)], dtype=np.float32)
        key = jax.random.key(seed)
        ks = jax.random.split(key, 5)
        x = jax.random.normal(ks[0], (B, T, EMB), jnp.float32)

        def w(k, scale=0.02):
            return jax.random.normal(k, (EMB, EMB), jnp.float32) * scale
        return {'x': x, 'Wq': w(ks[1]), 'bq': jnp.zeros((EMB,), jnp.float32), 'Wk': w(ks[2]), 'bk': jnp.zeros((EMB,), jnp.float32), 'Wv': w(ks[3]), 'bv': jnp.zeros((EMB,), jnp.float32), 'Wo': w(ks[4], scale=0.02 / math.sqrt(24)), 'bo': jnp.zeros((EMB,), jnp.float32)}
    _L1_attn_all = _L1_attn_setup()
    _L1_attn_in = {k: v for k, v in _L1_attn_all.items() if k in ('Wq', 'bq', 'Wk', 'bk', 'Wv', 'bv', 'Wo', 'bo')}
    del _L1_attn_all

    def _L1_xattn_setup():
        import jax, jax.numpy as jnp
        import numpy as np
        import math
        H = 256
        NH = 16
        HD = H // NH
        EPS_LN = 1e-05
        RES_SCALE_MAX = 0.3

        def _nan_clean(x, lim=10000.0):
            return jnp.nan_to_num(x, nan=0.0, posinf=lim, neginf=-lim)
        key = jax.random.key(seed)
        ks = jax.random.split(key, 12)
        B, S, T = (4, 256, 32)
        std = 1.0 / math.sqrt(H)
        return {'hidden_states': jax.random.normal(ks[0], (B, S, H), jnp.float32), 'audio_tokens': jax.random.normal(ks[1], (B, T, H), jnp.float32), 'attention_mask': jax.random.randint(ks[2], (B, T), 0, 2, jnp.int32), 'Wq': jax.random.normal(ks[3], (H, H), jnp.float32) * std, 'bq': jnp.zeros((H,), jnp.float32), 'Wk': jax.random.normal(ks[4], (H, H), jnp.float32) * std, 'bk': jnp.zeros((H,), jnp.float32), 'Wv': jax.random.normal(ks[5], (H, H), jnp.float32) * std, 'bv': jnp.zeros((H,), jnp.float32), 'Wo': jax.random.normal(ks[6], (H, H), jnp.float32) * std, 'bo': jnp.zeros((H,), jnp.float32), 'ln_gamma': jnp.ones((H,), jnp.float32), 'ln_beta': jnp.zeros((H,), jnp.float32), 'residual_scale': jnp.float32(0.05)}
    _L1_xattn_all = _L1_xattn_setup()
    _L1_xattn_in = {k: v for k, v in _L1_xattn_all.items() if k in ('Wq', 'bq', 'Wk', 'bk', 'Wv', 'bv', 'Wo', 'bo', 'ln_gamma', 'ln_beta', 'residual_scale')}
    del _L1_xattn_all

    def _L1_ffn_setup():
        import jax, jax.numpy as jnp
        import numpy as np
        TOP_K = 2
        key = jax.random.key(seed)
        ks = jax.random.split(key, 6)
        B, S, H, F, E = (1, 256, 256, 176, 8)
        Fs = 2 * F
        std = jnp.float32(0.02)
        return {'hidden_states': jax.random.normal(ks[0], (B, S, H), jnp.float32), 'gate_weight': jax.random.normal(ks[1], (E, H), jnp.float32) * std, 'gate_up_weights': jax.random.normal(ks[2], (E, 2 * F, H), jnp.float32) * std, 'down_weights': jax.random.normal(ks[3], (E, H, F), jnp.float32) * std, 'shared_gate_up': jax.random.normal(ks[4], (2 * Fs, H), jnp.float32) * std, 'shared_down': jax.random.normal(ks[5], (H, Fs), jnp.float32) * std}
    _L1_ffn_all = _L1_ffn_setup()
    _L1_ffn_in = {k: v for k, v in _L1_ffn_all.items() if k in ('gate_weight', 'gate_up_weights', 'down_weights', 'shared_gate_up', 'shared_down')}
    del _L1_ffn_all
    return {'x': x, 'ctx_2048': ctx_2048, 'mask_BxS2_ik0': mask_BxS2_ik0, 'L0_attn_Wq': _L0_attn_in['Wq'], 'L0_attn_bq': _L0_attn_in['bq'], 'L0_attn_Wk': _L0_attn_in['Wk'], 'L0_attn_bk': _L0_attn_in['bk'], 'L0_attn_Wv': _L0_attn_in['Wv'], 'L0_attn_bv': _L0_attn_in['bv'], 'L0_attn_Wo': _L0_attn_in['Wo'], 'L0_attn_bo': _L0_attn_in['bo'], 'L0_xattn_Wq': _L0_xattn_in['Wq'], 'L0_xattn_bq': _L0_xattn_in['bq'], 'L0_xattn_Wkv': _L0_xattn_in['Wkv'], 'L0_xattn_bkv': _L0_xattn_in['bkv'], 'L0_xattn_Wp': _L0_xattn_in['Wp'], 'L0_xattn_bp': _L0_xattn_in['bp'], 'L0_ffn_w1': _L0_ffn_in['w1'], 'L0_ffn_w3': _L0_ffn_in['w3'], 'L0_ffn_w2': _L0_ffn_in['w2'], 'L0_ffn_wr': _L0_ffn_in['wr'], 'L1_attn_Wq': _L1_attn_in['Wq'], 'L1_attn_bq': _L1_attn_in['bq'], 'L1_attn_Wk': _L1_attn_in['Wk'], 'L1_attn_bk': _L1_attn_in['bk'], 'L1_attn_Wv': _L1_attn_in['Wv'], 'L1_attn_bv': _L1_attn_in['bv'], 'L1_attn_Wo': _L1_attn_in['Wo'], 'L1_attn_bo': _L1_attn_in['bo'], 'L1_xattn_Wq': _L1_xattn_in['Wq'], 'L1_xattn_bq': _L1_xattn_in['bq'], 'L1_xattn_Wk': _L1_xattn_in['Wk'], 'L1_xattn_bk': _L1_xattn_in['bk'], 'L1_xattn_Wv': _L1_xattn_in['Wv'], 'L1_xattn_bv': _L1_xattn_in['bv'], 'L1_xattn_Wo': _L1_xattn_in['Wo'], 'L1_xattn_bo': _L1_xattn_in['bo'], 'L1_xattn_ln_gamma': _L1_xattn_in['ln_gamma'], 'L1_xattn_ln_beta': _L1_xattn_in['ln_beta'], 'L1_xattn_residual_scale': _L1_xattn_in['residual_scale'], 'L1_ffn_gate_weight': _L1_ffn_in['gate_weight'], 'L1_ffn_gate_up_weights': _L1_ffn_in['gate_up_weights'], 'L1_ffn_down_weights': _L1_ffn_in['down_weights'], 'L1_ffn_shared_gate_up': _L1_ffn_in['shared_gate_up'], 'L1_ffn_shared_down': _L1_ffn_in['shared_down']}

def reference(x, ctx_2048, mask_BxS2_ik0, L0_attn_Wq, L0_attn_bq, L0_attn_Wk, L0_attn_bk, L0_attn_Wv, L0_attn_bv, L0_attn_Wo, L0_attn_bo, L0_xattn_Wq, L0_xattn_bq, L0_xattn_Wkv, L0_xattn_bkv, L0_xattn_Wp, L0_xattn_bp, L0_ffn_w1, L0_ffn_w3, L0_ffn_w2, L0_ffn_wr, L1_attn_Wq, L1_attn_bq, L1_attn_Wk, L1_attn_bk, L1_attn_Wv, L1_attn_bv, L1_attn_Wo, L1_attn_bo, L1_xattn_Wq, L1_xattn_bq, L1_xattn_Wk, L1_xattn_bk, L1_xattn_Wv, L1_xattn_bv, L1_xattn_Wo, L1_xattn_bo, L1_xattn_ln_gamma, L1_xattn_ln_beta, L1_xattn_residual_scale, L1_ffn_gate_weight, L1_ffn_gate_up_weights, L1_ffn_down_weights, L1_ffn_shared_gate_up, L1_ffn_shared_down):
    import jax
    import jax.numpy as jnp

    def _L0_attn_ref(x, Wq, bq, Wk, bk, Wv, bv, Wo, bo):
        import jax, jax.numpy as jnp
        import numpy as np
        N_HEADS = 16
        D_HEAD = 128
        D_MODEL = 256
        MAXLEN = 256
        b, t, _ = x.shape
        h, dh = (N_HEADS, D_HEAD)
        scale = 1.0 / np.sqrt(dh).astype(np.float32)
        q = (x @ Wq + bq).reshape(b, h, t, dh)
        k = (x @ Wk + bk).reshape(b, t, h, dh).transpose(0, 2, 3, 1)
        v = (x @ Wv + bv).reshape(b, t, h, dh).transpose(0, 2, 1, 3)
        logits = jnp.einsum('bhtd,bhds->bhts', q, k) * scale
        mask = jnp.triu(jnp.full((t, t), -jnp.inf, dtype=x.dtype), k=1)
        weights = jax.nn.softmax(logits + mask, axis=-1)
        out = jnp.einsum('bhts,bhsd->bhtd', weights, v)
        out = out.transpose(0, 2, 1, 3).reshape(b, t, h * dh)
        return out @ Wo + bo

    def _L0_xattn_ref(x, cond, Wq, bq, Wkv, bkv, Wp, bp):
        import jax, jax.numpy as jnp
        import numpy as np
        D_MODEL = 256
        NUM_HEADS = 16
        HEAD_DIM = D_MODEL // NUM_HEADS

        def _fq_sym(x, axis):
            s = jnp.max(jnp.abs(x), axis=axis, keepdims=True) / 127.0
            s = jnp.maximum(s, 1e-08)
            q = jnp.clip(jnp.round(x / s), -127.0, 127.0) * s
            return x + jax.lax.stop_gradient(q - x)

        def _fq_unsigned(x, axis):
            s = jnp.max(x, axis=axis, keepdims=True) / 255.0
            s = jnp.maximum(s, 1e-08)
            q = jnp.clip(jnp.round(x / s), 0.0, 255.0) * s
            return x + jax.lax.stop_gradient(q - x)
        B, N, C = x.shape
        H, hd = (NUM_HEADS, HEAD_DIM)
        q = (x @ Wq + bq).reshape(1, B * N, H, hd)
        kv = (cond @ Wkv + bkv).reshape(1, -1, 2, H, hd)
        k, v = (kv[:, :, 0], kv[:, :, 1])
        scale = 1.0 / np.sqrt(hd).astype(np.float32)
        q = jnp.transpose(q * scale, (0, 2, 1, 3))
        k = jnp.transpose(k, (0, 2, 1, 3))
        v = jnp.transpose(v, (0, 2, 1, 3))
        q = _fq_sym(q, axis=-1)
        k = _fq_sym(k, axis=-1)
        v = _fq_sym(v, axis=2)
        attn = jnp.einsum('bhqd,bhkd->bhqk', q, k)
        attn = jax.nn.softmax(attn.astype(jnp.float32), axis=-1)
        attn = _fq_unsigned(attn, axis=-1)
        out = jnp.einsum('bhqk,bhkd->bhqd', attn, v)
        out = jnp.transpose(out, (0, 2, 1, 3)).reshape(B, N, C)
        return out @ Wp + bp

    def _L0_ffn_ref(x, w1, w3, w2, wr):
        import jax, jax.numpy as jnp
        import numpy as np
        TOP_K = 2
        B, S, D = x.shape
        xr = x.reshape(-1, D)
        route_probs = jax.nn.softmax(xr @ wr.T, axis=-1)
        routes_k, indices_k = jax.lax.top_k(route_probs, TOP_K)
        gates = routes_k / jnp.sum(routes_k, axis=-1, keepdims=True)
        h = jax.nn.silu(xr @ w1.T)
        h = jax.nn.silu(h @ w3.T)
        h = h @ w2.T
        out = jnp.zeros_like(xr)
        for k in range(TOP_K):
            out = out.at[indices_k[:, k]].add(gates[:, k:k + 1] * h)
        return out.reshape(B, S, D)

    def _L1_attn_ref(x, Wq, bq, Wk, bk, Wv, bv, Wo, bo):
        import math
        import jax, jax.numpy as jnp
        import numpy as np
        NUM_HEAD = 16
        EMB = 256
        HEAD_DIM = EMB // NUM_HEAD
        B, T = (2, 256)

        def get_slopes(n):
            start = 2 ** (-2 ** (-(math.log2(n) - 3)))
            return np.array([start * start ** i for i in range(n)], dtype=np.float32)
        Bx, Tx, C = x.shape
        slopes = jnp.asarray(get_slopes(NUM_HEAD))

        def split_heads(y):
            return y.reshape(Bx, Tx, NUM_HEAD, HEAD_DIM).transpose(0, 2, 1, 3)
        q = split_heads(x @ Wq + bq)
        k = split_heads(x @ Wk + bk)
        v = split_heads(x @ Wv + bv)
        attn = jnp.einsum('bhqd,bhkd->bhqk', q, k) / jnp.sqrt(jnp.float32(HEAD_DIM))
        alibi = -slopes[:, None, None] * (Tx - 1 - jnp.arange(Tx, dtype=jnp.float32))[None, None, :]
        attn = attn + alibi
        causal = jnp.tril(jnp.ones((Tx, Tx), dtype=bool))[None, None]
        attn = jnp.where(causal, attn, jnp.finfo(jnp.float32).min)
        p = jax.nn.softmax(attn, axis=-1)
        out = jnp.einsum('bhqk,bhkd->bhqd', p, v).transpose(0, 2, 1, 3).reshape(Bx, Tx, C)
        return out @ Wo + bo

    def _L1_xattn_ref(hidden_states, audio_tokens, attention_mask, Wq, bq, Wk, bk, Wv, bv, Wo, bo, ln_gamma, ln_beta, residual_scale):
        import jax, jax.numpy as jnp
        import numpy as np
        import math
        H = 256
        NH = 16
        HD = H // NH
        EPS_LN = 1e-05
        RES_SCALE_MAX = 0.3

        def _nan_clean(x, lim=10000.0):
            return jnp.nan_to_num(x, nan=0.0, posinf=lim, neginf=-lim)
        B, S, _ = hidden_states.shape
        T = audio_tokens.shape[1]
        hs = _nan_clean(hidden_states).astype(jnp.float32)
        at = _nan_clean(audio_tokens).astype(jnp.float32)

        def proj(x, W, b, L):
            y = x @ W.T + b
            return y.reshape(B, L, NH, HD).transpose(0, 2, 1, 3)
        q = _nan_clean(proj(hs, Wq, bq, S))
        k = _nan_clean(proj(at, Wk, bk, T))
        v = _nan_clean(proj(at, Wv, bv, T))
        scale = max(math.sqrt(HD), 1e-08)
        scores = jnp.einsum('bhsd,bhtd->bhst', q, k) / scale
        scores = jnp.clip(scores, -50.0, 50.0)
        scores = jnp.nan_to_num(scores, nan=0.0, posinf=50.0, neginf=-50.0)
        attend = (attention_mask.astype(jnp.float32) > 0.5)[:, None, None, :]
        scores = jnp.where(attend, scores, -10000.0)
        scores = jnp.clip(scores, -50.0, 50.0)
        probs = jax.nn.softmax(scores, axis=-1)
        probs = jnp.nan_to_num(probs, nan=0.0, posinf=1.0, neginf=0.0)
        probs = probs / (probs.sum(axis=-1, keepdims=True) + 1e-08)
        ctx = jnp.einsum('bhst,bhtd->bhsd', probs, v)
        ctx = ctx.transpose(0, 2, 1, 3).reshape(B, S, H)
        delta = _nan_clean(ctx @ Wo.T + bo)
        rs = jnp.clip(residual_scale, 0.0, RES_SCALE_MAX)
        delta = rs * delta
        mu = delta.mean(axis=-1, keepdims=True)
        var = jnp.mean((delta - mu) ** 2, axis=-1, keepdims=True)
        delta = (delta - mu) / jnp.sqrt(var + EPS_LN) * ln_gamma + ln_beta
        return delta

    def _L1_ffn_ref(hidden_states, gate_weight, gate_up_weights, down_weights, shared_gate_up, shared_down):
        import jax, jax.numpy as jnp
        import numpy as np
        TOP_K = 2
        B, S, H = hidden_states.shape
        E, twoF, _ = gate_up_weights.shape
        F = twoF // 2
        T = B * S
        x = hidden_states.reshape(T, H)
        logits = x @ gate_weight.T
        scores = jax.nn.softmax(logits, axis=-1)
        topk_w, topk_idx = jax.lax.top_k(scores, TOP_K)
        combine = jnp.zeros((T, E), x.dtype).at[jnp.arange(T)[:, None], topk_idx].add(topk_w)
        gu = jnp.einsum('th,efh->tef', x, gate_up_weights)
        act = jax.nn.silu(gu[..., :F]) * gu[..., F:]
        y = jnp.einsum('tef,te,ehf->th', act, combine, down_weights)
        Fs = shared_gate_up.shape[0] // 2
        sgu = x @ shared_gate_up.T
        sact = jax.nn.silu(sgu[:, :Fs]) * sgu[:, Fs:]
        y = y + sact @ shared_down.T
        return y.reshape(B, S, H)
    x = _layernorm(x + _L0_attn_ref(x, L0_attn_Wq, L0_attn_bq, L0_attn_Wk, L0_attn_bk, L0_attn_Wv, L0_attn_bv, L0_attn_Wo, L0_attn_bo), axis=-1)
    x = _layernorm(x + _L0_xattn_ref(x, ctx_2048, L0_xattn_Wq, L0_xattn_bq, L0_xattn_Wkv, L0_xattn_bkv, L0_xattn_Wp, L0_xattn_bp), axis=-1)
    x = _layernorm(x + _L0_ffn_ref(x, L0_ffn_w1, L0_ffn_w3, L0_ffn_w2, L0_ffn_wr), axis=-1)
    x = _layernorm(x + _L1_attn_ref(x, L1_attn_Wq, L1_attn_bq, L1_attn_Wk, L1_attn_bk, L1_attn_Wv, L1_attn_bv, L1_attn_Wo, L1_attn_bo), axis=-1)
    x = _layernorm(x + _L1_xattn_ref(x, ctx_2048, mask_BxS2_ik0, L1_xattn_Wq, L1_xattn_bq, L1_xattn_Wk, L1_xattn_bk, L1_xattn_Wv, L1_xattn_bv, L1_xattn_Wo, L1_xattn_bo, L1_xattn_ln_gamma, L1_xattn_ln_beta, L1_xattn_residual_scale), axis=-1)
    x = _layernorm(x + _L1_ffn_ref(x, L1_ffn_gate_weight, L1_ffn_gate_up_weights, L1_ffn_down_weights, L1_ffn_shared_gate_up, L1_ffn_shared_down), axis=-1)
    return x

_drawn_inputs = setup_inputs


def setup_inputs(seed=0):
    import zlib

    import numpy as np

    out = dict(_drawn_inputs(seed))
    spreads = {'L0_attn_bq': (0.0, 0.8),
     'L0_attn_bk': (0.0, 0.8),
     'L0_attn_bv': (0.0, 0.1),
     'L0_attn_bo': (0.0, 0.1),
     'L0_xattn_bq': (0.0, 0.8),
     'L0_xattn_bkv': (0.0, 0.32),
     'L0_xattn_bp': (0.0, 0.1),
     'L1_attn_bq': (0.0, 0.8),
     'L1_attn_bk': (0.0, 0.8),
     'L1_attn_bv': (0.0, 0.8),
     'L1_attn_bo': (0.0, 0.1),
     'L1_xattn_bq': (0.0, 0.275),
     'L1_xattn_bk': (0.0, 0.8),
     'L1_xattn_bv': (0.0, 0.1),
     'L1_xattn_bo': (0.0, 0.1),
     'L1_xattn_ln_gamma': (1.0, 0.2),
     'L1_xattn_ln_beta': (0.0, 0.1)}
    factors = {'L0_attn_Wq': 8.0,
     'L0_attn_Wk': 8.0,
     'L0_xattn_Wq': 8.0,
     'L0_xattn_Wkv': 4.69,
     'L1_attn_Wq': 8.0,
     'L1_attn_Wk': 8.0,
     'L1_attn_Wv': 8.0,
     'L1_attn_Wo': 6.589,
     'L1_ffn_gate_weight': 8.0,
     'L1_ffn_gate_up_weights': 8.0,
     'L1_ffn_down_weights': 8.0,
     'L1_ffn_shared_gate_up': 2.853,
     'L1_ffn_shared_down': 2.776}
    for name, (base, spread) in spreads.items():
        noise = np.random.default_rng([zlib.crc32(name.encode()), seed]).standard_normal(out[name].shape)
        drawn = base * np.exp(spread * noise) if base else spread * noise
        out[name] = jnp.asarray(drawn.astype(out[name].dtype))
    for name, factor in factors.items():
        out[name] = (out[name] * factor).astype(out[name].dtype)
    return out
```

```python
from contextlib import ExitStack

import numpy as np
import concourse.bass as bass
from concourse import mybir
from concourse.alu_op_type import AluOpType as ALU

F32 = mybir.dt.float32
BF16 = mybir.dt.bfloat16
I16 = mybir.dt.int16
I32 = mybir.dt.int32
U32 = mybir.dt.uint32
ACT = mybir.ActivationFunctionType
AX = mybir.AxisListType

B, T, D, S = 8, 56, 256, 1500
TOKENS = B * T
TP = 2 * T
TT = TOKENS // TP
C2 = D // 128
KEYS = B * S
KP = 125
KT = KEYS // KP
H = 16
HD = D // H
DH0 = 128
EPS = 1e-5
LN255 = float(np.log(255.0))
MASKED = -1e30
E, F, FS = 8, 176, 352
UNIT = 2 * KP
V_STEP = 2
UNITS = KEYS // UNIT
P1_KEYS = 1000
P1_STEPS = KEYS // P1_KEYS
HEAD_STEPS = 48
PARTS = (0, 1, 2, 0, 1, 0)
K_PARTS = (0, 0, 0, 1, 1, 2)
QK_ROWS = 16 * len(PARTS)


class Core:

    def __init__(self, nc, ctx):
        self.nc, self.ctx = nc, ctx
        self.held = []

    def sem(self, name):
        self.held.append(self.nc.alloc_semaphore(name))
        return self.held[-1]

    def renew_sems(self):
        with self.nc.Block() as block:

            @block.gpsimd
            def _(pool):
                for sem in self.held:
                    pool.sem_clear(sem)

        for sem in self.held:
            self.nc.release_semaphore(sem)
        self.held = []

    def sems(self, prefix, names):
        return {n: self.sem(f"{prefix}_{n}") for n in names.split()}


def linker(engine, sem):
    done = [0]

    def link(instruction):
        done[0] += 1
        instruction.then_inc(sem, 1)
        engine.wait_ge(sem, done[0])

    return link


def bcast(ap, shape):
    return ap.broadcast_to(shape)


NORM_SEMS = "var_ready std_ready x_ready xT_psum xT_ready"


def norm_vector(nc, dve, link, k, s, y):
    link(nc.vector.tensor_tensor(k.sum[:], y, k.res[:], ALU.add))
    for t in range(TT):
        last = nc.vector.bn_stats(k.stats[:, t, :], k.sum[:, t, :])
    link(last)
    for t in range(TT):
        last = nc.vector.bn_aggr(k.mv[:, t, :], k.stats[:, t, :])
    last.then_inc(s["var_ready"], 1)
    dve.wait_ge(s["std_ready"], 1)
    link(nc.vector.reciprocal(k.rstd[:], k.std[:]))
    for t in range(TT):
        last = nc.vector.tensor_scalar(k.x_tok[:, t, :], k.sum[:, t, :], k.mv[:, t, 0:1],
                                       k.rstd[:, t:t + 1], ALU.subtract, ALU.mult)
    last.then_inc(s["x_ready"], 1)


def norm_scalar(nc, act, k, s, xT_psum):
    act.wait_ge(s["var_ready"], 1)
    nc.scalar.activation(k.std[:], k.mv[:, :, 1], ACT.Sqrt, bias=EPS).then_inc(s["std_ready"], 1)
    act.wait_ge(s["xT_psum"], 1)
    nc.scalar.activation(k.x_T[:], xT_psum, ACT.Copy).then_inc(s["xT_ready"], 1)


def transpose_rows(nc, k, out, rows):
    for c in range(C2):
        for t in range(TT):
            last = nc.tensor.transpose(out[:, c, t * TP:(t + 1) * TP],
                                       rows[:, t, c * 128:(c + 1) * 128], k.ident[0:TP, 0:TP])
    return last


def norm_tensor(nc, pe, k, s, xT_psum):
    pe.wait_ge(s["x_ready"], 1)
    transpose_rows(nc, k, xT_psum, k.x_tok).then_inc(s["xT_psum"], 1)


ATT_SEMS = ("s_ready t_link shifted exp_done p_ready pT_ready pT_sbuf o_ready o_sbuf")
GROUPS = TT * H // 4


def attention_tensor(nc, pe, k, s, score_operands, value_product, sc, pt, o):
    for g in range(GROUPS + 3):
        if g < GROUPS:
            p, heads = g // 4, range(4 * (g % 4), 4 * (g % 4) + 4)
            if g >= 2:
                pe.wait_ge(s["shifted"], g - 1)
            for j, h in enumerate(heads):
                q, kk = score_operands(p, h)
                last = nc.tensor.matmul(sc[g % 2][0:TP, j * TP:(j + 1) * TP], q, kk,
                                        start=True, stop=True)
            last.then_inc(s["s_ready"], 1)
        if 2 <= g <= GROUPS + 1:
            i = g - 2
            pe.wait_ge(s["p_ready"], i + 1)
            if i >= 2:
                pe.wait_ge(s["pT_sbuf"], i - 1)
            for j in range(4):
                last = nc.tensor.transpose(pt[i % 2][0:TP, j * TP:(j + 1) * TP],
                                           k.prob[:, i % 2, j, :], k.ident[0:TP, 0:TP])
            last.then_inc(s["pT_ready"], 1)
        if g >= 3:
            i = g - 3
            pe.wait_ge(s["pT_sbuf"], i + 1)
            if i >= 2:
                pe.wait_ge(s["o_sbuf"], i - 1)
            for j in range(4):
                h = 4 * (i % 4) + j
                last = value_product(o[i % 2], i // 4, h, j, k.probT[:, i % 2, j, :])
            last.then_inc(s["o_ready"], 1)


def attention_vector(nc, dve, k, s, add_term, sc):
    n = [0]

    def link(ins):
        n[0] += 1
        ins.then_inc(s["t_link"], 1)
        dve.wait_ge(s["t_link"], n[0])

    for g in range(GROUPS + 1):
        if g < GROUPS:
            dve.wait_ge(s["s_ready"], g + 1)
            if g >= 2:
                dve.wait_ge(s["exp_done"], g - 1)
            n[0] += 1
            add_term(g, k.shift[:, g % 2, :, :], sc[g % 2]).then_inc(s["t_link"], 1)
            dve.wait_ge(s["t_link"], n[0])
            link(nc.vector.tensor_reduce(k.row[:, 0:4], k.shift[:, g % 2], AX.X, ALU.max, negate=True))
            nc.vector.tensor_tensor(k.shift[:, g % 2], k.shift[:, g % 2],
                                    bcast(k.row[:, 0:4].unsqueeze(2), [TP, 4, TP]),
                                    ALU.add).then_inc(s["shifted"], 1)
        if g >= 1:
            i = g - 1
            dve.wait_ge(s["exp_done"], i + 1)
            link(nc.vector.tensor_reduce(k.row[:, 4:8], k.expo[:, i % 2], AX.X, ALU.add))
            link(nc.vector.reciprocal(k.row[:, 8:12], k.row[:, 4:8]))
            if i >= 2:
                dve.wait_ge(s["pT_ready"], i - 1)
            nc.vector.tensor_tensor(k.prob[:, i % 2], k.expo[:, i % 2],
                                    bcast(k.row[:, 8:12].unsqueeze(2), [TP, 4, TP]),
                                    ALU.mult).then_inc(s["p_ready"], 1)


def attention_scalar(nc, act, k, s, scale, pt, o, place_output):
    for g in range(GROUPS + 3):
        if g < GROUPS:
            act.wait_ge(s["shifted"], g + 1)
            if g >= 2:
                act.wait_ge(s["p_ready"], g - 1)
            nc.scalar.activation(k.expo[:, g % 2], k.shift[:, g % 2], ACT.Exp,
                                 scale=scale).then_inc(s["exp_done"], 1)
        if 2 <= g <= GROUPS + 1:
            i = g - 2
            act.wait_ge(s["pT_ready"], i + 1)
            if i >= 2:
                act.wait_ge(s["o_ready"], i - 1)
            nc.scalar.activation(k.probT[:, i % 2], pt[i % 2][0:TP, 0:4 * TP].rearrange(
                "p (j t) -> p j t", j=4), ACT.Copy).then_inc(s["pT_sbuf"], 1)
        if g >= 3:
            i = g - 3
            act.wait_ge(s["o_ready"], i + 1)
            place_output(i, o[i % 2]).then_inc(s["o_sbuf"], 1)


def attention_buffers(nc, ctx, k):
    buffer = lambda name: ctx.enter_context(nc.sbuf_tensor(f"{name}_{k.phase}", [TP, 2, 4, TP], F32))
    k.shift, k.expo, k.prob, k.probT = buffer("shift"), buffer("expo"), buffer("prob"), buffer("probT")
    k.row = ctx.enter_context(nc.sbuf_tensor(f"row_{k.phase}", [TP, 12], F32))


def layer0_attention(nc, k, d):
    k.phase = "a0"
    with ExitStack() as ctx:
        sb = lambda n, sh, dt=F32: ctx.enter_context(nc.sbuf_tensor(n, sh, dt))
        w = sb("a0_w", [128, 3, C2, H * DH0])
        wo = sb("a0_wo", [128, H, D])
        bqk = sb("a0_bqk", [128, 2, H])
        bv = sb("a0_bv", [TP, H * DH0])
        q_T = sb("a0_qT", [128, TOKENS, H])
        q_pair = sb("a0_qpair", [128, 2, 4, TP])
        k_T = sb("a0_kT", [128, H, TOKENS])
        v = sb("a0_v", [TP, TT, H * DH0])
        mask = sb("a0_mask", [TP, TP])
        bo = sb("a0_bo", [TP, D])
        attention_buffers(nc, ctx, k)
        o_T = w[:].rearrange("p a c n -> p (a c n)")[:, 0:H * TOKENS].rearrange("p (h n) -> p h n", h=H)
        ps = ctx.enter_context(nc.psum_tensor("a0_ps", [128, 8, 512], F32))
        s = k.sems("a0", "x wq wk wv wo bias qk_ready q_evac k_evac v_ready v_evac idm mask res y q_pair "
                   + ATT_SEMS + " " + NORM_SEMS)
        y = ps[0:TP, 6:8, :].rearrange("p b (t n) -> p (b t) n", n=D)
        sc, pt, o = [ps[:, i, :] for i in (0, 1)], [ps[:, i, :] for i in (2, 3)], [ps[:, i, :] for i in (4, 5)]
        with nc.Block() as block:

            @block.sync
            def _(sp):
                sp.dma_start(k.x_T[:], d["x_T"].rearrange("(c p) n -> p c n", p=128)).then_inc(s["x"], 16)
                sp.dma_start(w[:, 0], d["a0_Wq"].rearrange("(c p) n -> p c n", p=128)).then_inc(s["wq"], 16)
                sp.dma_start(w[:, 1], d["a0_Wk"].rearrange("(c p) n -> p c n", p=128)).then_inc(s["wk"], 16)
                sp.dma_start(w[:, 2], d["a0_Wv"].rearrange("(c p) n -> p c n", p=128)).then_inc(s["wv"], 16)
                sp.dma_start(wo[:], d["a0_Wo"].rearrange("(h p) n -> p h n", p=128)).then_inc(s["wo"], 16)

            @block.gpsimd
            def _(pool):
                nc.gpsimd.memset(k.ident[:], 0.0).then_inc(s["idm"], 1)
                pool.wait_ge(s["idm"], 1)
                nc.gpsimd.affine_select(out=k.ident[:], in_=k.ident[:], compare_op=ALU.not_equal, fill=1.0,
                                        base=0, pattern=[[-1, 128]], channel_multiplier=1).then_inc(s["idm"], 1)
                pool.wait_ge(s["idm"], 2)
                nc.gpsimd.tensor_copy(k.ident_b[:], k.ident[:]).then_inc(s["idm"], 1)
                nc.gpsimd.memset(mask[:], 0.0).then_inc(s["idm"], 1)
                pool.wait_ge(s["idm"], 4)
                nc.gpsimd.affine_select(out=mask[:], in_=mask[:], compare_op=ALU.is_ge, fill=MASKED, base=0,
                                        pattern=[[-1, TP]], channel_multiplier=1).then_inc(s["idm"], 1)
                pool.wait_ge(s["idm"], 5)
                nc.gpsimd.affine_select(out=mask[:, 0:T], in_=mask[:, 0:T], compare_op=ALU.is_ge, fill=MASKED,
                                        base=T - 1, pattern=[[0, T]], channel_multiplier=-1)\
                    .then_inc(s["mask"], 1)
                q_flat = q_T[:].rearrange("p (b r) h -> p b (r h)", b=B)
                pool.wait_ge(s["q_evac"], H)
                for g in range(GROUPS):
                    p, h = g // 4, 4 * (g % 4)
                    if g >= 2:
                        pool.wait_ge(s["s_ready"], g - 1)
                    nc.gpsimd.tensor_copy(q_pair[:, g % 2].rearrange("p j (b t) -> p b j t", b=2),
                                          q_flat[:, 2 * p:2 * p + 2, h * T:(h + 4) * T].rearrange(
                                              "p b (j t) -> p b j t", j=4)).then_inc(s["q_pair"], 1)

            @block.tensor
            def _(pe):
                pe.wait_ge(s["x"], 16)
                pe.wait_ge(s["wq"], 16)
                pe.wait_ge(s["wk"], 16)
                for h in range(H):
                    for n in range(2):
                        if h >= 2:
                            pe.wait_ge(s["k_evac" if n else "q_evac"], h - 1)
                        for c in range(C2):
                            last = nc.tensor.matmul(ps[:, 2 * (h % 2) + n, 0:TOKENS],
                                                    w[:, n, c, h * DH0:(h + 1) * DH0], k.x_T[:, c, :],
                                                    start=(c == 0), stop=(c == C2 - 1))
                        last.then_inc(s["qk_ready"], 1)
                pe.wait_ge(s["wv"], 16)
                for i in range(TT * 4):
                    t, n = i // 4, i % 4
                    if i >= 2:
                        pe.wait_ge(s["v_evac"], i - 1)
                    for c in range(C2):
                        last = nc.tensor.matmul(ps[0:TP, 4 + i % 2, :], k.x_T[:, c, t * TP:(t + 1) * TP],
                                                w[:, 2, c, n * 512:(n + 1) * 512],
                                                start=(c == 0), stop=(c == C2 - 1))
                    last.then_inc(s["v_ready"], 1)
                pe.wait_ge(s["q_evac"], H)
                pe.wait_ge(s["k_evac"], H)
                pe.wait_ge(s["v_evac"], 4 * TT)
                pe.wait_ge(s["idm"], 3)

                def score_operands(p, h):
                    g = 4 * p + h // 4
                    if h % 4 == 0:
                        pe.wait_ge(s["q_pair"], g + 1)
                    return q_pair[:, g % 2, h % 4, :], k_T[:, h, p * TP:(p + 1) * TP]

                def value_product(out, p, h, j, probs):
                    return nc.tensor.matmul(out[:, j * TP:(j + 1) * TP], v[:, p, h * DH0:(h + 1) * DH0], probs,
                                            start=True, stop=True)

                attention_tensor(nc, pe, k, s, score_operands, value_product, sc, pt, o)
                pe.wait_ge(s["wo"], 16)
                pe.wait_ge(s["o_sbuf"], GROUPS)
                for t in range(TT):
                    for h in range(H):
                        last = nc.tensor.matmul(y[:, t, :], o_T[:, h, t * TP:(t + 1) * TP], wo[:, h, :],
                                                start=(h == 0), stop=(h == H - 1))
                last.then_inc(s["y"], 1)
                norm_tensor(nc, pe, k, s, ps[:, 0:2, 0:TOKENS])

            @block.scalar
            def _(act):
                act.dma_start(bqk[:], d["a0_bqk"]).then_inc(s["bias"], 16)
                act.dma_start(bv[:], d["a0_bv"].partition_broadcast(TP)).then_inc(s["bias"], 16)
                act.dma_start(bo[:], d["a0_bo"].partition_broadcast(TP)).then_inc(s["bias"], 16)
                act.dma_start(k.x_tok[:], d["x"].rearrange("(t p) n -> p t n", p=TP)).then_inc(s["bias"], 16)
                act.wait_ge(s["bias"], 64)
                for h in range(H):
                    act.wait_ge(s["qk_ready"], 2 * h + 1)
                    nc.scalar.activation(q_T[:, :, h], ps[:, 2 * (h % 2), 0:TOKENS], ACT.Identity,
                                         bias=bqk[:, 0, h:h + 1]).then_inc(s["q_evac"], 1)

                def place_output(g, bank):
                    h = 4 * (g % 4)
                    return nc.scalar.activation(
                        o_T[:, h:h + 4, (g // 4) * TP:(g // 4 + 1) * TP],
                        bank[:, 0:4 * TP].rearrange("p (j t) -> p j t", j=4), ACT.Copy)

                attention_scalar(nc, act, k, s, float(1.0 / np.sqrt(DH0)), pt, o, place_output)
                norm_scalar(nc, act, k, s, ps[:, 0:2, 0:TOKENS])

            @block.vector
            def _(dve):
                link = linker(dve, s["res"])
                dve.wait_ge(s["bias"], 64)
                link(nc.vector.tensor_tensor(k.res[:], k.x_tok[:],
                                             bcast(bo[:].unsqueeze(1), [TP, TT, D]), ALU.add))
                for h in range(H):
                    dve.wait_ge(s["qk_ready"], 2 * h + 2)
                    nc.vector.tensor_scalar(k_T[:, h, :], ps[:, 2 * (h % 2) + 1, 0:TOKENS],
                                            bqk[:, 1, h:h + 1], None, ALU.add).then_inc(s["k_evac"], 1)
                for i in range(TT * 4):
                    t, n = i // 4, i % 4
                    dve.wait_ge(s["v_ready"], i + 1)
                    nc.vector.tensor_tensor(v[:, t, n * 512:(n + 1) * 512], ps[0:TP, 4 + i % 2, :],
                                            bv[:, n * 512:(n + 1) * 512], ALU.add).then_inc(s["v_evac"], 1)
                dve.wait_ge(s["mask"], 1)

                def add_term(g, out, scores):
                    return nc.vector.tensor_tensor(out, scores[0:TP, 0:4 * TP].rearrange("p (j t) -> p j t", j=4),
                                                   bcast(mask[:].unsqueeze(1), [TP, 4, TP]), ALU.add)

                attention_vector(nc, dve, k, s, add_term, sc)
                dve.wait_ge(s["y"], 1)
                norm_vector(nc, dve, link, k, s, y)


def layer0_context(nc, k, d):
    with ExitStack() as ctx:
        sb = lambda n, sh, dt=F32: ctx.enter_context(nc.sbuf_tensor(n, sh, dt))
        w = sb("b0_w", [128, C2, 2 * D])
        bias_rows = sb("b0_bias_rows", [3, 2 * D], BF16)
        ones = sb("b0_ones", [3, KP], BF16)
        rows = sb("b0_ctx", [128, 3, C2, UNIT])
        k_max = sb("b0_kmax", [KP, 2, H * 2])
        k_scale = sb("b0_kscale", [KP, 3, H * 2])
        k_inv = sb("b0_kinv", [KP, H * 2])
        k_steps = sb("b0_ksteps", [KP, 2, 2, D], I16)
        k_back = sb("b0_kback", [KP, 3, 2, D])
        residue = sb("b0_residue", [128, 2, C2 * UNIT])
        parts = sb("b0_parts", [128, 3, 3, C2, 2 * UNIT], BF16)
        v_rows = sb("b0_v", [KP, KT, D])
        early = v_rows[0:1, :, :].rearrange("p t n -> p (t n)")
        bias = early[:, 0:2 * D]
        rest = early[:, 2 * D:6 * D].rearrange("p (i n) -> p i n", i=2)
        bias_parts = early[:, 6 * D:9 * D].bitcast(BF16).rearrange("p (i n) -> p i n", i=3)
        v_max = sb("b0_vmax", [KP, D])
        v_unit = sb("b0_vunit", [KP, D])
        v_all = sb("b0_vall", [KP, 2, D])
        v_int = k_steps
        ps = ctx.enter_context(nc.psum_tensor("b0_ps", [128, 8, 512], F32))
        s = k.sems("b0", "w bias split bias_rows ones l0 l1 l2 kv k_read v_read link k_scale k_int k_float k_back kT hi "
                   "residue mid lo stored vlink vint vsteps vzero")
        loaded = [s["l0"], s["l1"], s["l2"]]
        ctx_T = d["ctx_T"].rearrange("(c p) n -> p c n", p=128)
        kd = k.k_parts
        IN_LOOP = 6
        ROUNDS = UNITS // IN_LOOP

        def rounds(engine, step, flush=lambda r: None):
            for r in range(2):
                for u in range(IN_LOOP):
                    step(r, u)
            with engine.Fori(2, ROUNDS) as r:
                for u in range(IN_LOOP):
                    step(r, u)
            flush(ROUNDS)

        def behind(work, r, u, lag):
            if u >= lag:
                work(r, u - lag)
            elif not (isinstance(r, int) and r == 0):
                work(r - 1, u - lag + IN_LOOP)

        def wait_unit(engine, sem, r, u, lag=0, per_unit=1):
            if isinstance(r, int) and r * IN_LOOP + u < lag:
                return
            engine.wait_ge(sem, per_unit * (r * IN_LOOP + (u - lag + 1)))

        with nc.Block() as block:

            @block.sync
            def _(sp):
                sp.dma_start(w[:], d["c0_Wkv"].rearrange("(c p) n -> p c n", p=128)).then_inc(s["w"], 16)
                sp.dma_start(bias, d["c0_bkv"]).then_inc(s["bias"], 16)
                sp.wait_ge(s["split"], 5)
                for i in range(3):
                    sp.dma_start(bias_rows[i:i + 1, :], bias_parts[0:1, i, :]).then_inc(s["bias_rows"], 16)

                def load(r, u):
                    wait_unit(sp, s["kv"], r, u, 3)
                    sp.dma_start(rows[:, u % 3], ctx_T[:, :, bass.ds(r * (IN_LOOP * UNIT) + u * UNIT, UNIT)])\
                        .then_inc(loaded[u % 3], 16)

                def store(r, u):
                    if u % 2 == 0:
                        return
                    wait_unit(sp, s["lo"], r, u)
                    if not (isinstance(r, int) and r == 0 and u == 1):
                        sp.wait_ge(s["stored"], (3 * r + u // 2) * 48)
                    for i in range(3):
                        sp.dma_start(kd[i].rearrange("(c p) n -> p c n", p=128)[
                            :, :, bass.ds(r * (IN_LOOP * UNIT) + (u // 2) * 2 * UNIT, 2 * UNIT)],
                            parts[:, (u // 2) % 3, i]).then_inc(s["stored"], 16)

                def step(r, u):
                    load(r, u)
                    behind(store, r, u, 6)

                def flush(r):
                    for u in range(6):
                        behind(store, r, u, 6)
                rounds(sp, step, flush)
                sp.wait_ge(s["stored"], (UNITS // 2) * 48)

            @block.tensor
            def _(pe):
                pe.wait_ge(s["w"], 16)
                pe.wait_ge(s["bias_rows"], 48)
                pe.wait_ge(s["ones"], 1)

                def project(r, u):
                    pe.wait_ge(loaded[u % 3], r * 32 + (u // 3 + 1) * 16)
                    wait_unit(pe, s["k_int"], r, u, 3)
                    wait_unit(pe, s["v_read"], r, u, 3)
                    for kv in range(2):
                        of = slice(kv * D, (kv + 1) * D)
                        for j in range(2):
                            out = ps[0:KP, 2 * (u % 3) + kv, j * D:(j + 1) * D]
                            nc.tensor.matmul(out, ones[:], bias_rows[:, of], start=True, stop=False)
                            for c in range(C2):
                                last = nc.tensor.matmul(out, rows[:, u % 3, c, j * KP:(j + 1) * KP],
                                                        w[:, c, of], start=False, stop=(c == C2 - 1))
                    last.then_inc(s["kv"], 1)

                def turn(r, u):
                    wait_unit(pe, s["k_back"], r, u)
                    wait_unit(pe, s["residue"], r, u, 2)
                    for c in range(C2):
                        for j in range(2):
                            last = nc.tensor.transpose(
                                ps[:, 6 + u % 2, c * UNIT + j * KP:c * UNIT + (j + 1) * KP],
                                k_back[:, u % 3, j, c * 128:(c + 1) * 128], k.ident[0:KP, 0:KP])
                    last.then_inc(s["kT"], 1)

                def step(r, u):
                    project(r, u)
                    behind(turn, r, u, 2)

                def flush(r):
                    for u in range(2):
                        behind(turn, r, u, 2)
                rounds(pe, step, flush)

            @block.vector
            def _(dve):
                split = linker(dve, s["split"])
                dve.wait_ge(s["bias"], 16)
                split(nc.vector.tensor_copy(bias_parts[:, 0, :], bias))
                split(nc.vector.tensor_tensor(rest[:, 0, :], bias, bias_parts[:, 0, :], ALU.subtract))
                split(nc.vector.tensor_copy(bias_parts[:, 1, :], rest[:, 0, :]))
                split(nc.vector.tensor_tensor(rest[:, 1, :], rest[:, 0, :], bias_parts[:, 1, :], ALU.subtract))
                split(nc.vector.tensor_copy(bias_parts[:, 2, :], rest[:, 1, :]))
                nc.vector.memset(ones[:], 1.0).then_inc(s["ones"], 1)
                nc.vector.memset(v_max[:], 0.0).then_inc(s["vzero"], 1)
                dve.wait_ge(s["vzero"], 1)

                def quantise(r, u):
                    n = r * IN_LOOP + u
                    heads = ps[0:KP, 2 * (u % 3), :].rearrange("p (j h e) -> p j h e", j=2, e=HD)
                    first = r * (2 * IN_LOOP) + 2 * u
                    wait_unit(dve, s["kv"], r, u)
                    nc.vector.tensor_reduce(k_max[:, u % 2, :].rearrange("p (j h) -> p j h", j=2), heads, AX.X,
                                            ALU.max, apply_absolute_value=True).then_inc(s["link"], 1)
                    wait_unit(dve, s["v_read"], r, u)
                    nc.vector.tensor_reduce(v_unit[:], v_rows[:, bass.ds(first, 2), :].rearrange(
                        "p t n -> p n t"), AX.X, ALU.max, apply_absolute_value=True)\
                        .then_inc(s["link"], 1)
                    dve.wait_ge(s["link"], 3 * n + 1)
                    wait_unit(dve, s["k_back"], r, u, 3)
                    nc.vector.tensor_scalar(k_scale[:, u % 3, :], k_max[:, u % 2, :], 1.0 / 127.0, 1e-8,
                                            ALU.mult, ALU.max).then_inc(s["k_scale"], 1)
                    dve.wait_ge(s["link"], 3 * n + 2)
                    wait_unit(dve, s["k_read"], r, u, 1)
                    nc.vector.tensor_tensor(v_max[:], v_max[:], v_unit[:], ALU.max)\
                        .then_inc(s["k_read"], 1)
                    wait_unit(dve, s["k_scale"], r, u)
                    nc.vector.reciprocal(k_inv[:], k_scale[:, u % 3, :]).then_inc(s["link"], 1)
                    dve.wait_ge(s["link"], 3 * n + 3)
                    wait_unit(dve, s["k_float"], r, u, 2)
                    nc.vector.tensor_tensor(
                        k_steps[:, u % 2].rearrange("p j (h e) -> p j h e", e=HD), heads,
                        bcast(k_inv[:].rearrange("p (j h) -> p j h", j=2).unsqueeze(3), [KP, 2, H, HD]),
                        ALU.mult).then_inc(s["k_int"], 1)

                def take_high(r, u):
                    wait_unit(dve, s["hi"], r, u)
                    wait_unit(dve, s["lo"], r, u, 2)
                    slot = (u // 2) % 3
                    nc.vector.tensor_tensor(
                        residue[:, u % 2, :].rearrange("p (c n) -> p c n", c=C2),
                        ps[:, 6 + u % 2, 0:C2 * UNIT].rearrange("p (c n) -> p c n", c=C2),
                        parts[:, slot, 0, :, (u % 2) * UNIT:(u % 2 + 1) * UNIT], ALU.subtract)\
                        .then_inc(s["residue"], 1)

                def step(r, u):
                    quantise(r, u)
                    behind(take_high, r, u, 3)

                def flush(r):
                    for u in range(3):
                        behind(take_high, r, u, 3)
                rounds(dve, step, flush)

                dve.wait_ge(s["vzero"], 2)
                vlink = linker(dve, s["vlink"])
                vlink(nc.vector.tensor_scalar(k.v_scale[0:KP, :], v_all[:, 0, :], 1.0 / 127.0, 1e-8,
                                              ALU.mult, ALU.max))
                vlink(nc.vector.reciprocal(v_all[:, 1, :], k.v_scale[0:KP, :]))
                for i in range(KT // V_STEP):
                    if i >= 2:
                        dve.wait_ge(s["vsteps"], i - 1)
                    nc.vector.tensor_tensor(v_int[:, i % 2], v_rows[:, i * V_STEP:(i + 1) * V_STEP, :],
                                            bcast(v_all[:, 1:2, :], [KP, V_STEP, D]), ALU.mult).then_inc(s["vint"], 1)

            @block.scalar
            def _(act):
                def keep_v(r, u):
                    wait_unit(act, s["kv"], r, u)
                    nc.scalar.activation(v_rows[:, bass.ds(r * (2 * IN_LOOP) + 2 * u, 2), :],
                                         ps[0:KP, 2 * (u % 3) + 1, :].rearrange("p (j n) -> p j n", j=2),
                                         ACT.Copy).then_inc(s["v_read"], 1)

                def to_float(r, u):
                    wait_unit(act, s["k_int"], r, u)
                    wait_unit(act, s["kT"], r, u, 3)
                    nc.scalar.activation(k_back[:, u % 3], k_steps[:, u % 2], ACT.Copy)\
                        .then_inc(s["k_float"], 1)

                def high(r, u):
                    slot, at = (u // 2) % 3, slice((u % 2) * UNIT, (u % 2 + 1) * UNIT)
                    wait_unit(act, s["kT"], r, u)
                    if u % 2 == 0 and not (isinstance(r, int) and r == 0):
                        act.wait_ge(s["stored"], (3 * r + (u // 2) - 2) * 48)
                    nc.scalar.activation(parts[:, slot, 0, :, at],
                                         ps[:, 6 + u % 2, 0:C2 * UNIT].rearrange("p (c n) -> p c n", c=C2),
                                         ACT.Copy).then_inc(s["hi"], 1)

                def mid(r, u):
                    slot, at = (u // 2) % 3, slice((u % 2) * UNIT, (u % 2 + 1) * UNIT)
                    wait_unit(act, s["residue"], r, u)
                    nc.scalar.activation(parts[:, slot, 1, :, at],
                                         residue[:, u % 2, :].rearrange("p (c n) -> p c n", c=C2),
                                         ACT.Copy).then_inc(s["mid"], 1)

                def step(r, u):
                    keep_v(r, u)
                    behind(high, r, u, 3)
                    to_float(r, u)
                    behind(mid, r, u, 3)

                def flush(r):
                    for u in range(3):
                        behind(high, r, u, 3)
                        behind(mid, r, u, 3)
                rounds(act, step, flush)
                for i in range(KT // V_STEP):
                    act.wait_ge(s["vint"], i + 1)
                    nc.scalar.activation(k.v_steps[0:KP, i * V_STEP:(i + 1) * V_STEP, :], v_int[:, i % 2],
                                         ACT.Copy).then_inc(s["vsteps"], 1)

            @block.gpsimd
            def _(pool):
                def step(r, u):
                    scale_back(r, u)
                    behind(low, r, u, 3)

                def flush(r):
                    for u in range(3):
                        behind(low, r, u, 3)

                def scale_back(r, u):
                    wait_unit(pool, s["k_float"], r, u)
                    nc.gpsimd.tensor_tensor(
                        k_back[:, u % 3].rearrange("p j (h e) -> p j h e", e=HD),
                        k_back[:, u % 3].rearrange("p j (h e) -> p j h e", e=HD),
                        bcast(k_scale[:, u % 3, :].rearrange("p (j h) -> p j h", j=2).unsqueeze(3),
                              [KP, 2, H, HD]), ALU.mult).then_inc(s["k_back"], 1)

                def low(r, u):
                    slot, at = (u // 2) % 3, slice((u % 2) * UNIT, (u % 2 + 1) * UNIT)
                    wait_unit(pool, s["mid"], r, u)
                    nc.gpsimd.tensor_tensor(parts[:, slot, 2, :, at],
                                            residue[:, u % 2, :].rearrange("p (c n) -> p c n", c=C2),
                                            parts[:, slot, 1, :, at], ALU.subtract).then_inc(s["lo"], 1)
                rounds(pool, step, flush)
                pool.wait_ge(s["k_read"], UNITS)
                nc.gpsimd.partition_all_reduce(v_all[:, 0, :], v_max[:], KP, bass.bass_isa.ReduceOp.absmax)\
                    .then_inc(s["vzero"], 1)


def layer0_query(nc, k, d):
    with ExitStack() as ctx:
        sb = lambda n, sh, dt=F32: ctx.enter_context(nc.sbuf_tensor(n, sh, dt))
        w = sb("q0_w", [128, C2, D])
        bias = sb("q0_bias", [TP, D])
        q = sb("q0_q", [TP, TT, D])
        steps = sb("q0_steps", [TP, TT, D], I16)
        q_max = sb("q0_max", [TP, 4, TT * H])
        back = sb("q0_back", [TP, 3, TT, D])
        parts = sb("q0_parts", [TP, 3, TT, D], BF16)
        parts_T = sb("q0_partsT", [128, 3, C2, TOKENS], BF16)
        ps = ctx.enter_context(nc.psum_tensor("q0_ps", [128, 8, 512], F32))
        s = k.sems("q0", "load q link parts turned out stored")
        q_ps = ps[0:TP, 0:2, :].rearrange("p b (t n) -> p (b t) n", n=D)
        turned = ps[:, 2:5, :].bitcast(BF16)[:, :, 0:C2 * TOKENS].rearrange("p i (c n) -> p i c n", c=C2)
        heads = lambda x: x.rearrange("p t (h e) -> p (t h) e", e=HD)
        each = lambda i: bcast(q_max[:, i, :].unsqueeze(2), [TP, TT * H, HD])
        with nc.Block() as block:

            @block.sync
            def _(sp):
                sp.dma_start(w[:], d["c0_Wq"].rearrange("(c p) n -> p c n", p=128)).then_inc(s["load"], 16)
                sp.dma_start(bias[:], d["c0_bq"].partition_broadcast(TP)).then_inc(s["load"], 16)
                sp.wait_ge(s["out"], 3)
                sp.dma_start(k.q_parts.rearrange("i (c p) n -> p i c n", p=128), parts_T[:])\
                    .then_inc(s["stored"], 16)
                sp.wait_ge(s["stored"], 16)

            @block.tensor
            def _(pe):
                pe.wait_ge(s["load"], 32)
                for t in range(TT):
                    for c in range(C2):
                        last = nc.tensor.matmul(q_ps[:, t, :], k.x_T[:, c, t * TP:(t + 1) * TP], w[:, c, :],
                                                start=(c == 0), stop=(c == C2 - 1))
                last.then_inc(s["q"], 1)
                for i in range(3):
                    pe.wait_ge(s["parts"], i + 1)
                    for c in range(C2):
                        for t in range(TT):
                            last = nc.tensor.transpose(turned[:, i, c, t * TP:(t + 1) * TP],
                                                       parts[:, i, t, c * 128:(c + 1) * 128],
                                                       k.ident_b[0:TP, 0:TP])
                    last.then_inc(s["turned"], 1)

            @block.vector
            def _(dve):
                link = linker(dve, s["link"])
                dve.wait_ge(s["load"], 32)
                dve.wait_ge(s["q"], 1)
                link(nc.vector.tensor_tensor(q[:], q_ps, bcast(bias[:].unsqueeze(1), [TP, TT, D]), ALU.add))
                link(nc.vector.tensor_reduce(q_max[:, 0, :], heads(q[:]), AX.X, ALU.max,
                                             apply_absolute_value=True))
                link(nc.vector.tensor_scalar(q_max[:, 1, :], q_max[:, 0, :], 0.25 / 127.0, 1e-8,
                                             ALU.mult, ALU.max))
                link(nc.vector.reciprocal(q_max[:, 2, :], q_max[:, 1, :]))
                link(nc.vector.tensor_scalar(q_max[:, 3, :], q_max[:, 2, :], 0.25, None, ALU.mult))
                link(nc.vector.tensor_tensor(heads(steps[:]), heads(q[:]), each(3), ALU.mult))
                link(nc.vector.scalar_tensor_tensor(heads(back[:, 0]), heads(steps[:]), -1.0, each(1),
                                                    ALU.mult, ALU.mult))
                for i in range(3):
                    nc.vector.tensor_copy(parts[:, i], back[:, i]).then_inc(s["parts"], 1)
                    if i < 2:
                        dve.wait_ge(s["parts"], i + 1)
                        link(nc.vector.tensor_tensor(back[:, i + 1], back[:, i], parts[:, i], ALU.subtract))

            @block.scalar
            def _(act):
                for i in range(3):
                    act.wait_ge(s["turned"], i + 1)
                    nc.scalar.activation(parts_T[:, i], turned[:, i], ACT.Copy).then_inc(s["out"], 1)


def layer0_cross_attention(nc, k, d):
    with ExitStack() as ctx:
        sb = lambda n, sh, dt=F32: ctx.enter_context(nc.sbuf_tensor(n, sh, dt))
        kx = sb("c0_kx", [128, 3, KEYS], BF16)
        qx = sb("c0_qx", [128, H, TOKENS], BF16)
        low = sb("c0_low", [TP, H, TT * P1_STEPS])
        sums = sb("c0_sums", [TP, H, TT * P1_STEPS])
        head_low = sb("c0_headlow", [TP, H, TT])
        row = sb("c0_row", [TP, 3, TT])
        row_parts = sb("c0_rowparts", [TP, TT, 3], BF16)
        v_now = sb("c0_vnow", [KP, 4, 2, 32], BF16)
        fold = sb("c0_fold", [128, HD])
        groups_out = sb("c0_groups", [128, TOKENS])
        steps = sb("c0_steps", [KP, 4, 2, TOKENS], I16)
        probs = sb("c0_probs", [KP, 4, 2, TOKENS], BF16)
        out = sb("c0_out", [TP, H, TT, HD])
        inv = sb("c0_inv", [TP, H, TT])
        ctx_rows = sb("c0_ctx", [TP, TT, D])
        ctx_T = sb("c0_ctxT", [128, C2, TOKENS])
        w = sb("c0_wp", [128, C2, D])
        bias = sb("c0_bp", [TP, D])
        ps = ctx.enter_context(nc.psum_tensor("c0_ps", [128, 8, 512], F32))
        s = k.sems("c0", "kx qx kx_ones qx_zero w fold pv_sb folded scored1 scored2 low act1 act2 cast pv row row_link row_ps row_sb out zero "
                   "tail diff weight ctx ctxT ctxT_sb y res " + NORM_SEMS)
        N1 = TT * P1_STEPS
        assert N1 == HEAD_STEPS and KT // 2 == HEAD_STEPS and P1_STEPS == HEAD_STEPS // 4
        y = ps[0:TP, 2:4, :].rearrange("p b (t n) -> p (b t) n", n=D)
        pv, row_ps = ps[:, 7, 0:TOKENS], ps[QK_ROWS:QK_ROWS + 3, 6, 0:TOKENS]
        folded = ps[0:TP, 6, 0:TT * HD]

        GROUPS1 = HEAD_STEPS // 4

        def until(engine, name, h, i, u, lag=0):
            if isinstance(h, int) and isinstance(i, int) and h * HEAD_STEPS + 4 * i + u < lag:
                return
            engine.wait_ge(s[name], h * HEAD_STEPS + (i * 4 + (u + 1 - lag)))

        def groups(engine, body, peel=False):
            if peel:
                body(0)
            with engine.Fori(int(peel), GROUPS1 - 1) as i:
                body(i)

        def stages(engine, stage, last):
            stage(0)
            stage(1)
            stage(2)
            with engine.Fori(3, H) as h:
                stage(h)
            last()

        at = lambda h: bass.ds(h, 1)
        flat = lambda ap: ap.rearrange("p a n -> p (a n)")

        with nc.Block() as block:

            @block.gpsimd
            def _(pool):
                nc.gpsimd.memset(fold[:], 0.0).then_inc(s["fold"], 1)
                for g in range(4):
                    pool.wait_ge(s["fold"], g + 1)
                    nc.gpsimd.affine_select(out=fold[:], in_=fold[:], compare_op=ALU.not_equal, fill=1.0,
                                            base=-32 * g, pattern=[[-1, HD]], channel_multiplier=1)\
                        .then_inc(s["fold"], 1)
                pool.wait_ge(s["fold"], 5)
                nc.gpsimd.memset(kx[QK_ROWS:, 1:3, :], 1.0).then_inc(s["kx_ones"], 1)

            @block.sync
            def _(sp):
                for j, part in enumerate(PARTS):
                    sp.dma_start(qx[16 * j:16 * j + 16, :, :], k.q_parts[part].rearrange(
                        "(h p) n -> p h n", p=HD)).then_inc(s["qx"], 16)
                sp.dma_start(w[:], d["c0_Wp"].rearrange("(c p) n -> p c n", p=128)).then_inc(s["w"], 16)
                sp.dma_start(bias[:], d["c0_bp"].partition_broadcast(TP)).then_inc(s["w"], 16)

                def load(h, slot):
                    if isinstance(h, int) and h > 0:
                        sp.wait_ge(s["kx"], h * (16 * len(K_PARTS)))
                    for j, part in enumerate(K_PARTS):
                        sp.dma_start(kx[16 * j:16 * j + 16, bass.ds(slot, 1), :],
                                     k.k_parts[part, bass.ds(h * HD, HD), :]).then_inc(s["kx"], 16)
                for h in range(3):
                    load(h, h)
                with sp.Fori(3, H) as h:
                    sp.wait_ge(s["scored1"], (h - 1) * HEAD_STEPS + 1)
                    load(h, h % 3)

            @block.tensor
            def _(pe):
                def find(h, i, u):
                    until(pe, "act1", h, i, u, 2)
                    for j in range(2):
                        last = nc.tensor.matmul(
                            ps[0:TP, 2 * (u % 2) + j, 0:500], flat(qx[:, at(h), u * TP:(u + 1) * TP]),
                            flat(kx[:, at(h % 3), bass.ds(i * P1_KEYS + j * 500, 500)]),
                            start=True, stop=True)
                    last.then_inc(s["scored1"], 1)

                def score(h, i, u):
                    until(pe, "act2", h, i, u, 1)
                    for j in range(2):
                        last = nc.tensor.matmul(
                            ps[0:KP, 4 + j, 0:TOKENS],
                            flat(kx[:, at(h % 3), bass.ds(i * (8 * KP) + (2 * u + j) * KP, KP)]),
                            flat(qx[:, at(h), :]), start=True, stop=True)
                    last.then_inc(s["scored2"], 1)

                def product(h, i, u):
                    until(pe, "cast", h, i, u + 1)
                    first = isinstance(i, int) and i == 0 and u == 0
                    for g in range(4):
                        last = nc.tensor.matmul(pv[32 * g:32 * g + 32, :], v_now[:, u + g // 2, g % 2, :],
                                                probs[:, u + g // 2, g % 2, :], start=first, stop=True,
                                                skip_group_check=True)
                    last.then_inc(s["pv"], 1)

                def place_maxima(h):
                    pe.wait_ge(s["row"], h * 3 + 3)
                    if not (isinstance(h, int) and h < 2):
                        pe.wait_ge(s["out"], h - 1)
                    for t in range(TT):
                        last = nc.tensor.matmul(row_ps[:, t * TP:(t + 1) * TP], row_parts[:, t, :],
                                                k.ident_b[0:TP, 0:TP], start=True, stop=True)
                    last.then_inc(s["row_ps"], 1)

                def product_lagged(h, i, u):
                    if u == 3:
                        product(h, i, 0)
                    elif u == 1 and not (isinstance(i, int) and i == 0):
                        product(h, i - 1, 2)

                def fold_groups(h):
                    pe.wait_ge(s["pv_sb"], h + 1)
                    for t in range(TT):
                        last = nc.tensor.matmul(folded[:, t * HD:(t + 1) * HD],
                                                groups_out[:, t * TP:(t + 1) * TP], fold[:], start=True, stop=True)
                    last.then_inc(s["folded"], 1)

                def stage(h):
                    if isinstance(h, int) and h == 1:
                        pe.wait_ge(s["kx_ones"], 1)
                    for u in range(4):
                        pe.wait_ge(s["kx"], h * (16 * len(K_PARTS)) + 16 * len(K_PARTS))
                        find(h, 0, u)
                        if u == 0 and not (isinstance(h, int) and h < 2):
                            product(h - 2, GROUPS1 - 1, 2)
                        if u == 1 and not (isinstance(h, int) and h < 1):
                            place_maxima(h - 1)
                    if isinstance(h, int) and h == 0:
                        def alone(i):
                            for u in range(4):
                                find(h, i + 1, u)
                        groups(pe, alone)
                        return
                    pe.wait_ge(s["row_sb"], h)
                    if not (isinstance(h, int) and h < 2):
                        fold_groups(h - 2)

                    def joint(i):
                        for u in range(4):
                            score(h - 1, i, u)
                            product_lagged(h - 1, i, u)
                            find(h, i + 1, u)
                    groups(pe, joint, peel=True)
                    for u in range(4):
                        score(h - 1, GROUPS1 - 1, u)
                        product_lagged(h - 1, GROUPS1 - 1, u)

                def last_stage():
                    product(H - 2, GROUPS1 - 1, 2)
                    place_maxima(H - 1)
                    pe.wait_ge(s["row_sb"], H)
                    fold_groups(H - 2)

                    def alone(i):
                        for u in range(4):
                            score(H - 1, i, u)
                            product_lagged(H - 1, i, u)
                    groups(pe, alone, peel=True)
                    alone(GROUPS1 - 1)
                    product(H - 1, GROUPS1 - 1, 2)
                    pe.wait_ge(s["out"], H - 1)
                    fold_groups(H - 1)

                pe.wait_ge(s["qx"], 16 * len(PARTS))
                pe.wait_ge(s["qx_zero"], 2)
                stages(pe, stage, last_stage)
                pe.wait_ge(s["ctx"], 1)
                transpose_rows(nc, k, ps[:, 0:2, 0:TOKENS], ctx_rows).then_inc(s["ctxT"], 1)
                pe.wait_ge(s["ctxT_sb"], 1)
                pe.wait_ge(s["w"], 32)
                for t in range(TT):
                    for c in range(C2):
                        last = nc.tensor.matmul(y[:, t, :], ctx_T[:, c, t * TP:(t + 1) * TP], w[:, c, :],
                                                start=(c == 0), stop=(c == C2 - 1))
                last.then_inc(s["y"], 1)
                norm_tensor(nc, pe, k, s, ps[:, 4:6, 0:TOKENS])

            @block.vector
            def _(dve):
                nc.vector.memset(qx[QK_ROWS:, :, :], 0.0).then_inc(s["qx_zero"], 1)
                nc.vector.memset(kx[QK_ROWS:, 0, :], 1.0).then_inc(s["qx_zero"], 1)
                nc.vector.memset(v_now[:], 0.0).then_inc(s["zero"], 1)
                dve.wait_ge(s["zero"], 1)

                def find(h, i, u):
                    until(dve, "scored1", h, i, u)
                    nc.vector.tensor_reduce(
                        flat(low[:, at(h), bass.ds(i + u * P1_STEPS, 1)]),
                        ps[0:TP, 2 * (u % 2):2 * (u % 2) + 2, 0:500], AX.XY, ALU.min).then_inc(s["low"], 1)

                def cut_maxima(h):
                    n = [0]

                    def link(ins):
                        n[0] += 1
                        ins.then_inc(s["row_link"], 1)
                        dve.wait_ge(s["row_link"], h * 3 + n[0])
                    link(nc.vector.tensor_reduce(row[:, 0, :], low[:, at(h), :].rearrange(
                        "p a (t n) -> p (a t) n", t=TT), AX.X, ALU.min, negate=True))
                    for i in range(3):
                        nc.vector.tensor_copy(row_parts[:, :, i], row[:, i, :]).then_inc(s["row"], 1)
                        if i < 2:
                            dve.wait_ge(s["row"], h * 3 + (i + 1))
                            link(nc.vector.tensor_tensor(row[:, i + 1, :], row[:, i, :], row_parts[:, :, i],
                                                         ALU.subtract))

                def place_maxima(h):
                    dve.wait_ge(s["row_ps"], h + 1)
                    nc.vector.tensor_copy(flat(qx[QK_ROWS:QK_ROWS + 3, at(h), :]), row_ps)\
                        .then_inc(s["row_sb"], 1)

                def cast(h, i, u):
                    until(dve, "act2", h, i, u)
                    if u % 2 == 0 and not (isinstance(h, int) and h == 0 and isinstance(i, int) and i == 0):
                        dve.wait_ge(s["pv"], h * (HEAD_STEPS // 2) + (i * 2 + (u // 2 - 1)))
                    nc.vector.tensor_copy(v_now[:, u, :, 0:HD],
                                          k.v_steps[:, bass.ds(i * 8 + 2 * u, 2), bass.ds(h * HD, HD)])
                    nc.vector.tensor_copy(probs[:, u], steps[:, u]).then_inc(s["cast"], 1)

                def take_groups(h):
                    dve.wait_ge(s["pv"], (h + 1) * (HEAD_STEPS // 2))
                    if not (isinstance(h, int) and h == 0):
                        dve.wait_ge(s["folded"], h)
                    nc.vector.tensor_copy(groups_out[:], pv).then_inc(s["pv_sb"], 1)

                def take_out(h):
                    dve.wait_ge(s["folded"], h + 1)
                    nc.vector.tensor_copy(out[:, at(h)].rearrange("p a t e -> p (a t e)"), folded)\
                        .then_inc(s["out"], 1)

                def stage(h):
                    for u in range(4):
                        find(h, 0, u)
                        if u == 1 and not (isinstance(h, int) and h < 1):
                            place_maxima(h - 1)
                        if u == 1 and not (isinstance(h, int) and h < 2):
                            take_groups(h - 2)
                    if not (isinstance(h, int) and h < 2):
                        take_out(h - 2)
                    alone = isinstance(h, int) and h == 0

                    def joint(i):
                        for u in range(4):
                            find(h, i + 1, u)
                            if not alone:
                                cast(h - 1, i, u)
                    groups(dve, joint, peel=isinstance(h, int) and h == 1)
                    until(dve, "low", h, GROUPS1 - 1, 3)
                    if not alone:
                        cast(h - 1, GROUPS1 - 1, 0)
                    cut_maxima(h)
                    if not alone:
                        for u in range(1, 4):
                            cast(h - 1, GROUPS1 - 1, u)

                def last_stage():
                    place_maxima(H - 1)
                    take_groups(H - 2)
                    take_out(H - 2)

                    def alone(i):
                        for u in range(4):
                            cast(H - 1, i, u)
                    groups(dve, alone)
                    alone(GROUPS1 - 1)
                    take_groups(H - 1)
                    take_out(H - 1)

                dve.wait_ge(s["w"], 32)
                nc.vector.tensor_tensor(k.res[:], k.x_tok[:], bcast(bias[:].unsqueeze(1), [TP, TT, D]),
                                        ALU.add)
                stages(dve, stage, last_stage)
                link = linker(dve, s["tail"])
                link(nc.vector.tensor_reduce(head_low[:].rearrange("p h t -> p (h t)"), low[:].rearrange(
                    "p h (t n) -> p (h t) n", t=TT), AX.X, ALU.min))
                lows = low[:].rearrange("p h (t n) -> p (h t) n", t=TT)
                nc.vector.tensor_tensor(lows, bcast(head_low[:].rearrange("p h t -> p (h t)").unsqueeze(2),
                                                    [TP, H * TT, P1_STEPS]), lows, ALU.subtract)\
                    .then_inc(s["diff"], 1)
                dve.wait_ge(s["weight"], 1)
                link(nc.vector.tensor_tensor(sums[:], sums[:], low[:], ALU.mult))
                link(nc.vector.tensor_reduce(head_low[:].rearrange("p h t -> p (h t)"), sums[:].rearrange(
                    "p h (t n) -> p (h t) n", t=TT), AX.X, ALU.add))
                link(nc.vector.reciprocal(inv[:], head_low[:]))
                link(nc.vector.tensor_scalar(inv[:], inv[:], 1.0 / 255.0, None, ALU.mult))
                link(nc.vector.tensor_tensor(out[:], out[:], bcast(inv[:].unsqueeze(3), [TP, H, TT, HD]),
                                             ALU.mult))
                nc.vector.tensor_tensor(
                    ctx_rows[:].rearrange("p t (h e) -> p h t e", h=H), out[:],
                    bcast(k.v_scale[0:TP, :].rearrange("p (h e) -> p h e", h=H).unsqueeze(2), [TP, H, TT, HD]),
                    ALU.mult).then_inc(s["ctx"], 1)
                dve.wait_ge(s["y"], 1)
                norm_vector(nc, dve, link, k, s, y)

            @block.scalar
            def _(act):
                def find(h, i, u):
                    until(act, "low", h, i, u)
                    block_at = bass.ds(i + u * P1_STEPS, 1)
                    banks = ps[0:TP, 2 * (u % 2):2 * (u % 2) + 2, 0:500]
                    nc.scalar.activation(banks, banks, ACT.Exp, scale=-1.0, bias=flat(low[:, at(h), block_at]),
                                         accum_out=flat(sums[:, at(h), block_at])).then_inc(s["act1"], 1)

                def take_steps(h, i, u):
                    until(act, "scored2", h, i, u)
                    until(act, "cast", h, i, u, 4)
                    nc.scalar.activation(steps[:, u], ps[0:KP, 4:6, 0:TOKENS], ACT.Exp, scale=-1.0, bias=LN255)\
                        .then_inc(s["act2"], 1)

                def stage(h):
                    for u in range(3):
                        find(h, 0, u)
                    alone = isinstance(h, int) and h == 0

                    def joint(i):
                        for u in range(4):
                            if not alone:
                                take_steps(h - 1, i, u)
                            if u == 0:
                                find(h, i, 3)
                            else:
                                find(h, i + 1, u - 1)
                    groups(act, joint, peel=isinstance(h, int) and h == 1)
                    if alone:
                        find(h, GROUPS1 - 1, 3)
                        return
                    for u in range(4):
                        take_steps(h - 1, GROUPS1 - 1, u)
                        if u == 0:
                            find(h, GROUPS1 - 1, 3)

                def last_stage():
                    def alone(i):
                        for u in range(4):
                            take_steps(H - 1, i, u)
                    groups(act, alone)
                    alone(GROUPS1 - 1)

                stages(act, stage, last_stage)
                act.wait_ge(s["diff"], 1)
                nc.scalar.activation(low[:], low[:], ACT.Exp).then_inc(s["weight"], 1)
                act.wait_ge(s["ctxT"], 1)
                nc.scalar.activation(ctx_T[:], ps[:, 0:2, 0:TOKENS], ACT.Copy).then_inc(s["ctxT_sb"], 1)
                norm_scalar(nc, act, k, s, ps[:, 4:6, 0:TOKENS])


def route_shift(nc, link, k, logits, shifted):
    r = k.route
    link(nc.vector.tensor_reduce(r[:, :, 24], logits, AX.X, ALU.max, negate=True))
    nc.vector.tensor_tensor(r[:, :, 0:8], logits, bcast(r[:, :, 24:25], [TP, TT, E]), ALU.add)\
        .then_inc(shifted, 1)


def route_choose(nc, link, k, gates, normalise, chosen):
    r = k.route
    link(nc.vector.tensor_reduce(r[:, :, 25], r[:, :, 8:16], AX.X, ALU.add))
    link(nc.vector.reciprocal(r[:, :, 26], r[:, :, 25]))
    link(nc.vector.tensor_tensor(r[:, :, 0:8], r[:, :, 8:16], bcast(r[:, :, 26:27], [TP, TT, E]), ALU.mult))
    for t in range(TT):
        last = nc.vector.max(r[:, t, 16:24], r[:, t, 0:8])
    link(last)
    for t in range(TT):
        last = nc.vector.max_index(k.route_at[:, t, :], r[:, t, 16:24], r[:, t, 0:8])
    link(last)
    link(nc.vector.tensor_copy(k.route_idx[:], k.route_at[:]))
    if normalise:
        link(nc.vector.tensor_tensor(r[:, :, 27], r[:, :, 16], r[:, :, 17], ALU.add))
        link(nc.vector.reciprocal(r[:, :, 28], r[:, :, 27]))
        link(nc.vector.tensor_tensor(r[:, :, 16:18], r[:, :, 16:18], bcast(r[:, :, 28:29], [TP, TT, 2]),
                                     ALU.mult))
    for i in range(2):
        to = (r[:, :, 8:16], gates)[i]
        link(nc.vector.tensor_tensor(r[:, :, 29:37], bcast(k.expert[:].unsqueeze(1), [TP, TT, E]),
                                     bcast(k.route_idx[:, :, i:i + 1], [TP, TT, E]), ALU.is_equal))
        link(nc.vector.tensor_tensor(to, r[:, :, 29:37], bcast(r[:, :, 16 + i:17 + i], [TP, TT, E]), ALU.mult))
    nc.vector.tensor_tensor(gates, gates, r[:, :, 8:16], ALU.add).then_inc(chosen, 1)


def layer0_mlp(nc, k, d):
    with ExitStack() as ctx:
        sb = lambda n, sh, dt=F32: ctx.enter_context(nc.sbuf_tensor(n, sh, dt))
        w = sb("f0_w", [128, 3, C2, D])
        wr = sb("f0_wr", [128, C2, E])
        h1 = sb("f0_h1", [128, C2, TOKENS])
        h2 = sb("f0_h2", [TP, TT, D])
        gates = sb("f0_gates", [TP, TT, E])
        mixed = sb("f0_mixed", [128, C2, E])
        y_sb = sb("f0_y", [TP, TT, D])
        ps = ctx.enter_context(nc.psum_tensor("f0_ps", [128, 8, 512], F32))
        s = k.sems("f0", "w logits shifted exp gates h1 h1_sb h2 h2_sb mixed mixed_sb y link zero iota " + NORM_SEMS)
        logits = ps[0:TP, 0, 0:TT * E].rearrange("p (t e) -> p t e", e=E)
        h2_ps = ps[0:TP, 3:5, :].rearrange("p b (t n) -> p (b t) n", n=D)
        with nc.Block() as block:

            @block.sync
            def _(sp):
                for i, n in enumerate(("f0_w1", "f0_w3", "f0_w2")):
                    sp.dma_start(w[:, i], d[n].rearrange("(c p) n -> p c n", p=128)).then_inc(s["w"], 16)
                sp.dma_start(wr[:], d["f0_wr"].rearrange("(c p) n -> p c n", p=128)).then_inc(s["w"], 16)

            @block.gpsimd
            def _(pool):
                nc.gpsimd.iota(k.expert_i[:], pattern=[[1, E]], base=0, channel_multiplier=0)\
                    .then_inc(s["iota"], 1)
                pool.wait_ge(s["iota"], 1)
                nc.gpsimd.tensor_copy(k.expert[:], k.expert_i[:]).then_inc(s["iota"], 1)

            @block.tensor
            def _(pe):
                pe.wait_ge(s["w"], 64)
                for t in range(TT):
                    for c in range(C2):
                        last = nc.tensor.matmul(logits[:, t, :], k.x_T[:, c, t * TP:(t + 1) * TP], wr[:, c, :],
                                                start=(c == 0), stop=(c == C2 - 1))
                last.then_inc(s["logits"], 1)
                for o in range(C2):
                    for c in range(C2):
                        last = nc.tensor.matmul(ps[:, 1 + o, 0:TOKENS], w[:, 0, c, o * 128:(o + 1) * 128],
                                                k.x_T[:, c, :], start=(c == 0), stop=(c == C2 - 1))
                last.then_inc(s["h1"], 1)
                pe.wait_ge(s["h1_sb"], 1)
                for t in range(TT):
                    for c in range(C2):
                        last = nc.tensor.matmul(h2_ps[:, t, :], h1[:, c, t * TP:(t + 1) * TP], w[:, 1, c, :],
                                                start=(c == 0), stop=(c == C2 - 1))
                last.then_inc(s["h2"], 1)
                pe.wait_ge(s["h2_sb"], 1)
                pe.wait_ge(s["gates"], 1)
                for c in range(C2):
                    for t in range(TT):
                        last = nc.tensor.matmul(ps[:, 5, c * E:(c + 1) * E], h2[:, t, c * 128:(c + 1) * 128],
                                                gates[:, t, :], start=(t == 0), stop=(t == TT - 1))
                last.then_inc(s["mixed"], 1)
                pe.wait_ge(s["mixed_sb"], 1)
                for c in range(C2):
                    last = nc.tensor.matmul(ps[0:E, 6, 0:D], mixed[:, c, :], w[:, 2, c, :],
                                            start=(c == 0), stop=(c == C2 - 1))
                last.then_inc(s["y"], 1)
                norm_tensor(nc, pe, k, s, ps[:, 1:3, 0:TOKENS])

            @block.scalar
            def _(act):
                act.wait_ge(s["shifted"], 1)
                nc.scalar.activation(k.route[:, :, 8:16], k.route[:, :, 0:8], ACT.Exp).then_inc(s["exp"], 1)
                act.wait_ge(s["h1"], 1)
                nc.scalar.activation(h1[:], ps[:, 1:3, 0:TOKENS], ACT.Silu).then_inc(s["h1_sb"], 1)
                act.wait_ge(s["h2"], 1)
                nc.scalar.activation(h2[:], h2_ps, ACT.Silu).then_inc(s["h2_sb"], 1)
                norm_scalar(nc, act, k, s, ps[:, 1:3, 0:TOKENS])

            @block.vector
            def _(dve):
                link = linker(dve, s["link"])
                link(nc.vector.memset(y_sb[:], 0.0))
                link(nc.vector.tensor_copy(k.res[:], k.x_tok[:]))
                dve.wait_ge(s["logits"], 1)
                dve.wait_ge(s["iota"], 2)
                route_shift(nc, link, k, logits, s["shifted"])
                dve.wait_ge(s["exp"], 1)
                route_choose(nc, link, k, gates[:], True, s["gates"])
                dve.wait_ge(s["mixed"], 1)
                nc.vector.tensor_copy(mixed[:], ps[:, 5, 0:C2 * E].rearrange("p (c e) -> p c e", e=E))\
                    .then_inc(s["mixed_sb"], 1)
                dve.wait_ge(s["y"], 1)
                link(nc.vector.tensor_copy(y_sb[0:E, 0, :], ps[0:E, 6, 0:D]))
                norm_vector(nc, dve, link, k, s, y_sb[:])


def layer1_attention(nc, k, d):
    k.phase = "a1"
    with ExitStack() as ctx:
        sb = lambda n, sh, dt=F32: ctx.enter_context(nc.sbuf_tensor(n, sh, dt))
        w = sb("a1_w", [128, 3, C2, D])
        wo = sb("a1_wo", [128, C2, D])
        bqk = sb("a1_bqk", [128, 2, C2])
        bv = sb("a1_bv", [TP, D])
        bo = sb("a1_bo", [TP, D])
        q_T = sb("a1_qT", [128, C2, TOKENS])
        k_T = sb("a1_kT", [128, C2, TOKENS])
        q_heads = sb("a1_qheads", [128, C2, 8, TOKENS])
        v = sb("a1_v", [TP, TT, D])
        term = sb("a1_term", [TP, H, TP])
        place_i = sb("a1_placei", [TP, TP], I32)
        place = sb("a1_place", [TP, TP])
        o_rows = sb("a1_o", [TP, TT, D])
        o_T = sb("a1_oT", [128, C2, TOKENS])
        attention_buffers(nc, ctx, k)
        ps = ctx.enter_context(nc.psum_tensor("a1_ps", [128, 8, 512], F32))
        s = k.sems("a1", "w bias qk q_sb k_sb v v_sb q_heads const mask head_mask term o_all oT oT_sb y link "
                   + ATT_SEMS + " " + NORM_SEMS)
        y = ps[0:TP, 6:8, :].rearrange("p b (t n) -> p (b t) n", n=D)
        v_ps = ps[0:TP, 4:6, :].rearrange("p b (t n) -> p (b t) n", n=D)
        sc, pt, o = [ps[:, i, :] for i in (0, 1)], [ps[:, i, :] for i in (2, 3)], [ps[:, i, :] for i in (4, 5)]
        slopes = [(2.0 ** (-2.0 ** -(np.log2(H) - 3))) ** (i + 1) for i in range(H)]
        with nc.Block() as block:

            @block.sync
            def _(sp):
                for i in range(3):
                    sp.dma_start(w[:, i], d["a1_Wqkv"][i].rearrange("(c p) n -> p c n", p=128))\
                        .then_inc(s["w"], 16)
                sp.dma_start(wo[:], d["a1_Wo"].rearrange("(c p) n -> p c n", p=128)).then_inc(s["w"], 16)
                sp.dma_start(bqk[:], d["a1_bqk"]).then_inc(s["bias"], 16)
                sp.dma_start(bv[:], d["a1_bv"].partition_broadcast(TP)).then_inc(s["bias"], 16)
                sp.dma_start(bo[:], d["a1_bo"].partition_broadcast(TP)).then_inc(s["bias"], 16)

            @block.gpsimd
            def _(pool):
                nc.gpsimd.memset(k.head_mask[:], 1.0).then_inc(s["const"], 1)
                nc.gpsimd.iota(place_i[:].rearrange("p (b t) -> p b t", b=2), pattern=[[0, 2], [1, T]], base=0,
                               channel_multiplier=0).then_inc(s["const"], 1)
                pool.wait_ge(s["const"], 2)
                nc.gpsimd.affine_select(out=k.head_mask[:], in_=k.head_mask[:], compare_op=ALU.is_ge, fill=0.0,
                                        base=0, pattern=[[-HD, 8]], channel_multiplier=1).then_inc(s["const"], 1)
                nc.gpsimd.tensor_copy(place[:], place_i[:]).then_inc(s["mask"], 1)
                pool.wait_ge(s["const"], 3)
                nc.gpsimd.affine_select(out=k.head_mask[:], in_=k.head_mask[:], compare_op=ALU.is_ge, fill=0.0,
                                        base=HD - 1, pattern=[[HD, 8]], channel_multiplier=-1)\
                    .then_inc(s["head_mask"], 1)
                pool.wait_ge(s["mask"], 1)
                for h in range(H):
                    nc.gpsimd.tensor_scalar(term[:, h, :], place[:], float(-(T - 1)), float(np.float32(slopes[h])),
                                            ALU.add, ALU.mult).then_inc(s["const"], 1)
                pool.wait_ge(s["const"], 3 + H)
                nc.gpsimd.affine_select(out=term[:], in_=term[:], compare_op=ALU.is_ge, fill=MASKED, base=0,
                                        pattern=[[0, H], [-1, TP]], channel_multiplier=1).then_inc(s["const"], 1)
                pool.wait_ge(s["const"], 4 + H)
                nc.gpsimd.affine_select(out=term[:, :, 0:T], in_=term[:, :, 0:T], compare_op=ALU.is_ge,
                                        fill=MASKED, base=T - 1, pattern=[[0, H], [0, T]], channel_multiplier=-1)\
                    .then_inc(s["term"], 1)

            @block.tensor
            def _(pe):
                pe.wait_ge(s["w"], 64)
                for n in range(2):
                    for o_ in range(C2):
                        for c in range(C2):
                            last = nc.tensor.matmul(ps[:, 2 * n + o_, 0:TOKENS],
                                                    w[:, n, c, o_ * 128:(o_ + 1) * 128], k.x_T[:, c, :],
                                                    start=(c == 0), stop=(c == C2 - 1))
                    last.then_inc(s["qk"], 1)
                for t in range(TT):
                    for c in range(C2):
                        last = nc.tensor.matmul(v_ps[:, t, :], k.x_T[:, c, t * TP:(t + 1) * TP], w[:, 2, c, :],
                                                start=(c == 0), stop=(c == C2 - 1))
                last.then_inc(s["v"], 1)
                pe.wait_ge(s["q_heads"], C2)
                pe.wait_ge(s["k_sb"], C2)
                pe.wait_ge(s["v_sb"], 1)

                def score_operands(p, h):
                    return (q_heads[:, h // 8, h % 8, p * TP:(p + 1) * TP],
                            k_T[:, h // 8, p * TP:(p + 1) * TP])

                def value_product(out, p, h, j, probs):
                    return nc.tensor.matmul(out[0:TP, j * HD:(j + 1) * HD], probs, v[:, p, h * HD:(h + 1) * HD],
                                            start=True, stop=True)

                attention_tensor(nc, pe, k, s, score_operands, value_product, sc, pt, o)
                pe.wait_ge(s["o_sbuf"], GROUPS)
                transpose_rows(nc, k, ps[:, 0:2, 0:TOKENS], o_rows).then_inc(s["oT"], 1)
                pe.wait_ge(s["oT_sb"], 1)
                for t in range(TT):
                    for c in range(C2):
                        last = nc.tensor.matmul(y[:, t, :], o_T[:, c, t * TP:(t + 1) * TP], wo[:, c, :],
                                                start=(c == 0), stop=(c == C2 - 1))
                last.then_inc(s["y"], 1)
                norm_tensor(nc, pe, k, s, ps[:, 2:4, 0:TOKENS])

            @block.scalar
            def _(act):
                act.wait_ge(s["bias"], 48)
                act.wait_ge(s["qk"], 1)
                for c in range(C2):
                    nc.scalar.activation(q_T[:, c, :], ps[:, c, 0:TOKENS], ACT.Identity,
                                         bias=bqk[:, 0, c:c + 1]).then_inc(s["q_sb"], 1)

                def place_output(g, bank):
                    h = 4 * (g % 4)
                    return nc.scalar.activation(o_rows[:, g // 4, h * HD:(h + 4) * HD], bank[0:TP, 0:4 * HD],
                                                ACT.Copy)

                attention_scalar(nc, act, k, s, 1.0, pt, o, place_output)
                act.wait_ge(s["oT"], 1)
                nc.scalar.activation(o_T[:], ps[:, 0:2, 0:TOKENS], ACT.Copy).then_inc(s["oT_sb"], 1)
                norm_scalar(nc, act, k, s, ps[:, 2:4, 0:TOKENS])

            @block.vector
            def _(dve):
                link = linker(dve, s["link"])
                dve.wait_ge(s["bias"], 48)
                nc.vector.tensor_tensor(k.res[:], k.x_tok[:], bcast(bo[:].unsqueeze(1), [TP, TT, D]), ALU.add)
                dve.wait_ge(s["qk"], 2)
                for c in range(C2):
                    nc.vector.tensor_scalar(k_T[:, c, :], ps[:, 2 + c, 0:TOKENS], bqk[:, 1, c:c + 1], None,
                                            ALU.add).then_inc(s["k_sb"], 1)
                dve.wait_ge(s["v"], 1)
                nc.vector.tensor_tensor(v[:], v_ps, bcast(bv[:].unsqueeze(1), [TP, TT, D]), ALU.add)\
                    .then_inc(s["v_sb"], 1)
                dve.wait_ge(s["q_sb"], C2)
                dve.wait_ge(s["head_mask"], 1)
                for c in range(C2):
                    nc.vector.tensor_tensor(q_heads[:, c], bcast(q_T[:, c:c + 1, :], [128, 8, TOKENS]),
                                            bcast(k.head_mask[:].unsqueeze(2), [128, 8, TOKENS]), ALU.mult)\
                        .then_inc(s["q_heads"], 1)
                dve.wait_ge(s["term"], 1)

                def add_term(g, out, scores):
                    h = 4 * (g % 4)
                    return nc.vector.scalar_tensor_tensor(
                        out, scores[0:TP, 0:4 * TP].rearrange("p (j t) -> p j t", j=4), 1.0 / np.sqrt(HD),
                        term[:, h:h + 4, :], ALU.mult, ALU.add)

                attention_vector(nc, dve, k, s, add_term, sc)
                dve.wait_ge(s["y"], 1)
                norm_vector(nc, dve, link, k, s, y)


def layer1_cross_attention(nc, k, d):
    with ExitStack() as ctx:
        sb = lambda n, sh, dt=F32: ctx.enter_context(nc.sbuf_tensor(n, sh, dt))
        TILES = S // KP
        GK = 500
        w = sb("c1_w", [128, 4, C2, D])
        bqk = sb("c1_bqk", [128, 2, C2])
        rows_of = {n: sb(f"c1_{n}", [KP, D]) for n in ("bv", "bo", "gamma", "beta")}
        q_T = sb("c1_qT", [128, C2, TOKENS])
        q_heads = sb("c1_qheads", [128, C2, 8, TOKENS])
        ctx_rows = sb("c1_ctx", [128, 2, C2, S])
        k_T = sb("c1_kT", [128, 2, C2, S])
        v = sb("c1_v", [KP, 2, TILES, H // 2, 2 * HD + 1])
        clipped = sb("c1_clipped", [KP, 2, H * T])
        probs = sb("c1_probs", [KP, 2, H * T])
        mask_i = sb("c1_maski", [KP, KT], I32)
        attend = sb("c1_attend", [KP, 2, KT])
        sums = sb("c1_sums", [TP, 4, H // 2])
        half = sb("c1_half", [TP, 2])
        own = sb("c1_own", [TP, H // 2, 2])
        out = sb("c1_out", [TP, 2, D])
        fold = sb("c1_fold", [TP, T])
        ctx_T = sb("c1_ctxT", [128, C2, TOKENS])
        rs = sb("c1_rs", [TP, 1])
        delta = sb("c1_delta", [TP, TT, D])
        ps = ctx.enter_context(nc.psum_tensor("c1_ps", [128, 8, 512], F32))
        s = k.sems("c1", "w bias mask l0 l1 q q_sb q_heads const fold half ones attend proj k_out v_out scored "
                   "clip exp pv link own merged ctx_out y rs var2 std2 " + NORM_SEMS)
        loaded = [s["l0"], s["l1"]]
        y = ps[0:TP, 0:2, :].rearrange("p b (t n) -> p (b t) n", n=D)
        src = d["ctx_T"].rearrange("(c p) n -> p c n", p=128)

        def halves(proj, tile, merge, slots=TILES):
            def run(engine):
                def half_step(b, parity, first=False, last=False):
                    for i in range(slots):
                        if not last:
                            proj(b, parity, i)
                        if not first:
                            tile(b - 1, 1 - parity, i)
                        if i == 3 and not first and not (isinstance(b, int) and b < 2):
                            merge(b - 2, parity)
                half_step(0, 0, first=True)
                half_step(1, 1)
                with engine.Fori(1, B // 2) as r:
                    half_step(2 * r, 0)
                    half_step(2 * r + 1, 1)
                half_step(B, 0, last=True)
                merge(B - 1, 1)
            return run

        def since(engine, sem, n, lag):
            if isinstance(n, int) and n < lag:
                return
            engine.wait_ge(sem, n + (1 - lag))

        def acc(parity):
            return ps[0:TP, 6 + parity, 0:(H // 2) * (2 * HD + 1)].rearrange("p (h e) -> p h e", h=H // 2)

        with nc.Block() as block:

            @block.sync
            def _(sp):
                for i in range(4):
                    sp.dma_start(w[:, i], d["c1_W"][i].rearrange("(c p) n -> p c n", p=128)).then_inc(s["w"], 16)
                sp.dma_start(bqk[:], d["c1_bqk"]).then_inc(s["bias"], 16)
                for n in rows_of:
                    sp.dma_start(rows_of[n][:], d[f"c1_{n}"].partition_broadcast(KP)).then_inc(s["bias"], 16)
                sp.dma_start(rs[:], d["c1_scale"].partition_broadcast(TP)).then_inc(s["bias"], 16)
                sp.dma_start(mask_i[:], d["mask"]).then_inc(s["mask"], 16)

                def load(b, parity):
                    if not (isinstance(b, int) and b < 2):
                        sp.wait_ge(s["proj"], b * TILES - TILES)
                    sp.dma_start(ctx_rows[:, parity], src[:, :, bass.ds(b * S, S)]).then_inc(loaded[parity], 16)
                load(0, 0)
                load(1, 1)
                with sp.Fori(1, B // 2) as r:
                    load(2 * r, 0)
                    load(2 * r + 1, 1)

            @block.gpsimd
            def _(pool):
                nc.gpsimd.memset(v[:, :, :, :, 2 * HD:2 * HD + 1], 1.0).then_inc(s["ones"], 1)
                nc.gpsimd.memset(fold[:], 0.0).then_inc(s["const"], 1)
                nc.gpsimd.memset(half[:], 1.0).then_inc(s["const"], 1)
                pool.wait_ge(s["const"], 2)
                for i in range(2):
                    nc.gpsimd.affine_select(out=fold[:], in_=fold[:], compare_op=ALU.not_equal, fill=1.0,
                                            base=-i * T, pattern=[[-1, T]], channel_multiplier=1)\
                        .then_inc(s["fold"], 1)
                    pool.wait_ge(s["fold"], i + 1)
                nc.gpsimd.affine_select(out=half[:, 0:1], in_=half[:, 0:1], compare_op=ALU.is_ge, fill=0.0,
                                        base=T - 1, pattern=[[0, 1]], channel_multiplier=-1).then_inc(s["half"], 1)
                nc.gpsimd.affine_select(out=half[:, 1:2], in_=half[:, 1:2], compare_op=ALU.is_ge, fill=0.0,
                                        base=-T, pattern=[[0, 1]], channel_multiplier=1).then_inc(s["half"], 1)

            @block.tensor
            def _(pe):
                pe.wait_ge(s["w"], 64)
                for o in range(C2):
                    for c in range(C2):
                        last = nc.tensor.matmul(ps[:, 2 + o, 0:TOKENS], w[:, 0, c, o * 128:(o + 1) * 128],
                                                k.x_T[:, c, :], start=(c == 0), stop=(c == C2 - 1))
                last.then_inc(s["q"], 1)
                pe.wait_ge(s["fold"], 2)
                pe.wait_ge(s["ones"], 1)

                def proj(b, parity, i):
                    if i == 0:
                        pe.wait_ge(loaded[parity], 16 + (b - parity) * 8)
                    if i < 2:
                        since(pe, s["v_out"], b * 6 + i, 2)
                    elif i < 8:
                        pe.wait_ge(s["k_out"], b * 6 + (i - 1))
                    else:
                        pe.wait_ge(s["v_out"], b * 6 + (i - 7))
                    if i < 6:
                        g, o = i // 2, i % 2
                        for c in range(C2):
                            last = nc.tensor.matmul(ps[:, i % 2, 0:GK], w[:, 1, c, o * 128:(o + 1) * 128],
                                                    ctx_rows[:, parity, c, g * GK:(g + 1) * GK],
                                                    start=(c == 0), stop=(c == C2 - 1))
                    else:
                        for j in range(2):
                            t = 2 * (i - 6) + j
                            for c in range(C2):
                                last = nc.tensor.matmul(ps[0:KP, i % 2, j * D:(j + 1) * D],
                                                        ctx_rows[:, parity, c, t * KP:(t + 1) * KP],
                                                        w[:, 2, c, :], start=(c == 0), stop=(c == C2 - 1))
                    last.then_inc(s["proj"], 1)

                def product(b, parity, i):
                    n = b * TILES + i
                    since(pe, s["exp"], n, 0)
                    if i == 0:
                        pe.wait_ge(s["v_out"], b * 6 + 6)
                        since(pe, s["ctx_out"], b, 2)
                    for h in range(H // 2):
                        last = nc.tensor.matmul(acc(parity)[:, h, :], probs[:, i % 2, h * TP:(h + 1) * TP],
                                                v[:, parity, i, h, :], start=(i == 0 and h == 0), stop=True,
                                                skip_group_check=True)
                    last.then_inc(s["pv"], 1)

                def tile(b, parity, i):
                    n = b * TILES + i
                    if i == 0:
                        pe.wait_ge(s["k_out"], b * 6 + 6)
                        if isinstance(b, int) and b == 0:
                            pe.wait_ge(s["q_heads"], C2)
                    since(pe, s["clip"], n, 2)
                    for c in range(C2):
                        last = nc.tensor.matmul(
                            ps[0:KP, 2 + 2 * (i % 2) + c, 0:TOKENS].rearrange("p (h t) -> p h t", h=8),
                            k_T[:, parity, c, i * KP:(i + 1) * KP], q_heads[:, c, :, bass.ds(b * T, T)],
                            start=True, stop=True)
                    last.then_inc(s["scored"], 1)
                    if i >= 1:
                        product(b, parity, i - 1)
                    if i == TILES - 1:
                        product(b, parity, i)

                def merge(b, parity):
                    pe.wait_ge(s["own"], b + 1)
                    for c in range(C2):
                        last = nc.tensor.matmul(ps[:, 6 + parity, c * T:(c + 1) * T],
                                                out[:, parity, c * 128:(c + 1) * 128], fold[:],
                                                start=True, stop=True)
                    last.then_inc(s["merged"], 1)

                halves(proj, tile, merge)(pe)
                pe.wait_ge(s["ctx_out"], B)
                for t in range(TT):
                    for c in range(C2):
                        last = nc.tensor.matmul(y[:, t, :], ctx_T[:, c, t * TP:(t + 1) * TP], w[:, 3, c, :],
                                                start=(c == 0), stop=(c == C2 - 1))
                last.then_inc(s["y"], 1)
                norm_tensor(nc, pe, k, s, ps[:, 2:4, 0:TOKENS])

            @block.scalar
            def _(act):
                act.wait_ge(s["q"], 1)
                act.wait_ge(s["rs"], 1)
                for c in range(C2):
                    nc.scalar.activation(q_T[:, c, :], ps[:, 2 + c, 0:TOKENS], ACT.Identity, scale=0.25,
                                         bias=bqk[:, 0, c:c + 1]).then_inc(s["q_sb"], 1)
                act.wait_ge(s["attend"], 2)

                def proj(b, parity, i):
                    if i < 6:
                        g, o = i // 2, i % 2
                        act.wait_ge(s["proj"], b * TILES + (i + 1))
                        if i == 0 and not (isinstance(b, int) and b < 2):
                            act.wait_ge(s["scored"], b * TILES - TILES)
                        nc.scalar.activation(k_T[:, parity, o, g * GK:(g + 1) * GK], ps[:, i % 2, 0:GK],
                                             ACT.Identity, bias=bqk[:, 1, o:o + 1]).then_inc(s["k_out"], 1)

                def tile(b, parity, i):
                    n = b * TILES + i
                    since(act, s["clip"], n, 0)
                    since(act, s["pv"], n, 2)
                    at = bass.ds(n, 1)
                    nc.scalar.activation(probs[:, i % 2], clipped[:, i % 2], ACT.Exp,
                                         scale=attend[:, 0, at], bias=attend[:, 1, at]).then_inc(s["exp"], 1)

                def merge(b, parity):
                    act.wait_ge(s["merged"], b + 1)
                    nc.scalar.activation(ctx_T[:, :, bass.ds(b * T, T)],
                                         ps[:, 6 + parity, 0:C2 * T].rearrange("p (c t) -> p c t", c=C2),
                                         ACT.Copy).then_inc(s["ctx_out"], 1)

                halves(proj, tile, merge)(act)
                act.wait_ge(s["var2"], 1)
                nc.scalar.activation(k.std[:], k.mv[:, :, 1], ACT.Sqrt, bias=EPS).then_inc(s["std2"], 1)
                norm_scalar(nc, act, k, s, ps[:, 2:4, 0:TOKENS])

            @block.vector
            def _(dve):
                dve.wait_ge(s["bias"], 96)
                nc.vector.tensor_scalar(bqk[:, 0, :], bqk[:, 0, :], 0.25, None, ALU.mult).then_inc(s["rs"], 1)
                nc.vector.tensor_scalar(rs[:], rs[:], 0.0, 0.3, ALU.max, ALU.min).then_inc(s["rs"], 1)
                dve.wait_ge(s["mask"], 16)
                nc.vector.tensor_scalar(attend[:, 0, :], mask_i[:], 0.5, None, ALU.is_gt).then_inc(s["attend"], 1)
                dve.wait_ge(s["attend"], 1)
                nc.vector.tensor_scalar(attend[:, 1, :], attend[:, 0, :], 50.0, -50.0, ALU.mult, ALU.add)\
                    .then_inc(s["attend"], 1)
                dve.wait_ge(s["q_sb"], C2)
                for c in range(C2):
                    nc.vector.tensor_tensor(q_heads[:, c], bcast(q_T[:, c:c + 1, :], [128, 8, TOKENS]),
                                            bcast(k.head_mask[:].unsqueeze(2), [128, 8, TOKENS]), ALU.mult)\
                        .then_inc(s["q_heads"], 1)
                dve.wait_ge(s["half"], 2)

                def proj(b, parity, i):
                    if i >= 6:
                        j = i - 6
                        dve.wait_ge(s["proj"], b * TILES + (i + 1))
                        if j == 0 and not (isinstance(b, int) and b < 2):
                            dve.wait_ge(s["pv"], b * TILES - TILES)
                        nc.vector.tensor_tensor(
                            v[:, parity, 2 * j:2 * j + 2, :, 0:2 * HD],
                            ps[0:KP, i % 2, :].rearrange("p (t h e) -> p t h e", t=2, e=2 * HD),
                            bcast(rows_of["bv"][:].rearrange("p (h e) -> p h e", e=2 * HD).unsqueeze(1),
                                  [KP, 2, H // 2, 2 * HD]), ALU.add).then_inc(s["v_out"], 1)

                def tile(b, parity, i):
                    n = b * TILES + i
                    since(dve, s["scored"], n, 0)
                    since(dve, s["exp"], n, 2)
                    nc.vector.tensor_scalar(clipped[:, i % 2].rearrange("p (c n) -> p c n", c=C2),
                                            ps[0:KP, 2 + 2 * (i % 2):4 + 2 * (i % 2), 0:TOKENS], -50.0, 50.0,
                                            ALU.max, ALU.min).then_inc(s["clip"], 1)
                    if i == TILES - 1:
                        normalise(b, parity)

                def normalise(b, parity):
                    dve.wait_ge(s["pv"], b * TILES + TILES)
                    n = [0]

                    def link(ins):
                        n[0] += 1
                        ins.then_inc(s["link"], 1)
                        dve.wait_ge(s["link"], b * 6 + n[0])
                    total = acc(parity)[:, :, 2 * HD]
                    link(nc.vector.reciprocal(sums[:, 0, :], total))
                    link(nc.vector.tensor_tensor(sums[:, 1, :], sums[:, 0, :], total, ALU.mult))
                    link(nc.vector.tensor_scalar(sums[:, 2, :], sums[:, 1, :], 1e-8, None, ALU.add))
                    link(nc.vector.reciprocal(sums[:, 3, :], sums[:, 2, :]))
                    link(nc.vector.tensor_tensor(sums[:, 1, :], sums[:, 0, :], sums[:, 3, :], ALU.mult))
                    link(nc.vector.tensor_tensor(own[:], bcast(sums[:, 1, :].unsqueeze(2), [TP, H // 2, 2]),
                                                 bcast(half[:].unsqueeze(1), [TP, H // 2, 2]), ALU.mult))
                    since(dve, s["merged"], b, 2)
                    nc.vector.tensor_tensor(
                        out[:, parity].rearrange("p (h a e) -> p h a e", h=H // 2, a=2),
                        acc(parity)[:, :, 0:2 * HD].rearrange("p h (a e) -> p h a e", a=2),
                        bcast(own[:].unsqueeze(3), [TP, H // 2, 2, HD]), ALU.mult).then_inc(s["own"], 1)

                halves(proj, tile, lambda b, parity: None)(dve)
                dve.wait_ge(s["y"], 1)
                n0 = B * 6
                n = [n0]

                def link(ins):
                    n[0] += 1
                    ins.then_inc(s["link"], 1)
                    dve.wait_ge(s["link"], n[0])

                row = lambda name: bcast(rows_of[name][0:TP, :].unsqueeze(1), [TP, TT, D])
                link(nc.vector.tensor_tensor(delta[:], y, row("bo"), ALU.add))
                link(nc.vector.tensor_scalar(delta[:], delta[:], rs[:, 0:1], None, ALU.mult))
                for t in range(TT):
                    last = nc.vector.bn_stats(k.stats[:, t, :], delta[:, t, :])
                link(last)
                for t in range(TT):
                    last = nc.vector.bn_aggr(k.mv[:, t, :], k.stats[:, t, :])
                last.then_inc(s["var2"], 1)
                dve.wait_ge(s["std2"], 1)
                link(nc.vector.reciprocal(k.rstd[:], k.std[:]))
                for t in range(TT):
                    last = nc.vector.tensor_scalar(delta[:, t, :], delta[:, t, :], k.mv[:, t, 0:1],
                                                   k.rstd[:, t:t + 1], ALU.subtract, ALU.mult)
                link(last)
                link(nc.vector.tensor_tensor(delta[:], delta[:], row("gamma"), ALU.mult))
                link(nc.vector.tensor_tensor(delta[:], delta[:], row("beta"), ALU.add))
                link(nc.vector.tensor_copy(k.res[:], k.x_tok[:]))
                norm_vector(nc, dve, link, k, s, delta[:])


def layer1_experts(nc, k, d):
    with ExitStack() as ctx:
        sb = lambda n, sh, dt=F32: ctx.enter_context(nc.sbuf_tensor(n, sh, dt))
        EC = E * F // 128
        SC = -(-FS // 128)
        size = lambda n: min(128, FS - (n - EC) * 128) if n >= EC else 128
        wr = sb("f1_wr", [128, C2, E])
        wgu = sb("f1_wgu", [128, 2, C2, E * F])
        sgu = sb("f1_sgu", [128, 2, C2, FS])
        wd = sb("f1_wd", [128, EC + SC, D])
        gates = sb("f1_gates", [TP, TT, E])
        gates_T = sb("f1_gatesT", [E, TOKENS])
        select = sb("f1_select", [E, E * F])
        silu = sb("f1_silu", [128, 2, TOKENS])
        mid = sb("f1_mid", [128, TOKENS])
        inner = sb("f1_inner", [128, 2, TOKENS])
        ps = ctx.enter_context(nc.psum_tensor("f1_ps", [128, 8, 512], F32))
        s = k.sems("f1", "wr wgu sgu wd logits shifted exp gates gT gT_sb sel select up silu mid inner down link "
                   "out " + NORM_SEMS)
        logits = ps[0:TP, 0, 0:TT * E].rearrange("p (t e) -> p t e", e=E)
        y = ps[0:TP, 6:8, :].rearrange("p b (t n) -> p (b t) n", n=D)
        with nc.Block() as block:

            @block.sync
            def _(sp):
                sp.dma_start(wr[:], d["f1_wr"].rearrange("(c p) n -> p c n", p=128)).then_inc(s["wr"], 16)
                for i in range(2):
                    sp.dma_start(wgu[:, i], d["f1_Wgu"][i].rearrange("(c p) n -> p c n", p=128))\
                        .then_inc(s["wgu"], 16)
                for i in range(2):
                    sp.dma_start(sgu[:, i], d["f1_Sgu"][i].rearrange("(c p) n -> p c n", p=128))\
                        .then_inc(s["sgu"], 16)
                sp.dma_start(wd[:, 0:EC, :], d["f1_Wd"].rearrange("(c p) n -> p c n", p=128)).then_inc(s["wd"], 16)
                for n in range(EC, EC + SC):
                    at = (n - EC) * 128
                    sp.dma_start(wd[0:size(n), n, :], d["f1_Sd"][at:at + size(n), :]).then_inc(s["wd"], 16)
                sp.wait_ge(s["x_ready"], 1)
                sp.dma_start(d["out"].rearrange("(t p) n -> p t n", p=TP), k.x_tok[:]).then_inc(s["out"], 16)
                sp.wait_ge(s["out"], 16)

            @block.gpsimd
            def _(pool):
                nc.gpsimd.memset(select[:], 1.0).then_inc(s["sel"], 1)
                pool.wait_ge(s["sel"], 1)
                nc.gpsimd.affine_select(out=select[:], in_=select[:], compare_op=ALU.is_ge, fill=0.0, base=0,
                                        pattern=[[1, E * F]], channel_multiplier=-F).then_inc(s["sel"], 1)
                pool.wait_ge(s["sel"], 2)
                nc.gpsimd.affine_select(out=select[:], in_=select[:], compare_op=ALU.is_ge, fill=0.0, base=F - 1,
                                        pattern=[[-1, E * F]], channel_multiplier=F).then_inc(s["select"], 1)

            @block.tensor
            def _(pe):
                pe.wait_ge(s["wr"], 16)
                for t in range(TT):
                    for c in range(C2):
                        last = nc.tensor.matmul(logits[:, t, :], k.x_T[:, c, t * TP:(t + 1) * TP], wr[:, c, :],
                                                start=(c == 0), stop=(c == C2 - 1))
                last.then_inc(s["logits"], 1)

                def up(n):
                    if n < 2:
                        pe.wait_ge(s["shifted"], 1)
                    else:
                        pe.wait_ge(s["inner"], n - 1)
                    of = sgu if n >= EC else wgu
                    at = (n - EC if n >= EC else n) * 128
                    for i in range(2):
                        for c in range(C2):
                            last = nc.tensor.matmul(ps[0:size(n), 2 * i + n % 2, 0:TOKENS],
                                                    of[:, i, c, at:at + size(n)], k.x_T[:, c, :],
                                                    start=(c == 0), stop=(c == C2 - 1))
                    if n < EC:
                        if n == 0:
                            pe.wait_ge(s["gates"], 1)
                            for t in range(TT):
                                tr = nc.tensor.transpose(ps[0:E, 5, t * TP:(t + 1) * TP], gates[:, t, :],
                                                         k.ident[0:TP, 0:TP])
                            tr.then_inc(s["gT"], 1)
                            pe.wait_ge(s["gT_sb"], 1)
                            pe.wait_ge(s["select"], 1)
                        last = nc.tensor.matmul(ps[:, 4 + n % 2, 0:TOKENS], select[:, at:at + 128], gates_T[:],
                                                start=True, stop=True)
                    last.then_inc(s["up"], 1)

                def down(n):
                    pe.wait_ge(s["inner"], n + 1)
                    for t in range(TT):
                        last = nc.tensor.matmul(y[:, t, :], inner[0:size(n), n % 2, t * TP:(t + 1) * TP],
                                                wd[0:size(n), n, :], start=(n == 0 and t % 2 == 0), stop=True,
                                                skip_group_check=True)
                    last.then_inc(s["down"], 1)

                pe.wait_ge(s["wgu"], 32)
                for n in range(EC + SC):
                    if n == EC:
                        pe.wait_ge(s["sgu"], 32)
                    up(n)
                    if n == 1:
                        pe.wait_ge(s["wd"], 16 * (1 + SC))
                    if n >= 1:
                        down(n - 1)
                down(EC + SC - 1)

            @block.scalar
            def _(act):
                act.wait_ge(s["shifted"], 1)
                nc.scalar.activation(k.route[:, :, 8:16], k.route[:, :, 0:8], ACT.Exp).then_inc(s["exp"], 1)
                act.wait_ge(s["gT"], 1)
                nc.scalar.activation(gates_T[:], ps[0:E, 5, 0:TOKENS], ACT.Copy).then_inc(s["gT_sb"], 1)
                for n in range(EC + SC):
                    act.wait_ge(s["up"], n + 1)
                    if n >= 2:
                        act.wait_ge(s["inner"], n - 1)
                    nc.scalar.activation(silu[0:size(n), n % 2, :], ps[0:size(n), n % 2, 0:TOKENS], ACT.Silu)\
                        .then_inc(s["silu"], 1)
                act.wait_ge(s["var_ready"], 1)
                nc.scalar.activation(k.std[:], k.mv[:, :, 1], ACT.Sqrt, bias=EPS).then_inc(s["std_ready"], 1)

            @block.vector
            def _(dve):
                link = linker(dve, s["link"])
                link(nc.vector.tensor_copy(k.res[:], k.x_tok[:]))
                dve.wait_ge(s["logits"], 1)
                route_shift(nc, link, k, logits, s["shifted"])
                dve.wait_ge(s["exp"], 1)
                route_choose(nc, link, k, gates[:], False, s["gates"])
                for n in range(EC + SC):
                    r = size(n)
                    dve.wait_ge(s["silu"], n + 1)
                    if n >= 2:
                        dve.wait_ge(s["down"], n - 1)
                    if 1 <= n < EC:
                        dve.wait_ge(s["inner"], n)
                    to = mid[0:r, :] if n < EC else inner[0:r, n % 2, :]
                    nc.vector.tensor_tensor(to, silu[0:r, n % 2, :], ps[0:r, 2 + n % 2, 0:TOKENS], ALU.mult)\
                        .then_inc(s["mid"] if n < EC else s["inner"], 1)
                    if n < EC:
                        dve.wait_ge(s["mid"], n + 1)
                        nc.vector.tensor_tensor(inner[:, n % 2, :], mid[:], ps[:, 4 + n % 2, 0:TOKENS], ALU.mult)\
                            .then_inc(s["inner"], 1)
                dve.wait_ge(s["down"], EC + SC)
                norm_vector(nc, dve, link, k, s, y)


def program(nc, k, d, phases=99):
    ctx = k.ctx
    sb = lambda n, sh, dt=F32: ctx.enter_context(nc.sbuf_tensor(n, sh, dt))
    k.x_tok = sb("x_tok", [TP, TT, D])
    k.x_T = sb("x_T", [128, C2, TOKENS])
    k.res = sb("res", [TP, TT, D])
    k.sum = sb("sum", [TP, TT, D])
    k.stats = sb("stats", [TP, TT, 6])
    k.mv = sb("mv", [TP, TT, 2])
    k.std = sb("std", [TP, TT])
    k.rstd = sb("rstd", [TP, TT])
    k.ident = sb("ident", [128, 128])
    k.ident_b = sb("ident_b", [128, 128], BF16)
    k.route = sb("route", [TP, TT, 37])
    k.route_at = sb("route_at", [TP, TT, 8], U32)
    k.route_idx = sb("route_idx", [TP, TT, 8])
    k.expert_i = sb("expert_i", [TP, E], I32)
    k.expert = sb("expert", [TP, E])
    k.head_mask = sb("head_mask", [128, 8])
    k.q_parts = nc.dram_tensor("q_parts", (3, D, TOKENS), BF16).ap()
    k.k_parts = nc.dram_tensor("k_parts", (3, D, KEYS), BF16).ap()
    sublayers = [layer0_attention, layer0_context, layer0_query, layer0_cross_attention, layer0_mlp,
                 layer1_attention, layer1_cross_attention, layer1_experts]
    with ExitStack() as cross:
        for n, sublayer in enumerate(sublayers[:phases]):
            if n == 1:
                k.v_steps = cross.enter_context(nc.sbuf_tensor("v_steps", [KP, KT, D], BF16))
                k.v_scale = cross.enter_context(nc.sbuf_tensor("v_scale", [KP, D], F32))
            if n == 4:
                cross.close()
            if n in (4, 7):
                k.renew_sems()
            sublayer(nc, k, d)


def build(nc, arrays, phases=99):
    d = {n: nc.dram_tensor(f"in_{n}", v.shape, mybir.dt.from_np(v.dtype), kind="ExternalInput").ap()
         for n, v in arrays.items()}
    d["out"] = nc.dram_tensor("out", (TOKENS, D), F32, kind="ExternalOutput").ap()
    with ExitStack() as ctx:
        program(nc, Core(nc, ctx), d, phases)


def layout(inputs):
    a = {n: np.asarray(v) for n, v in inputs.items()}
    chunked = lambda b: b.reshape(-1, 128).T
    x = a["x"].reshape(TOKENS, D)
    gu = a["L1_ffn_gate_up_weights"]
    out = {
        "x": x, "x_T": x.T, "ctx_T": a["ctx_2048"].reshape(KEYS, D).T,
        "mask": a["mask_BxS2_ik0"].reshape(KT, KP).T,
        "a0_Wq": a["L0_attn_Wq"], "a0_Wk": a["L0_attn_Wk"], "a0_Wv": a["L0_attn_Wv"], "a0_Wo": a["L0_attn_Wo"],
        "a0_bqk": np.stack([chunked(a["L0_attn_bq"]), chunked(a["L0_attn_bk"])], 1),
        "a0_bv": a["L0_attn_bv"], "a0_bo": a["L0_attn_bo"],
        "c0_Wq": a["L0_xattn_Wq"], "c0_bq": a["L0_xattn_bq"],
        "c0_Wkv": a["L0_xattn_Wkv"], "c0_bkv": a["L0_xattn_bkv"].reshape(1, 2 * D),
        "c0_Wp": a["L0_xattn_Wp"], "c0_bp": a["L0_xattn_bp"],
        "f0_w1": a["L0_ffn_w1"].T, "f0_w3": a["L0_ffn_w3"].T, "f0_w2": a["L0_ffn_w2"].T, "f0_wr": a["L0_ffn_wr"].T,
        "a1_Wqkv": np.stack([a["L1_attn_Wq"], a["L1_attn_Wk"], a["L1_attn_Wv"]]), "a1_Wo": a["L1_attn_Wo"],
        "a1_bqk": np.stack([chunked(a["L1_attn_bq"]), chunked(a["L1_attn_bk"])], 1),
        "a1_bv": a["L1_attn_bv"], "a1_bo": a["L1_attn_bo"],
        "c1_W": np.stack([a["L1_xattn_" + n].T for n in ("Wq", "Wk", "Wv", "Wo")]),
        "c1_bqk": np.stack([chunked(a["L1_xattn_bq"]), chunked(a["L1_xattn_bk"])], 1),
        "c1_bv": a["L1_xattn_bv"], "c1_bo": a["L1_xattn_bo"],
        "c1_gamma": a["L1_xattn_ln_gamma"], "c1_beta": a["L1_xattn_ln_beta"],
        "c1_scale": a["L1_xattn_residual_scale"].reshape(1),
        "f1_wr": a["L1_ffn_gate_weight"].T,
        "f1_Wgu": np.stack([gu[:, :F].reshape(E * F, D).T, gu[:, F:].reshape(E * F, D).T]),
        "f1_Wd": a["L1_ffn_down_weights"].transpose(0, 2, 1).reshape(E * F, D),
        "f1_Sgu": np.stack([a["L1_ffn_shared_gate_up"][:FS].T, a["L1_ffn_shared_gate_up"][FS:].T]),
        "f1_Sd": a["L1_ffn_shared_down"].T,
    }
    return {n: np.ascontiguousarray(v) for n, v in out.items()}


def kernel(**inputs):
    import concourse.bacc as bacc
    from concourse.bass_utils import run_bass_kernel_spmd

    arrays = layout(inputs)
    nc = bacc.Bacc("TRN2", target_bir_lowering=False, num_devices=1)
    build(nc, arrays)
    r = run_bass_kernel_spmd(nc, [{f"in_{n}": v for n, v in arrays.items()}], core_ids=[0])
    return r.results[0]["out"].reshape(B, T, D)
```

```python
from contextlib import ExitStack

import numpy as np
import concourse.bass as bass
from concourse import mybir
from concourse.alu_op_type import AluOpType as ALU

F32 = mybir.dt.float32
BF16 = mybir.dt.bfloat16
I16 = mybir.dt.int16
I32 = mybir.dt.int32
U32 = mybir.dt.uint32
ACT = mybir.ActivationFunctionType
AX = mybir.AxisListType

B, T, D, S = 8, 56, 256, 1500
TOKENS = B * T
TP = 2 * T
TT = TOKENS // TP
C2 = D // 128
KEYS = B * S
KP = 125
KT = KEYS // KP
H = 16
HD = D // H
DH0 = 128
EPS = 1e-5
LN255 = float(np.log(255.0))
MASKED = -1e30
E, F, FS = 8, 176, 352
UNIT = 2 * KP
V_STEP = 2
UNITS = KEYS // UNIT
P1_KEYS = 1000
P1_STEPS = KEYS // P1_KEYS
HEAD_STEPS = 48
PARTS = (0, 1, 2, 0, 1, 0)
K_PARTS = (0, 0, 0, 1, 1, 2)
QK_ROWS = 16 * len(PARTS)


class Core:

    def __init__(self, nc, ctx):
        self.nc, self.ctx = nc, ctx
        self.held = []

    def sem(self, name):
        self.held.append(self.nc.alloc_semaphore(name))
        return self.held[-1]

    def renew_sems(self):
        with self.nc.Block() as block:

            @block.gpsimd
            def _(pool):
                for sem in self.held:
                    pool.sem_clear(sem)

        for sem in self.held:
            self.nc.release_semaphore(sem)
        self.held = []

    def sems(self, prefix, names):
        return {n: self.sem(f"{prefix}_{n}") for n in names.split()}


def linker(engine, sem):
    done = [0]

    def link(instruction):
        done[0] += 1
        instruction.then_inc(sem, 1)
        engine.wait_ge(sem, done[0])

    return link


def bcast(ap, shape):
    return ap.broadcast_to(shape)


NORM_SEMS = "var_ready std_ready x_ready xT_psum xT_ready"


def norm_vector(nc, dve, link, k, s, y):
    link(nc.vector.tensor_tensor(k.sum[:], y, k.res[:], ALU.add))
    for t in range(TT):
        last = nc.vector.bn_stats(k.stats[:, t, :], k.sum[:, t, :])
    link(last)
    for t in range(TT):
        last = nc.vector.bn_aggr(k.mv[:, t, :], k.stats[:, t, :])
    last.then_inc(s["var_ready"], 1)
    dve.wait_ge(s["std_ready"], 1)
    link(nc.vector.reciprocal(k.rstd[:], k.std[:]))
    for t in range(TT):
        last = nc.vector.tensor_scalar(k.x_tok[:, t, :], k.sum[:, t, :], k.mv[:, t, 0:1],
                                       k.rstd[:, t:t + 1], ALU.subtract, ALU.mult)
    last.then_inc(s["x_ready"], 1)


def norm_scalar(nc, act, k, s, xT_psum):
    act.wait_ge(s["var_ready"], 1)
    nc.scalar.activation(k.std[:], k.mv[:, :, 1], ACT.Sqrt, bias=EPS).then_inc(s["std_ready"], 1)
    act.wait_ge(s["xT_psum"], 1)
    nc.scalar.activation(k.x_T[:], xT_psum, ACT.Copy).then_inc(s["xT_ready"], 1)


def transpose_rows(nc, k, out, rows):
    for c in range(C2):
        for t in range(TT):
            last = nc.tensor.transpose(out[:, c, t * TP:(t + 1) * TP],
                                       rows[:, t, c * 128:(c + 1) * 128], k.ident[0:TP, 0:TP])
    return last


def norm_tensor(nc, pe, k, s, xT_psum):
    pe.wait_ge(s["x_ready"], 1)
    transpose_rows(nc, k, xT_psum, k.x_tok).then_inc(s["xT_psum"], 1)


ATT_SEMS = ("s_ready t_link shifted exp_done p_ready pT_ready pT_sbuf o_ready o_sbuf")
GROUPS = TT * H // 4


def attention_tensor(nc, pe, k, s, score_operands, value_product, sc, pt, o):
    for g in range(GROUPS + 3):
        if g < GROUPS:
            p, heads = g // 4, range(4 * (g % 4), 4 * (g % 4) + 4)
            if g >= 2:
                pe.wait_ge(s["shifted"], g - 1)
            for j, h in enumerate(heads):
                q, kk = score_operands(p, h)
                last = nc.tensor.matmul(sc[g % 2][0:TP, j * TP:(j + 1) * TP], q, kk,
                                        start=True, stop=True)
            last.then_inc(s["s_ready"], 1)
        if 2 <= g <= GROUPS + 1:
            i = g - 2
            pe.wait_ge(s["p_ready"], i + 1)
            if i >= 2:
                pe.wait_ge(s["pT_sbuf"], i - 1)
            for j in range(4):
                last = nc.tensor.transpose(pt[i % 2][0:TP, j * TP:(j + 1) * TP],
                                           k.prob[:, i % 2, j, :], k.ident[0:TP, 0:TP])
            last.then_inc(s["pT_ready"], 1)
        if g >= 3:
            i = g - 3
            pe.wait_ge(s["pT_sbuf"], i + 1)
            if i >= 2:
                pe.wait_ge(s["o_sbuf"], i - 1)
            for j in range(4):
                h = 4 * (i % 4) + j
                last = value_product(o[i % 2], i // 4, h, j, k.probT[:, i % 2, j, :])
            last.then_inc(s["o_ready"], 1)


def attention_vector(nc, dve, k, s, add_term, sc):
    n = [0]

    def link(ins):
        n[0] += 1
        ins.then_inc(s["t_link"], 1)
        dve.wait_ge(s["t_link"], n[0])

    for g in range(GROUPS + 1):
        if g < GROUPS:
            dve.wait_ge(s["s_ready"], g + 1)
            if g >= 2:
                dve.wait_ge(s["exp_done"], g - 1)
            n[0] += 1
            add_term(g, k.shift[:, g % 2, :, :], sc[g % 2]).then_inc(s["t_link"], 1)
            dve.wait_ge(s["t_link"], n[0])
            nc.vector.tensor_reduce(k.row[:, g % 2, 0:4], k.shift[:, g % 2], AX.X, ALU.max, negate=True)\
                .then_inc(s["shifted"], 1)
        if g >= 1:
            i = g - 1
            dve.wait_ge(s["exp_done"], i + 1)
            link(nc.vector.reciprocal(k.row[:, i % 2, 8:12], k.row[:, i % 2, 4:8]))
            if i >= 2:
                dve.wait_ge(s["pT_ready"], i - 1)
            nc.vector.tensor_tensor(k.prob[:, i % 2], k.expo[:, i % 2],
                                    bcast(k.row[:, i % 2, 8:12].unsqueeze(2), [TP, 4, TP]),
                                    ALU.mult).then_inc(s["p_ready"], 1)


def attention_scalar(nc, act, k, s, pt, o, place_output):
    for g in range(GROUPS + 3):
        if g < GROUPS:
            act.wait_ge(s["shifted"], g + 1)
            if g >= 2:
                act.wait_ge(s["p_ready"], g - 1)
            for j in range(4):
                last = nc.scalar.activation(k.expo[:, g % 2, j], k.shift[:, g % 2, j], ACT.Exp,
                                            bias=k.row[:, g % 2, j:j + 1],
                                            accum_out=k.row[:, g % 2, 4 + j:5 + j])
            last.then_inc(s["exp_done"], 1)
        if 2 <= g <= GROUPS + 1:
            i = g - 2
            act.wait_ge(s["pT_ready"], i + 1)
            if i >= 2:
                act.wait_ge(s["o_ready"], i - 1)
            nc.scalar.activation(k.probT[:, i % 2], pt[i % 2][0:TP, 0:4 * TP].rearrange(
                "p (j t) -> p j t", j=4), ACT.Copy).then_inc(s["pT_sbuf"], 1)
        if g >= 3:
            i = g - 3
            act.wait_ge(s["o_ready"], i + 1)
            place_output(i, o[i % 2]).then_inc(s["o_sbuf"], 1)


def attention_buffers(nc, ctx, k):
    buffer = lambda name: ctx.enter_context(nc.sbuf_tensor(f"{name}_{k.phase}", [TP, 2, 4, TP], F32))
    k.shift, k.expo, k.prob, k.probT = buffer("shift"), buffer("expo"), buffer("prob"), buffer("probT")
    k.row = ctx.enter_context(nc.sbuf_tensor(f"row_{k.phase}", [TP, 2, 12], F32))


def layer0_attention(nc, k, d):
    k.phase = "a0"
    with ExitStack() as ctx:
        sb = lambda n, sh, dt=F32: ctx.enter_context(nc.sbuf_tensor(n, sh, dt))
        w = sb("a0_w", [128, 3, C2, H * DH0])
        wo = sb("a0_wo", [128, H, D])
        bqk = sb("a0_bqk", [128, 2, H])
        bv = sb("a0_bv", [TP, H * DH0])
        q_T = sb("a0_qT", [128, TOKENS, H])
        q_pair = sb("a0_qpair", [128, 2, 4, TP])
        k_T = sb("a0_kT", [128, H, TOKENS])
        v = sb("a0_v", [TP, TT, H * DH0])
        mask = sb("a0_mask", [TP, TP])
        bo = sb("a0_bo", [TP, D])
        attention_buffers(nc, ctx, k)
        kv_bias = k.sum[0:1, 0:2, :].rearrange("p t n -> p (t n)")
        bias_parts = sb("a0_kv_parts", [1, 3, 2 * D], BF16)
        o_T = w[:].rearrange("p a c n -> p (a c n)")[:, 0:H * TOKENS].rearrange("p (h n) -> p h n", h=H)
        ps = ctx.enter_context(nc.psum_tensor("a0_ps", [128, 8, 512], F32))
        s = k.sems("a0", "kv_w kv_bias kv_split kv_rows x wqk0 wqk1 wqk2 wqk3 wv wo bias qk_ready q_evac k_evac v_ready v_evac idm mask res y q_pair "
                   + ATT_SEMS + " " + NORM_SEMS)
        y = ps[0:TP, 6:8, :].rearrange("p b (t n) -> p (b t) n", n=D)
        sc, pt, o = [ps[:, i, :] for i in (0, 1)], [ps[:, i, :] for i in (2, 3)], [ps[:, i, :] for i in (4, 5)]
        with nc.Block() as block:

            @block.sync
            def _(sp):
                sp.dma_start(k.x_T[:], d["x_T"].rearrange("(c p) n -> p c n", p=128)).then_inc(s["x"], 16)
                for i in range(4):
                    of = slice(i * 4 * DH0, (i + 1) * 4 * DH0)
                    for n, name in enumerate(("a0_Wq", "a0_Wk")):
                        sp.dma_start(w[:, n, :, of], d[name].rearrange("(c p) n -> p c n", p=128)[:, :, of])\
                            .then_inc(s[f"wqk{i}"], 16)
                sp.dma_start(w[:, 2], d["a0_Wv"].rearrange("(c p) n -> p c n", p=128)).then_inc(s["wv"], 16)
                sp.dma_start(wo[:], d["a0_Wo"].rearrange("(h p) n -> p h n", p=128)).then_inc(s["wo"], 16)
                sp.dma_start(kv_bias, d["c0_bkv"]).then_inc(s["kv_bias"], 16)
                sp.dma_start(k.kv_w, d["c0_Wkv"].rearrange("(c p) n -> p c n", p=128)).then_inc(s["kv_w"], 16)
                sp.wait_ge(s["kv_split"], 5)
                for i in range(3):
                    sp.dma_start(k.kv_bias_rows[i:i + 1, :], bias_parts[0:1, i, :]).then_inc(s["kv_rows"], 16)
                sp.wait_ge(s["kv_w"], 16)
                sp.wait_ge(s["kv_rows"], 48)

            @block.gpsimd
            def _(pool):
                nc.gpsimd.memset(k.ident[:], 0.0).then_inc(s["idm"], 1)
                pool.wait_ge(s["idm"], 1)
                nc.gpsimd.affine_select(out=k.ident[:], in_=k.ident[:], compare_op=ALU.not_equal, fill=1.0,
                                        base=0, pattern=[[-1, 128]], channel_multiplier=1).then_inc(s["idm"], 1)
                pool.wait_ge(s["idm"], 2)
                nc.gpsimd.tensor_copy(k.ident_b[:], k.ident[:]).then_inc(s["idm"], 1)
                nc.gpsimd.memset(mask[:], 0.0).then_inc(s["idm"], 1)
                pool.wait_ge(s["idm"], 4)
                nc.gpsimd.affine_select(out=mask[:], in_=mask[:], compare_op=ALU.is_ge, fill=MASKED, base=0,
                                        pattern=[[-1, TP]], channel_multiplier=1).then_inc(s["idm"], 1)
                pool.wait_ge(s["idm"], 5)
                nc.gpsimd.affine_select(out=mask[:, 0:T], in_=mask[:, 0:T], compare_op=ALU.is_ge, fill=MASKED,
                                        base=T - 1, pattern=[[0, T]], channel_multiplier=-1)\
                    .then_inc(s["mask"], 1)
                split = linker(pool, s["kv_split"])
                pool.wait_ge(s["kv_bias"], 16)
                for i in range(3):
                    split(nc.gpsimd.tensor_copy(bias_parts[:, i, :], kv_bias))
                    if i < 2:
                        split(nc.gpsimd.tensor_tensor(kv_bias, kv_bias, bias_parts[:, i, :], ALU.subtract))
                q_flat = q_T[:].rearrange("p (b r) h -> p b (r h)", b=B)
                pool.wait_ge(s["q_evac"], H)
                for g in range(GROUPS):
                    p, h = g // 4, 4 * (g % 4)
                    if g >= 2:
                        pool.wait_ge(s["s_ready"], g - 1)
                    nc.gpsimd.tensor_copy(q_pair[:, g % 2].rearrange("p j (b t) -> p b j t", b=2),
                                          q_flat[:, 2 * p:2 * p + 2, h * T:(h + 4) * T].rearrange(
                                              "p b (j t) -> p b j t", j=4)).then_inc(s["q_pair"], 1)

            @block.tensor
            def _(pe):
                pe.wait_ge(s["x"], 16)
                for h in range(H):
                    if h % 4 == 0:
                        pe.wait_ge(s[f"wqk{h // 4}"], 32)
                    for n in range(2):
                        if h >= 2:
                            pe.wait_ge(s["k_evac" if n else "q_evac"], h - 1)
                        for c in range(C2):
                            last = nc.tensor.matmul(ps[:, 2 * (h % 2) + n, 0:TOKENS],
                                                    w[:, n, c, h * DH0:(h + 1) * DH0], k.x_T[:, c, :],
                                                    start=(c == 0), stop=(c == C2 - 1))
                        last.then_inc(s["qk_ready"], 1)
                pe.wait_ge(s["wv"], 16)
                for i in range(TT * 4):
                    t, n = i // 4, i % 4
                    if i >= 2:
                        pe.wait_ge(s["v_evac"], i - 1)
                    for c in range(C2):
                        last = nc.tensor.matmul(ps[0:TP, 4 + i % 2, :], k.x_T[:, c, t * TP:(t + 1) * TP],
                                                w[:, 2, c, n * 512:(n + 1) * 512],
                                                start=(c == 0), stop=(c == C2 - 1))
                    last.then_inc(s["v_ready"], 1)
                pe.wait_ge(s["q_evac"], H)
                pe.wait_ge(s["k_evac"], H)
                pe.wait_ge(s["v_evac"], 4 * TT)
                pe.wait_ge(s["idm"], 3)

                def score_operands(p, h):
                    g = 4 * p + h // 4
                    if h % 4 == 0:
                        pe.wait_ge(s["q_pair"], g + 1)
                    return q_pair[:, g % 2, h % 4, :], k_T[:, h, p * TP:(p + 1) * TP]

                def value_product(out, p, h, j, probs):
                    return nc.tensor.matmul(out[:, j * TP:(j + 1) * TP], v[:, p, h * DH0:(h + 1) * DH0], probs,
                                            start=True, stop=True)

                attention_tensor(nc, pe, k, s, score_operands, value_product, sc, pt, o)
                pe.wait_ge(s["wo"], 16)
                pe.wait_ge(s["o_sbuf"], GROUPS)
                for t in range(TT):
                    for h in range(H):
                        last = nc.tensor.matmul(y[:, t, :], o_T[:, h, t * TP:(t + 1) * TP], wo[:, h, :],
                                                start=(h == 0), stop=(h == H - 1))
                last.then_inc(s["y"], 1)
                norm_tensor(nc, pe, k, s, ps[:, 0:2, 0:TOKENS])

            @block.scalar
            def _(act):
                act.dma_start(bqk[:], d["a0_bqk"]).then_inc(s["bias"], 16)
                act.dma_start(bv[:], d["a0_bv"].partition_broadcast(TP)).then_inc(s["bias"], 16)
                act.dma_start(bo[:], d["a0_bo"].partition_broadcast(TP)).then_inc(s["bias"], 16)
                act.dma_start(k.x_tok[:], d["x"].rearrange("(t p) n -> p t n", p=TP)).then_inc(s["bias"], 16)
                act.wait_ge(s["bias"], 64)
                for h in range(H):
                    act.wait_ge(s["qk_ready"], 2 * h + 1)
                    nc.scalar.activation(q_T[:, :, h], ps[:, 2 * (h % 2), 0:TOKENS], ACT.Identity,
                                         bias=bqk[:, 0, h:h + 1]).then_inc(s["q_evac"], 1)

                def place_output(g, bank):
                    h = 4 * (g % 4)
                    return nc.scalar.activation(
                        o_T[:, h:h + 4, (g // 4) * TP:(g // 4 + 1) * TP],
                        bank[:, 0:4 * TP].rearrange("p (j t) -> p j t", j=4), ACT.Copy)

                attention_scalar(nc, act, k, s, pt, o, place_output)
                norm_scalar(nc, act, k, s, ps[:, 0:2, 0:TOKENS])

            @block.vector
            def _(dve):
                link = linker(dve, s["res"])
                dve.wait_ge(s["bias"], 64)
                link(nc.vector.tensor_tensor(k.res[:], k.x_tok[:],
                                             bcast(bo[:].unsqueeze(1), [TP, TT, D]), ALU.add))
                for h in range(H):
                    dve.wait_ge(s["qk_ready"], 2 * h + 2)
                    nc.vector.tensor_scalar(k_T[:, h, :], ps[:, 2 * (h % 2) + 1, 0:TOKENS],
                                            bqk[:, 1, h:h + 1], None, ALU.add).then_inc(s["k_evac"], 1)
                for i in range(TT * 4):
                    t, n = i // 4, i % 4
                    dve.wait_ge(s["v_ready"], i + 1)
                    nc.vector.tensor_tensor(v[:, t, n * 512:(n + 1) * 512], ps[0:TP, 4 + i % 2, :],
                                            bv[:, n * 512:(n + 1) * 512], ALU.add).then_inc(s["v_evac"], 1)
                dve.wait_ge(s["mask"], 1)

                def add_term(g, out, scores):
                    return nc.vector.scalar_tensor_tensor(
                        out, scores[0:TP, 0:4 * TP].rearrange("p (j t) -> p j t", j=4), float(1.0 / np.sqrt(DH0)),
                        bcast(mask[:].unsqueeze(1), [TP, 4, TP]), ALU.mult, ALU.add)

                attention_vector(nc, dve, k, s, add_term, sc)
                dve.wait_ge(s["y"], 1)
                norm_vector(nc, dve, link, k, s, y)


def layer0_context(nc, k, d):
    with ExitStack() as ctx:
        sb = lambda n, sh, dt=F32: ctx.enter_context(nc.sbuf_tensor(n, sh, dt))
        w, bias_rows = k.kv_w, k.kv_bias_rows
        ones = sb("b0_ones", [3, KP], BF16)
        rows = sb("b0_ctx", [128, 3, C2, UNIT])
        k_max = sb("b0_kmax", [KP, 2, H * 2])
        k_scale = sb("b0_kscale", [KP, 3, H * 2])
        k_inv = sb("b0_kinv", [KP, H * 2])
        k_steps = sb("b0_ksteps", [KP, 2, 2, D], I16)
        k_back = sb("b0_kback", [KP, 3, 2, D])
        residue = sb("b0_residue", [128, 2, C2 * UNIT])
        parts = sb("b0_parts", [128, 3, 3, C2, 2 * UNIT], BF16)
        v_rows = sb("b0_v", [KP, KT, D])
        v_max = sb("b0_vmax", [KP, D])
        v_unit = sb("b0_vunit", [KP, D])
        v_all = sb("b0_vall", [KP, 2, D])
        v_int = k_steps
        ps = ctx.enter_context(nc.psum_tensor("b0_ps", [128, 8, 512], F32))
        s = k.sems("b0", "ones l0 l1 l2 kv k_read v_read link k_scale k_int k_float k_back kT hi "
                   "residue mid lo stored vlink vint vsteps vzero")
        loaded = [s["l0"], s["l1"], s["l2"]]
        ctx_T = d["ctx_T"].rearrange("(c p) n -> p c n", p=128)
        kd = k.k_parts
        IN_LOOP = 6
        ROUNDS = UNITS // IN_LOOP

        def rounds(engine, step, flush=lambda r: None):
            for r in range(2):
                for u in range(IN_LOOP):
                    step(r, u)
            with engine.Fori(2, ROUNDS) as r:
                for u in range(IN_LOOP):
                    step(r, u)
            flush(ROUNDS)

        def behind(work, r, u, lag):
            if u >= lag:
                work(r, u - lag)
            elif not (isinstance(r, int) and r == 0):
                work(r - 1, u - lag + IN_LOOP)

        def wait_unit(engine, sem, r, u, lag=0, per_unit=1):
            if isinstance(r, int) and r * IN_LOOP + u < lag:
                return
            engine.wait_ge(sem, per_unit * (r * IN_LOOP + (u - lag + 1)))

        with nc.Block() as block:

            @block.sync
            def _(sp):
                def load(r, u):
                    wait_unit(sp, s["kv"], r, u, 3)
                    sp.dma_start(rows[:, u % 3], ctx_T[:, :, bass.ds(r * (IN_LOOP * UNIT) + u * UNIT, UNIT)])\
                        .then_inc(loaded[u % 3], 16)

                def store(r, u):
                    if u % 2 == 0:
                        return
                    wait_unit(sp, s["lo"], r, u)
                    if not (isinstance(r, int) and r == 0 and u == 1):
                        sp.wait_ge(s["stored"], (3 * r + u // 2) * 48)
                    for i in range(3):
                        sp.dma_start(kd[i].rearrange("(c p) n -> p c n", p=128)[
                            :, :, bass.ds(r * (IN_LOOP * UNIT) + (u // 2) * 2 * UNIT, 2 * UNIT)],
                            parts[:, (u // 2) % 3, i]).then_inc(s["stored"], 16)

                def step(r, u):
                    load(r, u)
                    behind(store, r, u, 6)

                def flush(r):
                    for u in range(6):
                        behind(store, r, u, 6)
                rounds(sp, step, flush)
                sp.wait_ge(s["stored"], (UNITS // 2) * 48)

            @block.tensor
            def _(pe):
                pe.wait_ge(s["ones"], 1)

                def project(r, u):
                    pe.wait_ge(loaded[u % 3], r * 32 + (u // 3 + 1) * 16)
                    wait_unit(pe, s["k_int"], r, u, 3)
                    wait_unit(pe, s["v_read"], r, u, 3)
                    for kv in range(2):
                        of = slice(kv * D, (kv + 1) * D)
                        for j in range(2):
                            out = ps[0:KP, 2 * (u % 3) + kv, j * D:(j + 1) * D]
                            nc.tensor.matmul(out, ones[:], bias_rows[:, of], start=True, stop=False)
                            for c in range(C2):
                                last = nc.tensor.matmul(out, rows[:, u % 3, c, j * KP:(j + 1) * KP],
                                                        w[:, c, of], start=False, stop=(c == C2 - 1))
                    last.then_inc(s["kv"], 1)

                def turn(r, u):
                    wait_unit(pe, s["k_back"], r, u)
                    wait_unit(pe, s["residue"], r, u, 2)
                    for c in range(C2):
                        for j in range(2):
                            last = nc.tensor.transpose(
                                ps[:, 6 + u % 2, c * UNIT + j * KP:c * UNIT + (j + 1) * KP],
                                k_back[:, u % 3, j, c * 128:(c + 1) * 128], k.ident[0:KP, 0:KP])
                    last.then_inc(s["kT"], 1)

                def step(r, u):
                    project(r, u)
                    behind(turn, r, u, 2)

                def flush(r):
                    for u in range(2):
                        behind(turn, r, u, 2)
                rounds(pe, step, flush)

            @block.vector
            def _(dve):
                nc.vector.memset(ones[:], 1.0).then_inc(s["ones"], 1)
                nc.vector.memset(v_max[:], 0.0).then_inc(s["vzero"], 1)
                dve.wait_ge(s["vzero"], 1)

                def quantise(r, u):
                    n = r * IN_LOOP + u
                    heads = ps[0:KP, 2 * (u % 3), :].rearrange("p (j h e) -> p j h e", j=2, e=HD)
                    first = r * (2 * IN_LOOP) + 2 * u
                    wait_unit(dve, s["kv"], r, u)
                    nc.vector.tensor_reduce(k_max[:, u % 2, :].rearrange("p (j h) -> p j h", j=2), heads, AX.X,
                                            ALU.max, apply_absolute_value=True).then_inc(s["link"], 1)
                    wait_unit(dve, s["v_read"], r, u)
                    nc.vector.tensor_reduce(v_unit[:], v_rows[:, bass.ds(first, 2), :].rearrange(
                        "p t n -> p n t"), AX.X, ALU.max, apply_absolute_value=True)\
                        .then_inc(s["link"], 1)
                    dve.wait_ge(s["link"], 3 * n + 1)
                    wait_unit(dve, s["k_back"], r, u, 3)
                    nc.vector.tensor_scalar(k_scale[:, u % 3, :], k_max[:, u % 2, :], 1.0 / 127.0, 1e-8,
                                            ALU.mult, ALU.max).then_inc(s["k_scale"], 1)
                    dve.wait_ge(s["link"], 3 * n + 2)
                    wait_unit(dve, s["k_read"], r, u, 1)
                    nc.vector.tensor_tensor(v_max[:], v_max[:], v_unit[:], ALU.max)\
                        .then_inc(s["k_read"], 1)
                    wait_unit(dve, s["k_scale"], r, u)
                    nc.vector.reciprocal(k_inv[:], k_scale[:, u % 3, :]).then_inc(s["link"], 1)
                    dve.wait_ge(s["link"], 3 * n + 3)
                    wait_unit(dve, s["k_float"], r, u, 2)
                    nc.vector.tensor_tensor(
                        k_steps[:, u % 2].rearrange("p j (h e) -> p j h e", e=HD), heads,
                        bcast(k_inv[:].rearrange("p (j h) -> p j h", j=2).unsqueeze(3), [KP, 2, H, HD]),
                        ALU.mult).then_inc(s["k_int"], 1)

                def take_high(r, u):
                    wait_unit(dve, s["hi"], r, u)
                    wait_unit(dve, s["lo"], r, u, 2)
                    slot = (u // 2) % 3
                    nc.vector.tensor_tensor(
                        residue[:, u % 2, :].rearrange("p (c n) -> p c n", c=C2),
                        ps[:, 6 + u % 2, 0:C2 * UNIT].rearrange("p (c n) -> p c n", c=C2),
                        parts[:, slot, 0, :, (u % 2) * UNIT:(u % 2 + 1) * UNIT], ALU.subtract)\
                        .then_inc(s["residue"], 1)

                def step(r, u):
                    quantise(r, u)
                    behind(take_high, r, u, 3)

                def flush(r):
                    for u in range(3):
                        behind(take_high, r, u, 3)
                rounds(dve, step, flush)

                dve.wait_ge(s["vzero"], 2)
                vlink = linker(dve, s["vlink"])
                vlink(nc.vector.tensor_scalar(k.v_scale[0:KP, :], v_all[:, 0, :], 1.0 / 127.0, 1e-8,
                                              ALU.mult, ALU.max))
                vlink(nc.vector.reciprocal(v_all[:, 1, :], k.v_scale[0:KP, :]))
                for i in range(KT // V_STEP):
                    if i >= 2:
                        dve.wait_ge(s["vsteps"], i - 1)
                    nc.vector.tensor_tensor(v_int[:, i % 2], v_rows[:, i * V_STEP:(i + 1) * V_STEP, :],
                                            bcast(v_all[:, 1:2, :], [KP, V_STEP, D]), ALU.mult).then_inc(s["vint"], 1)

            @block.scalar
            def _(act):
                def keep_v(r, u):
                    wait_unit(act, s["kv"], r, u)
                    nc.scalar.activation(v_rows[:, bass.ds(r * (2 * IN_LOOP) + 2 * u, 2), :],
                                         ps[0:KP, 2 * (u % 3) + 1, :].rearrange("p (j n) -> p j n", j=2),
                                         ACT.Copy).then_inc(s["v_read"], 1)

                def to_float(r, u):
                    wait_unit(act, s["k_int"], r, u)
                    wait_unit(act, s["kT"], r, u, 3)
                    nc.scalar.activation(k_back[:, u % 3], k_steps[:, u % 2], ACT.Copy)\
                        .then_inc(s["k_float"], 1)

                def high(r, u):
                    slot, at = (u // 2) % 3, slice((u % 2) * UNIT, (u % 2 + 1) * UNIT)
                    wait_unit(act, s["kT"], r, u)
                    if u % 2 == 0 and not (isinstance(r, int) and r == 0):
                        act.wait_ge(s["stored"], (3 * r + (u // 2) - 2) * 48)
                    nc.scalar.activation(parts[:, slot, 0, :, at],
                                         ps[:, 6 + u % 2, 0:C2 * UNIT].rearrange("p (c n) -> p c n", c=C2),
                                         ACT.Copy).then_inc(s["hi"], 1)

                def mid(r, u):
                    slot, at = (u // 2) % 3, slice((u % 2) * UNIT, (u % 2 + 1) * UNIT)
                    wait_unit(act, s["residue"], r, u)
                    nc.scalar.activation(parts[:, slot, 1, :, at],
                                         residue[:, u % 2, :].rearrange("p (c n) -> p c n", c=C2),
                                         ACT.Copy).then_inc(s["mid"], 1)

                def step(r, u):
                    keep_v(r, u)
                    behind(high, r, u, 3)
                    to_float(r, u)
                    behind(mid, r, u, 3)

                def flush(r):
                    for u in range(3):
                        behind(high, r, u, 3)
                        behind(mid, r, u, 3)
                rounds(act, step, flush)
                for i in range(KT // V_STEP):
                    act.wait_ge(s["vint"], i + 1)
                    nc.scalar.activation(k.v_steps[0:KP, i * V_STEP:(i + 1) * V_STEP, :], v_int[:, i % 2],
                                         ACT.Copy).then_inc(s["vsteps"], 1)

            @block.gpsimd
            def _(pool):
                def step(r, u):
                    scale_back(r, u)
                    behind(low, r, u, 3)

                def flush(r):
                    for u in range(3):
                        behind(low, r, u, 3)

                def scale_back(r, u):
                    wait_unit(pool, s["k_float"], r, u)
                    nc.gpsimd.tensor_tensor(
                        k_back[:, u % 3].rearrange("p j (h e) -> p j h e", e=HD),
                        k_back[:, u % 3].rearrange("p j (h e) -> p j h e", e=HD),
                        bcast(k_scale[:, u % 3, :].rearrange("p (j h) -> p j h", j=2).unsqueeze(3),
                              [KP, 2, H, HD]), ALU.mult).then_inc(s["k_back"], 1)

                def low(r, u):
                    slot, at = (u // 2) % 3, slice((u % 2) * UNIT, (u % 2 + 1) * UNIT)
                    wait_unit(pool, s["mid"], r, u)
                    nc.gpsimd.tensor_tensor(parts[:, slot, 2, :, at],
                                            residue[:, u % 2, :].rearrange("p (c n) -> p c n", c=C2),
                                            parts[:, slot, 1, :, at], ALU.subtract).then_inc(s["lo"], 1)
                rounds(pool, step, flush)
                pool.wait_ge(s["k_read"], UNITS)
                nc.gpsimd.partition_all_reduce(v_all[:, 0, :], v_max[:], KP, bass.bass_isa.ReduceOp.absmax)\
                    .then_inc(s["vzero"], 1)


def load_head(sp, k, h, slot):
    for j, part in enumerate(K_PARTS):
        sp.dma_start(k.kx[16 * j:16 * j + 16, bass.ds(slot, 1), :],
                     k.k_parts[part, bass.ds(h * HD, HD), :]).then_inc(k.kx_loaded, 16)


def layer0_query(nc, k, d):
    with ExitStack() as ctx:
        sb = lambda n, sh, dt=F32: ctx.enter_context(nc.sbuf_tensor(n, sh, dt))
        w = sb("q0_w", [128, C2, D])
        bias = sb("q0_bias", [TP, D])
        q = sb("q0_q", [TP, TT, D])
        steps = sb("q0_steps", [TP, TT, D], I16)
        q_max = sb("q0_max", [TP, 4, TT * H])
        back = sb("q0_back", [TP, 3, TT, D])
        parts = sb("q0_parts", [TP, 3, TT, D], BF16)
        parts_T = sb("q0_partsT", [128, 3, C2, TOKENS], BF16)
        ps = ctx.enter_context(nc.psum_tensor("q0_ps", [128, 8, 512], F32))
        s = k.sems("q0", "ones load q link parts turned out stored")
        q_ps = ps[0:TP, 0:2, :].rearrange("p b (t n) -> p (b t) n", n=D)
        turned = ps[:, 2:5, :].bitcast(BF16)[:, :, 0:C2 * TOKENS].rearrange("p i (c n) -> p i c n", c=C2)
        heads = lambda x: x.rearrange("p t (h e) -> p (t h) e", e=HD)
        each = lambda i: bcast(q_max[:, i, :].unsqueeze(2), [TP, TT * H, HD])
        with nc.Block() as block:

            @block.sync
            def _(sp):
                sp.dma_start(w[:], d["c0_Wq"].rearrange("(c p) n -> p c n", p=128)).then_inc(s["load"], 16)
                sp.dma_start(bias[:], d["c0_bq"].partition_broadcast(TP)).then_inc(s["load"], 16)
                load_head(sp, k, 0, 0)
                sp.wait_ge(s["out"], 3)
                sp.dma_start(k.q_parts.rearrange("i (c p) n -> p i c n", p=128), parts_T[:])\
                    .then_inc(s["stored"], 16)
                sp.wait_ge(s["stored"], 16)

            @block.gpsimd
            def _(pool):
                nc.gpsimd.memset(k.kx[QK_ROWS:, 0, :], 1.0).then_inc(s["ones"], 1)
                pool.wait_ge(s["ones"], 1)

            @block.tensor
            def _(pe):
                pe.wait_ge(s["load"], 32)
                for t in range(TT):
                    for c in range(C2):
                        last = nc.tensor.matmul(q_ps[:, t, :], k.x_T[:, c, t * TP:(t + 1) * TP], w[:, c, :],
                                                start=(c == 0), stop=(c == C2 - 1))
                last.then_inc(s["q"], 1)
                for i in range(3):
                    pe.wait_ge(s["parts"], i + 1)
                    for c in range(C2):
                        for t in range(TT):
                            last = nc.tensor.transpose(turned[:, i, c, t * TP:(t + 1) * TP],
                                                       parts[:, i, t, c * 128:(c + 1) * 128],
                                                       k.ident_b[0:TP, 0:TP])
                    last.then_inc(s["turned"], 1)

            @block.vector
            def _(dve):
                link = linker(dve, s["link"])
                dve.wait_ge(s["load"], 32)
                dve.wait_ge(s["q"], 1)
                link(nc.vector.tensor_tensor(q[:], q_ps, bcast(bias[:].unsqueeze(1), [TP, TT, D]), ALU.add))
                link(nc.vector.tensor_reduce(q_max[:, 0, :], heads(q[:]), AX.X, ALU.max,
                                             apply_absolute_value=True))
                link(nc.vector.tensor_scalar(q_max[:, 1, :], q_max[:, 0, :], 0.25 / 127.0, 1e-8,
                                             ALU.mult, ALU.max))
                link(nc.vector.reciprocal(q_max[:, 2, :], q_max[:, 1, :]))
                link(nc.vector.tensor_scalar(q_max[:, 3, :], q_max[:, 2, :], 0.25, None, ALU.mult))
                link(nc.vector.tensor_tensor(heads(steps[:]), heads(q[:]), each(3), ALU.mult))
                link(nc.vector.scalar_tensor_tensor(heads(back[:, 0]), heads(steps[:]), -1.0, each(1),
                                                    ALU.mult, ALU.mult))
                for i in range(3):
                    nc.vector.tensor_copy(parts[:, i], back[:, i]).then_inc(s["parts"], 1)
                    if i < 2:
                        dve.wait_ge(s["parts"], i + 1)
                        link(nc.vector.tensor_tensor(back[:, i + 1], back[:, i], parts[:, i], ALU.subtract))

            @block.scalar
            def _(act):
                for i in range(3):
                    act.wait_ge(s["turned"], i + 1)
                    nc.scalar.activation(parts_T[:, i], turned[:, i], ACT.Copy).then_inc(s["out"], 1)


def layer0_cross_attention(nc, k, d):
    with ExitStack() as ctx:
        sb = lambda n, sh, dt=F32: ctx.enter_context(nc.sbuf_tensor(n, sh, dt))
        kx = k.kx
        qx = sb("c0_qx", [128, H, TOKENS], BF16)
        low = sb("c0_low", [TP, H, TT * P1_STEPS])
        sums = sb("c0_sums", [TP, H, TT * P1_STEPS])
        head_low = sb("c0_headlow", [TP, H, TT])
        row = sb("c0_row", [TP, 3, TT])
        row_parts = sb("c0_rowparts", [TP, TT, 3], BF16)
        v_now = sb("c0_vnow", [KP, 4, 2, 32], BF16)
        fold = sb("c0_fold", [128, HD])
        groups_out = sb("c0_groups", [128, TOKENS])
        steps = sb("c0_steps", [KP, 4, 2, TOKENS], I16)
        probs = sb("c0_probs", [KP, 4, 2, TOKENS], BF16)
        out = sb("c0_out", [TP, H, TT, HD])
        inv = sb("c0_inv", [TP, H, TT])
        ctx_rows = sb("c0_ctx", [TP, TT, D])
        ctx_T = sb("c0_ctxT", [128, C2, TOKENS])
        w = sb("c0_wp", [128, C2, D])
        bias = sb("c0_bp", [TP, D])
        side_w = k.shared_w[:].rearrange("p (i c n) -> p i c n", i=2, c=C2)
        side_bk = sb("c0_sidebk", [128, C2])
        side_bv = k.shared_rows
        side_rows = sb("c0_siderows", [128, 2, C2, UNIT])
        side_k = sb("c0_sidek", [128, 2, C2, UNIT])
        side_v = sb("c0_sidev", [KP, 2, 2, H, HD + 1])
        ps = ctx.enter_context(nc.psum_tensor("c0_ps", [128, 8, 512], F32))
        s = k.sems("c0", "side_w side_l0 side_l1 side_st0 side_st1 side_done side_out qx kx_ones qx_zero w fold pv_sb folded scored1 scored2 low act1 act2 cast pv row row_link row_ps row_sb out zero "
                   "tail diff weight ctx ctxT ctxT_sb y res " + NORM_SEMS)
        N1 = TT * P1_STEPS
        assert N1 == HEAD_STEPS and KT // 2 == HEAD_STEPS and P1_STEPS == HEAD_STEPS // 4
        y = ps[0:TP, 2:4, :].rearrange("p b (t n) -> p (b t) n", n=D)
        pv, row_ps = ps[:, 7, 0:TOKENS], ps[QK_ROWS:QK_ROWS + 3, 6, 0:TOKENS]
        folded = ps[0:TP, 6, 0:TT * HD]

        GROUPS1 = HEAD_STEPS // 4

        def until(engine, name, h, i, u, lag=0):
            if isinstance(h, int) and isinstance(i, int) and h * HEAD_STEPS + 4 * i + u < lag:
                return
            engine.wait_ge(s[name], h * HEAD_STEPS + (i * 4 + (u + 1 - lag)))

        def groups(engine, body, count=GROUPS1 - 1):
            body(0)
            with engine.Fori(1, count) as i:
                body(i)

        def below(h, n):
            return isinstance(h, int) and h < n

        def banks1(h, u):
            return 2 * u if below(h, 1) else 2 * (u % 2)

        def banks2(h, u):
            return 0 if isinstance(h, int) and h == H - 1 and u % 2 else 4

        SIDE_FROM, SIDE_UNITS = 3, 4
        assert (H - 1 - SIDE_FROM) * SIDE_UNITS == UNITS
        side_loaded, side_stored = (s["side_l0"], s["side_l1"]), (s["side_st0"], s["side_st1"])
        side_ps = ps[:, 6, :]

        def side_groups(engine, h, joint):
            joint(0)
            with engine.Fori(0, SIDE_UNITS // 2) as r:
                for a in range(2):
                    pair = (h - SIDE_FROM) * 2 + r
                    joint(r * 4 + (2 * a + 1), (0, pair, a))
                    joint(r * 4 + (2 * a + 2), (1, pair, a))
            joint(GROUPS1 - 3)
            joint(GROUPS1 - 2)

        def stages(engine, joint, tail):
            def stage(h, side=False):
                run = side_groups if side else lambda engine, h, body: groups(engine, body)
                run(engine, h, lambda i, item=None: joint(h, i, item))
                tail(h)
            for h in range(SIDE_FROM):
                stage(h)
            with engine.Fori(SIDE_FROM, H - 1) as h:
                stage(h, side=True)
            stage(H - 1)
            groups(engine, lambda i: joint(H, i, None), GROUPS1)

        at = lambda h: bass.ds(h, 1)
        flat = lambda ap: ap.rearrange("p a n -> p (a n)")

        with nc.Block() as block:

            @block.gpsimd
            def _(pool):
                nc.gpsimd.memset(fold[:], 0.0).then_inc(s["fold"], 1)
                for g in range(4):
                    pool.wait_ge(s["fold"], g + 1)
                    nc.gpsimd.affine_select(out=fold[:], in_=fold[:], compare_op=ALU.not_equal, fill=1.0,
                                            base=-32 * g, pattern=[[-1, HD]], channel_multiplier=1)\
                        .then_inc(s["fold"], 1)
                pool.wait_ge(s["fold"], 5)
                nc.gpsimd.memset(kx[QK_ROWS:, 1:3, :], 1.0).then_inc(s["kx_ones"], 1)

            @block.sync
            def _(sp):
                for j, part in enumerate(PARTS):
                    sp.dma_start(qx[16 * j:16 * j + 16, :, :], k.q_parts[part].rearrange(
                        "(h p) n -> p h n", p=HD)).then_inc(s["qx"], 16)
                sp.dma_start(w[:], d["c0_Wp"].rearrange("(c p) n -> p c n", p=128)).then_inc(s["w"], 16)
                sp.dma_start(bias[:], d["c0_bp"].partition_broadcast(TP)).then_inc(s["w"], 16)

                for i in range(2):
                    sp.dma_start(side_w[:, i], d["c1_W"][1 + i].rearrange("(c p) n -> p c n", p=128))\
                        .then_inc(s["side_w"], 16)
                sp.dma_start(side_bk[:], d["c1_bqk"][:, 1, :]).then_inc(s["side_w"], 16)
                sp.dma_start(side_bv[:], d["c1_bv"].partition_broadcast(KP)).then_inc(s["side_w"], 16)

                def load(h, slot):
                    if isinstance(h, int) and 0 < h < 3:
                        sp.wait_ge(k.kx_loaded, h * (16 * len(K_PARTS)))
                    load_head(sp, k, h, slot)

                def load_unit(m, pair, a):
                    if not (isinstance(m, int) and m < 2):
                        sp.wait_ge(s["side_done"], 2 * m - 2)
                        sp.wait_ge(side_stored[a], pair * 32)
                    sp.dma_start(side_rows[:, a], src[:, :, bass.ds(m * UNIT, UNIT)]).then_inc(side_loaded[a], 16)

                def store_unit(m, a):
                    sp.wait_ge(s["side_out"], 2 * m + 2)
                    sp.dma_start(k.k1_T.rearrange("(c p) n -> p c n", p=128)[:, :, bass.ds(m * UNIT, UNIT)],
                                 side_k[:, a]).then_inc(side_stored[a], 16)
                    sp.wait_ge(s["side_out"], 2 * m + 3)
                    sp.dma_start(k.v1.rearrange("(t p) n -> p t n", p=KP)[:, bass.ds(m * 2, 2), :],
                                 side_v[:, a].rearrange("p t h e -> p t (h e)")).then_inc(side_stored[a], 16)

                def during(h):
                    sp.wait_ge(s["scored1"], (h - 1) * HEAD_STEPS + 4)
                    for n in range(SIDE_UNITS):
                        m = (h - SIDE_FROM - 1) * SIDE_UNITS + n
                        load_unit(m, (h - SIDE_FROM - 1) * 2 + n // 2, n % 2)
                        if n == 0:
                            load(h, h % 3)
                        if not (isinstance(m, int) and m == 0):
                            store_unit(m - 1, (n - 1) % 2)

                src = d["ctx_T"].rearrange("(c p) n -> p c n", p=128)
                for h in range(1, 3):
                    load(h, h)
                sp.wait_ge(s["scored1"], 2 * HEAD_STEPS + 4)
                load(3, 0)
                during(SIDE_FROM + 1)
                with sp.Fori(SIDE_FROM + 2, H) as h:
                    during(h)
                store_unit(UNITS - 1, 1)
                for a in range(2):
                    sp.wait_ge(side_stored[a], UNITS * 16)

            @block.tensor
            def _(pe):
                def find(h, i, u):
                    until(pe, "act1", h, i, u, 4 if below(h, 1) else 2)
                    for j in range(2):
                        last = nc.tensor.matmul(
                            ps[0:TP, banks1(h, u) + j, 0:500], flat(qx[:, at(h), u * TP:(u + 1) * TP]),
                            flat(kx[:, at(h % 3), bass.ds(i * P1_KEYS + j * 500, 500)]),
                            start=True, stop=True)
                    last.then_inc(s["scored1"], 1)

                def score(h, i, u):
                    if not (isinstance(h, int) and h == H - 1):
                        until(pe, "act2", h, i, u, 1)
                    elif isinstance(i, int) and i == 0 and u == 0:
                        until(pe, "act2", h, i, u, 1)
                    elif isinstance(i, int) and i == 0 and u == 1:
                        until(pe, "act1", h, GROUPS1 - 1, 3)
                    else:
                        until(pe, "act2", h, i, u, 2)
                    for j in range(2):
                        last = nc.tensor.matmul(
                            ps[0:KP, banks2(h, u) + j, 0:TOKENS],
                            flat(kx[:, at(h % 3), bass.ds(i * (8 * KP) + (2 * u + j) * KP, KP)]),
                            flat(qx[:, at(h), :]), start=True, stop=True)
                    last.then_inc(s["scored2"], 1)

                def product(h, i, u):
                    until(pe, "cast", h, i, u + 1)
                    first = isinstance(i, int) and i == 0 and u == 0
                    for g in range(4):
                        last = nc.tensor.matmul(pv[32 * g:32 * g + 32, :], v_now[:, u + g // 2, g % 2, :],
                                                probs[:, u + g // 2, g % 2, :], start=first, stop=True,
                                                skip_group_check=True)
                    last.then_inc(s["pv"], 1)

                def place_maxima(h):
                    pe.wait_ge(s["row"], h * 3 + 3)
                    if not (isinstance(h, int) and h < 2):
                        pe.wait_ge(s["out"], h - 1)
                    for t in range(TT):
                        last = nc.tensor.matmul(row_ps[:, t * TP:(t + 1) * TP], row_parts[:, t, :],
                                                k.ident_b[0:TP, 0:TP], start=True, stop=True)
                    last.then_inc(s["row_ps"], 1)

                def side_piece(item, u):
                    kind, pair, a = item
                    if u == 0:
                        if kind == 0:
                            pe.wait_ge(side_loaded[a], pair * 16 + 16)
                        pe.wait_ge(s["side_out"], pair * 4 + (2 * a + kind + 1))
                    half, c = u // 2, u % 2
                    if kind == 0:
                        last = nc.tensor.matmul(side_ps[:, half * UNIT:(half + 1) * UNIT],
                                                side_w[:, 0, c, half * 128:(half + 1) * 128],
                                                side_rows[:, a, c, :], start=(c == 0), stop=(c == C2 - 1))
                    else:
                        last = nc.tensor.matmul(side_ps[0:KP, half * D:(half + 1) * D],
                                                side_rows[:, a, c, half * KP:(half + 1) * KP],
                                                side_w[:, 1, c, :], start=(c == 0), stop=(c == C2 - 1))
                    if u == 3:
                        last.then_inc(s["side_done"], 1)

                def product_lagged(h, i, u):
                    if u == 3:
                        product(h, i, 0)
                    elif u == 1 and not (isinstance(i, int) and i == 0):
                        product(h, i - 1, 2)

                def fold_groups(h):
                    pe.wait_ge(s["pv_sb"], h + 1)
                    for t in range(TT):
                        last = nc.tensor.matmul(folded[:, t * HD:(t + 1) * HD],
                                                groups_out[:, t * TP:(t + 1) * TP], fold[:], start=True, stop=True)
                    last.then_inc(s["folded"], 1)

                def joint(h, i, item):
                    first = isinstance(i, int) and i == 0
                    if first and not below(h, 1):
                        pe.wait_ge(s["row_sb"], h)
                    for u in range(4):
                        if not below(h, 1):
                            score(h - 1, i, u)
                            if first and u == 1 and not below(h, 2):
                                product(h - 2, GROUPS1 - 1, 2)
                            if first and u == 3 and not below(h, 2):
                                pe.wait_ge(s["pv_sb"], h - 1)
                            product_lagged(h - 1, i, u)
                        if item is not None and u == 1:
                            if item[0] == 0 and item[2] == 0:
                                pe.wait_ge(s["out"], h - 1)
                            side_piece(item, 0)
                        if not (isinstance(h, int) and h == H):
                            find(h, i + 1, u)
                        if first and u == 3 and not below(h, 2):
                            fold_groups(h - 2)
                        if item is not None and u > 0:
                            side_piece(item, u)

                def tail(h):
                    for u in range(4):
                        if not below(h, 1):
                            score(h - 1, GROUPS1 - 1, u)
                            product_lagged(h - 1, GROUPS1 - 1, u)
                        if not (isinstance(h, int) and h == H - 1):
                            begin_head(h + 1, u)
                        if u == 2:
                            place_maxima(h)

                def begin_head(h, u):
                    pe.wait_ge(k.kx_loaded, h * (16 * len(K_PARTS)) + 16 * len(K_PARTS))
                    if isinstance(h, int) and h == 1:
                        pe.wait_ge(s["kx_ones"], 1)
                    find(h, 0, u)

                pe.wait_ge(s["qx"], 16 * len(PARTS))
                pe.wait_ge(s["qx_zero"], 1)
                pe.wait_ge(s["side_w"], 64)
                for u in range(4):
                    begin_head(0, u)
                stages(pe, joint, tail)
                product(H - 1, GROUPS1 - 1, 2)
                fold_groups(H - 1)
                pe.wait_ge(s["ctx"], 1)
                transpose_rows(nc, k, ps[:, 0:2, 0:TOKENS], ctx_rows).then_inc(s["ctxT"], 1)
                pe.wait_ge(s["ctxT_sb"], 1)
                pe.wait_ge(s["w"], 32)
                for t in range(TT):
                    for c in range(C2):
                        last = nc.tensor.matmul(y[:, t, :], ctx_T[:, c, t * TP:(t + 1) * TP], w[:, c, :],
                                                start=(c == 0), stop=(c == C2 - 1))
                last.then_inc(s["y"], 1)
                norm_tensor(nc, pe, k, s, ps[:, 4:6, 0:TOKENS])

            @block.vector
            def _(dve):
                nc.vector.memset(qx[QK_ROWS:, :, :], 0.0).then_inc(s["qx_zero"], 1)
                nc.vector.memset(v_now[:], 0.0).then_inc(s["zero"], 1)
                dve.wait_ge(s["zero"], 1)

                def find(h, i, u):
                    until(dve, "scored1", h, i, u)
                    nc.vector.tensor_reduce(
                        flat(low[:, at(h), bass.ds(i + u * P1_STEPS, 1)]),
                        ps[0:TP, banks1(h, u):banks1(h, u) + 2, 0:500], AX.XY, ALU.min).then_inc(s["low"], 1)

                def cut_maxima(h):
                    n = [0]

                    def link(ins):
                        n[0] += 1
                        ins.then_inc(s["row_link"], 1)
                        dve.wait_ge(s["row_link"], h * 3 + n[0])
                    link(nc.vector.tensor_reduce(row[:, 0, :], low[:, at(h), :].rearrange(
                        "p a (t n) -> p (a t) n", t=TT), AX.X, ALU.min, negate=True))
                    for i in range(3):
                        nc.vector.tensor_copy(row_parts[:, :, i], row[:, i, :]).then_inc(s["row"], 1)
                        if i < 2:
                            dve.wait_ge(s["row"], h * 3 + (i + 1))
                            link(nc.vector.tensor_tensor(row[:, i + 1, :], row[:, i, :], row_parts[:, :, i],
                                                         ALU.subtract))

                def place_maxima(h):
                    dve.wait_ge(s["row_ps"], h + 1)
                    nc.vector.tensor_copy(flat(qx[QK_ROWS:QK_ROWS + 3, at(h), :]), row_ps)\
                        .then_inc(s["row_sb"], 1)

                def cast(h, i, u):
                    until(dve, "act2", h, i, u)
                    if u % 2 == 0 and not (isinstance(h, int) and h == 0 and isinstance(i, int) and i == 0):
                        dve.wait_ge(s["pv"], h * (HEAD_STEPS // 2) + (i * 2 + (u // 2 - 1)))
                    nc.vector.tensor_copy(v_now[:, u, :, 0:HD],
                                          k.v_steps[:, bass.ds(i * 8 + 2 * u, 2), bass.ds(h * HD, HD)])
                    nc.vector.tensor_copy(probs[:, u], steps[:, u]).then_inc(s["cast"], 1)

                def take_groups(h):
                    dve.wait_ge(s["pv"], (h + 1) * (HEAD_STEPS // 2))
                    if not (isinstance(h, int) and h == 0):
                        dve.wait_ge(s["folded"], h)
                    nc.vector.tensor_copy(groups_out[:], pv).then_inc(s["pv_sb"], 1)

                def take_out(h):
                    dve.wait_ge(s["folded"], h + 1)
                    nc.vector.tensor_copy(out[:, at(h)].rearrange("p a t e -> p (a t e)"), folded)\
                        .then_inc(s["out"], 1)

                def take_side(item):
                    kind, pair, a = item
                    dve.wait_ge(s["side_done"], pair * 4 + (2 * a + kind + 1))
                    if kind == 0:
                        for c in range(C2):
                            last = nc.vector.tensor_scalar(side_k[:, a, c, :], side_ps[:, c * UNIT:(c + 1) * UNIT],
                                                           side_bk[:, c:c + 1], None, ALU.add)
                    else:
                        last = nc.vector.tensor_tensor(
                            side_v[:, a, :, :, 0:HD],
                            side_ps[0:KP, :].rearrange("p (t h e) -> p t h e", t=2, e=HD),
                            bcast(side_bv[:].rearrange("p (h e) -> p h e", e=HD).unsqueeze(1),
                                  [KP, 2, H, HD]), ALU.add)
                    last.then_inc(s["side_out"], 1)

                def joint(h, i, item):
                    first = isinstance(i, int) and i == 0
                    for u in range(4):
                        if not (isinstance(h, int) and h == H):
                            find(h, i + 1, u)
                        if not below(h, 1):
                            cast(h - 1, i, u)
                        if first and u == 1 and not below(h, 2):
                            take_groups(h - 2)
                    if first and not below(h, 2):
                        take_out(h - 2)
                    if item is not None:
                        take_side(item)

                def tail(h):
                    until(dve, "low", h, GROUPS1 - 1, 3)
                    for u in range(4):
                        if not (isinstance(h, int) and h == H - 1):
                            find(h + 1, 0, u)
                        if u == 3:
                            place_maxima(h)
                        if not below(h, 1):
                            cast(h - 1, GROUPS1 - 1, u)
                        if u == 0:
                            cut_maxima(h)

                dve.wait_ge(s["w"], 32)
                nc.vector.tensor_tensor(k.res[:], k.x_tok[:], bcast(bias[:].unsqueeze(1), [TP, TT, D]),
                                        ALU.add)
                dve.wait_ge(s["side_w"], 64)
                nc.vector.memset(side_v[:], 1.0).then_inc(s["side_out"], 1)
                dve.wait_ge(s["side_out"], 1)
                for u in range(4):
                    find(0, 0, u)
                stages(dve, joint, tail)
                take_groups(H - 1)
                take_out(H - 1)
                link = linker(dve, s["tail"])
                link(nc.vector.tensor_reduce(head_low[:].rearrange("p h t -> p (h t)"), low[:].rearrange(
                    "p h (t n) -> p (h t) n", t=TT), AX.X, ALU.min))
                lows = low[:].rearrange("p h (t n) -> p (h t) n", t=TT)
                nc.vector.tensor_tensor(lows, bcast(head_low[:].rearrange("p h t -> p (h t)").unsqueeze(2),
                                                    [TP, H * TT, P1_STEPS]), lows, ALU.subtract)\
                    .then_inc(s["diff"], 1)
                dve.wait_ge(s["weight"], 1)
                link(nc.vector.tensor_tensor(sums[:], sums[:], low[:], ALU.mult))
                link(nc.vector.tensor_reduce(head_low[:].rearrange("p h t -> p (h t)"), sums[:].rearrange(
                    "p h (t n) -> p (h t) n", t=TT), AX.X, ALU.add))
                link(nc.vector.reciprocal(inv[:], head_low[:]))
                link(nc.vector.tensor_scalar(inv[:], inv[:], 1.0 / 255.0, None, ALU.mult))
                link(nc.vector.tensor_tensor(out[:], out[:], bcast(inv[:].unsqueeze(3), [TP, H, TT, HD]),
                                             ALU.mult))
                nc.vector.tensor_tensor(
                    ctx_rows[:].rearrange("p t (h e) -> p h t e", h=H), out[:],
                    bcast(k.v_scale[0:TP, :].rearrange("p (h e) -> p h e", h=H).unsqueeze(2), [TP, H, TT, HD]),
                    ALU.mult).then_inc(s["ctx"], 1)
                dve.wait_ge(s["y"], 1)
                norm_vector(nc, dve, link, k, s, y)

            @block.scalar
            def _(act):
                def find(h, i, u):
                    until(act, "low", h, i, u)
                    block_at = bass.ds(i + u * P1_STEPS, 1)
                    banks = ps[0:TP, banks1(h, u):banks1(h, u) + 2, 0:500]
                    nc.scalar.activation(banks, banks, ACT.Exp, scale=-1.0, bias=flat(low[:, at(h), block_at]),
                                         accum_out=flat(sums[:, at(h), block_at])).then_inc(s["act1"], 1)

                def take_steps(h, i, u):
                    until(act, "scored2", h, i, u)
                    until(act, "cast", h, i, u, 4)
                    nc.scalar.activation(steps[:, u], ps[0:KP, banks2(h, u):banks2(h, u) + 2, 0:TOKENS], ACT.Exp, scale=-1.0, bias=LN255)\
                        .then_inc(s["act2"], 1)

                def joint(h, i, item):
                    for u in range(4):
                        if not below(h, 1):
                            take_steps(h - 1, i, u)
                        if not (isinstance(h, int) and h == H):
                            find(h, i if u == 0 else i + 1, (u + 3) % 4)

                def tail(h):
                    for u in range(4):
                        if not below(h, 1):
                            take_steps(h - 1, GROUPS1 - 1, u)
                        if u == 0:
                            find(h, GROUPS1 - 1, 3)
                        elif not (isinstance(h, int) and h == H - 1):
                            find(h + 1, 0, u - 1)

                for u in range(3):
                    find(0, 0, u)
                stages(act, joint, tail)
                act.wait_ge(s["diff"], 1)
                nc.scalar.activation(low[:], low[:], ACT.Exp).then_inc(s["weight"], 1)
                act.wait_ge(s["ctxT"], 1)
                nc.scalar.activation(ctx_T[:], ps[:, 0:2, 0:TOKENS], ACT.Copy).then_inc(s["ctxT_sb"], 1)
                norm_scalar(nc, act, k, s, ps[:, 4:6, 0:TOKENS])


def route_shift(nc, link, k, logits, shifted):
    r = k.route
    link(nc.vector.tensor_reduce(r[:, :, 24], logits, AX.X, ALU.max, negate=True))
    nc.vector.tensor_tensor(r[:, :, 0:8], logits, bcast(r[:, :, 24:25], [TP, TT, E]), ALU.add)\
        .then_inc(shifted, 1)


def route_choose(nc, link, k, gates, normalise, chosen):
    r = k.route
    link(nc.vector.tensor_reduce(r[:, :, 25], r[:, :, 8:16], AX.X, ALU.add))
    link(nc.vector.reciprocal(r[:, :, 26], r[:, :, 25]))
    link(nc.vector.tensor_tensor(r[:, :, 0:8], r[:, :, 8:16], bcast(r[:, :, 26:27], [TP, TT, E]), ALU.mult))
    for t in range(TT):
        last = nc.vector.max(r[:, t, 16:24], r[:, t, 0:8])
    link(last)
    for t in range(TT):
        last = nc.vector.max_index(k.route_at[:, t, :], r[:, t, 16:24], r[:, t, 0:8])
    link(last)
    link(nc.vector.tensor_copy(k.route_idx[:], k.route_at[:]))
    if normalise:
        link(nc.vector.tensor_tensor(r[:, :, 27], r[:, :, 16], r[:, :, 17], ALU.add))
        link(nc.vector.reciprocal(r[:, :, 28], r[:, :, 27]))
        link(nc.vector.tensor_tensor(r[:, :, 16:18], r[:, :, 16:18], bcast(r[:, :, 28:29], [TP, TT, 2]),
                                     ALU.mult))
    for i in range(2):
        to = (r[:, :, 8:16], gates)[i]
        link(nc.vector.tensor_tensor(r[:, :, 29:37], bcast(k.expert[:].unsqueeze(1), [TP, TT, E]),
                                     bcast(k.route_idx[:, :, i:i + 1], [TP, TT, E]), ALU.is_equal))
        link(nc.vector.tensor_tensor(to, r[:, :, 29:37], bcast(r[:, :, 16 + i:17 + i], [TP, TT, E]), ALU.mult))
    nc.vector.tensor_tensor(gates, gates, r[:, :, 8:16], ALU.add).then_inc(chosen, 1)


def layer0_mlp(nc, k, d):
    with ExitStack() as ctx:
        sb = lambda n, sh, dt=F32: ctx.enter_context(nc.sbuf_tensor(n, sh, dt))
        w = sb("f0_w", [128, 3, C2, D])
        wr = sb("f0_wr", [128, C2, E])
        h1 = sb("f0_h1", [128, C2, TOKENS])
        h2 = sb("f0_h2", [TP, TT, D])
        gates = sb("f0_gates", [TP, TT, E])
        mixed = sb("f0_mixed", [128, C2, E])
        y_sb = sb("f0_y", [TP, TT, D])
        ps = ctx.enter_context(nc.psum_tensor("f0_ps", [128, 8, 512], F32))
        s = k.sems("f0", "w layer1 logits shifted exp gates h1 h1_sb h2 h2_sb mixed mixed_sb y link zero iota " + NORM_SEMS)
        logits = ps[0:TP, 0, 0:TT * E].rearrange("p (t e) -> p t e", e=E)
        h2_ps = ps[0:TP, 3:5, :].rearrange("p b (t n) -> p (b t) n", n=D)
        with nc.Block() as block:

            @block.sync
            def _(sp):
                for i, n in enumerate(("f0_w1", "f0_w3", "f0_w2")):
                    sp.dma_start(w[:, i], d[n].rearrange("(c p) n -> p c n", p=128)).then_inc(s["w"], 16)
                sp.dma_start(wr[:], d["f0_wr"].rearrange("(c p) n -> p c n", p=128)).then_inc(s["w"], 16)
                loads = load_attention(sp, k, d, s["layer1"])
                sp.wait_ge(s["layer1"], 16 * loads)

            @block.gpsimd
            def _(pool):
                nc.gpsimd.iota(k.expert_i[:], pattern=[[1, E]], base=0, channel_multiplier=0)\
                    .then_inc(s["iota"], 1)
                pool.wait_ge(s["iota"], 1)
                nc.gpsimd.tensor_copy(k.expert[:], k.expert_i[:]).then_inc(s["iota"], 1)

            @block.tensor
            def _(pe):
                pe.wait_ge(s["w"], 64)
                for t in range(TT):
                    for c in range(C2):
                        last = nc.tensor.matmul(logits[:, t, :], k.x_T[:, c, t * TP:(t + 1) * TP], wr[:, c, :],
                                                start=(c == 0), stop=(c == C2 - 1))
                last.then_inc(s["logits"], 1)
                for o in range(C2):
                    for c in range(C2):
                        last = nc.tensor.matmul(ps[:, 1 + o, 0:TOKENS], w[:, 0, c, o * 128:(o + 1) * 128],
                                                k.x_T[:, c, :], start=(c == 0), stop=(c == C2 - 1))
                last.then_inc(s["h1"], 1)
                pe.wait_ge(s["h1_sb"], 1)
                for t in range(TT):
                    for c in range(C2):
                        last = nc.tensor.matmul(h2_ps[:, t, :], h1[:, c, t * TP:(t + 1) * TP], w[:, 1, c, :],
                                                start=(c == 0), stop=(c == C2 - 1))
                last.then_inc(s["h2"], 1)
                pe.wait_ge(s["h2_sb"], 1)
                pe.wait_ge(s["gates"], 1)
                for c in range(C2):
                    for t in range(TT):
                        last = nc.tensor.matmul(ps[:, 5, c * E:(c + 1) * E], h2[:, t, c * 128:(c + 1) * 128],
                                                gates[:, t, :], start=(t == 0), stop=(t == TT - 1))
                last.then_inc(s["mixed"], 1)
                pe.wait_ge(s["mixed_sb"], 1)
                for c in range(C2):
                    last = nc.tensor.matmul(ps[0:E, 6, 0:D], mixed[:, c, :], w[:, 2, c, :],
                                            start=(c == 0), stop=(c == C2 - 1))
                last.then_inc(s["y"], 1)
                norm_tensor(nc, pe, k, s, ps[:, 1:3, 0:TOKENS])

            @block.scalar
            def _(act):
                act.wait_ge(s["shifted"], 1)
                nc.scalar.activation(k.route[:, :, 8:16], k.route[:, :, 0:8], ACT.Exp).then_inc(s["exp"], 1)
                act.wait_ge(s["h1"], 1)
                nc.scalar.activation(h1[:], ps[:, 1:3, 0:TOKENS], ACT.Silu).then_inc(s["h1_sb"], 1)
                act.wait_ge(s["h2"], 1)
                nc.scalar.activation(h2[:], h2_ps, ACT.Silu).then_inc(s["h2_sb"], 1)
                norm_scalar(nc, act, k, s, ps[:, 1:3, 0:TOKENS])

            @block.vector
            def _(dve):
                link = linker(dve, s["link"])
                link(nc.vector.memset(y_sb[:], 0.0))
                link(nc.vector.tensor_copy(k.res[:], k.x_tok[:]))
                dve.wait_ge(s["logits"], 1)
                dve.wait_ge(s["iota"], 2)
                route_shift(nc, link, k, logits, s["shifted"])
                dve.wait_ge(s["exp"], 1)
                route_choose(nc, link, k, gates[:], True, s["gates"])
                dve.wait_ge(s["mixed"], 1)
                nc.vector.tensor_copy(mixed[:], ps[:, 5, 0:C2 * E].rearrange("p (c e) -> p c e", e=E))\
                    .then_inc(s["mixed_sb"], 1)
                dve.wait_ge(s["y"], 1)
                link(nc.vector.tensor_copy(y_sb[0:E, 0, :], ps[0:E, 6, 0:D]))
                norm_vector(nc, dve, link, k, s, y_sb[:])


def layer1_attention(nc, k, d):
    k.phase = "a1"
    with ExitStack() as ctx:
        sb = lambda n, sh, dt=F32: ctx.enter_context(nc.sbuf_tensor(n, sh, dt))
        w, wo, bqk, bv, bo = k.a1_weights
        q_T = sb("a1_qT", [128, C2, TOKENS])
        k_T = sb("a1_kT", [128, C2, TOKENS])
        q_heads = sb("a1_qheads", [128, C2, 8, TOKENS])
        v = sb("a1_v", [TP, TT, D])
        term = sb("a1_term", [TP, H, TP])
        place_i = sb("a1_placei", [TP, TP], I32)
        place = sb("a1_place", [TP, TP])
        o_rows = sb("a1_o", [TP, TT, D])
        o_T = sb("a1_oT", [128, C2, TOKENS])
        attention_buffers(nc, ctx, k)
        ps = ctx.enter_context(nc.psum_tensor("a1_ps", [128, 8, 512], F32))
        s = k.sems("a1", "qk q_sb k_sb v v_sb q_heads const mask head_mask term o_all oT oT_sb y link "
                   + ATT_SEMS + " " + NORM_SEMS)
        y = ps[0:TP, 6:8, :].rearrange("p b (t n) -> p (b t) n", n=D)
        v_ps = ps[0:TP, 4:6, :].rearrange("p b (t n) -> p (b t) n", n=D)
        sc, pt, o = [ps[:, i, :] for i in (0, 1)], [ps[:, i, :] for i in (2, 3)], [ps[:, i, :] for i in (4, 5)]
        slopes = [(2.0 ** (-2.0 ** -(np.log2(H) - 3))) ** (i + 1) for i in range(H)]
        with nc.Block() as block:

            @block.gpsimd
            def _(pool):
                nc.gpsimd.memset(k.head_mask[:], 1.0).then_inc(s["const"], 1)
                nc.gpsimd.iota(place_i[:].rearrange("p (b t) -> p b t", b=2), pattern=[[0, 2], [1, T]], base=0,
                               channel_multiplier=0).then_inc(s["const"], 1)
                pool.wait_ge(s["const"], 2)
                nc.gpsimd.affine_select(out=k.head_mask[:], in_=k.head_mask[:], compare_op=ALU.is_ge, fill=0.0,
                                        base=0, pattern=[[-HD, 8]], channel_multiplier=1).then_inc(s["const"], 1)
                nc.gpsimd.tensor_copy(place[:], place_i[:]).then_inc(s["mask"], 1)
                pool.wait_ge(s["const"], 3)
                nc.gpsimd.affine_select(out=k.head_mask[:], in_=k.head_mask[:], compare_op=ALU.is_ge, fill=0.0,
                                        base=HD - 1, pattern=[[HD, 8]], channel_multiplier=-1)\
                    .then_inc(s["head_mask"], 1)
                pool.wait_ge(s["mask"], 1)
                for h in range(H):
                    nc.gpsimd.tensor_scalar(term[:, h, :], place[:], float(-(T - 1)), float(np.float32(slopes[h])),
                                            ALU.add, ALU.mult).then_inc(s["const"], 1)
                pool.wait_ge(s["const"], 3 + H)
                nc.gpsimd.affine_select(out=term[:], in_=term[:], compare_op=ALU.is_ge, fill=MASKED, base=0,
                                        pattern=[[0, H], [-1, TP]], channel_multiplier=1).then_inc(s["const"], 1)
                pool.wait_ge(s["const"], 4 + H)
                nc.gpsimd.affine_select(out=term[:, :, 0:T], in_=term[:, :, 0:T], compare_op=ALU.is_ge,
                                        fill=MASKED, base=T - 1, pattern=[[0, H], [0, T]], channel_multiplier=-1)\
                    .then_inc(s["term"], 1)

            @block.tensor
            def _(pe):
                for n in range(2):
                    for o_ in range(C2):
                        for c in range(C2):
                            last = nc.tensor.matmul(ps[:, 2 * n + o_, 0:TOKENS],
                                                    w[:, n, c, o_ * 128:(o_ + 1) * 128], k.x_T[:, c, :],
                                                    start=(c == 0), stop=(c == C2 - 1))
                    last.then_inc(s["qk"], 1)
                for t in range(TT):
                    for c in range(C2):
                        last = nc.tensor.matmul(v_ps[:, t, :], k.x_T[:, c, t * TP:(t + 1) * TP], w[:, 2, c, :],
                                                start=(c == 0), stop=(c == C2 - 1))
                last.then_inc(s["v"], 1)
                pe.wait_ge(s["q_heads"], C2)
                pe.wait_ge(s["k_sb"], C2)
                pe.wait_ge(s["v_sb"], 1)

                def score_operands(p, h):
                    return (q_heads[:, h // 8, h % 8, p * TP:(p + 1) * TP],
                            k_T[:, h // 8, p * TP:(p + 1) * TP])

                def value_product(out, p, h, j, probs):
                    return nc.tensor.matmul(out[0:TP, j * HD:(j + 1) * HD], probs, v[:, p, h * HD:(h + 1) * HD],
                                            start=True, stop=True)

                attention_tensor(nc, pe, k, s, score_operands, value_product, sc, pt, o)
                pe.wait_ge(s["o_sbuf"], GROUPS)
                transpose_rows(nc, k, ps[:, 0:2, 0:TOKENS], o_rows).then_inc(s["oT"], 1)
                pe.wait_ge(s["oT_sb"], 1)
                for t in range(TT):
                    for c in range(C2):
                        last = nc.tensor.matmul(y[:, t, :], o_T[:, c, t * TP:(t + 1) * TP], wo[:, c, :],
                                                start=(c == 0), stop=(c == C2 - 1))
                last.then_inc(s["y"], 1)
                norm_tensor(nc, pe, k, s, ps[:, 2:4, 0:TOKENS])

            @block.scalar
            def _(act):
                act.wait_ge(s["qk"], 1)
                for c in range(C2):
                    nc.scalar.activation(q_T[:, c, :], ps[:, c, 0:TOKENS], ACT.Identity,
                                         bias=bqk[:, 0, c:c + 1]).then_inc(s["q_sb"], 1)

                act.wait_ge(s["q_sb"], C2)
                act.wait_ge(s["head_mask"], 1)
                mask_heads(nc, k, q_heads, q_T).then_inc(s["q_heads"], 1)

                def place_output(g, bank):
                    h = 4 * (g % 4)
                    return nc.scalar.activation(o_rows[:, g // 4, h * HD:(h + 4) * HD], bank[0:TP, 0:4 * HD],
                                                ACT.Copy)

                attention_scalar(nc, act, k, s, pt, o, place_output)
                act.wait_ge(s["oT"], 1)
                nc.scalar.activation(o_T[:], ps[:, 0:2, 0:TOKENS], ACT.Copy).then_inc(s["oT_sb"], 1)
                norm_scalar(nc, act, k, s, ps[:, 2:4, 0:TOKENS])

            @block.vector
            def _(dve):
                link = linker(dve, s["link"])
                nc.vector.tensor_tensor(k.res[:], k.x_tok[:], bcast(bo[:].unsqueeze(1), [TP, TT, D]), ALU.add)
                dve.wait_ge(s["qk"], 2)
                for c in range(C2):
                    nc.vector.tensor_scalar(k_T[:, c, :], ps[:, 2 + c, 0:TOKENS], bqk[:, 1, c:c + 1], None,
                                            ALU.add).then_inc(s["k_sb"], 1)
                dve.wait_ge(s["v"], 1)
                nc.vector.tensor_tensor(v[:], v_ps, bcast(bv[:].unsqueeze(1), [TP, TT, D]), ALU.add)\
                    .then_inc(s["v_sb"], 1)
                dve.wait_ge(s["q_sb"], C2)
                dve.wait_ge(s["head_mask"], 1)
                nc.vector.tensor_tensor(q_heads[:, 0], bcast(q_T[:, 0:1, :], [128, 8, TOKENS]),
                                        bcast(k.head_mask[:].unsqueeze(2), [128, 8, TOKENS]), ALU.mult)\
                    .then_inc(s["q_heads"], 1)
                dve.wait_ge(s["term"], 1)

                def add_term(g, out, scores):
                    h = 4 * (g % 4)
                    return nc.vector.scalar_tensor_tensor(
                        out, scores[0:TP, 0:4 * TP].rearrange("p (j t) -> p j t", j=4), 1.0 / np.sqrt(HD),
                        term[:, h:h + 4, :], ALU.mult, ALU.add)

                attention_vector(nc, dve, k, s, add_term, sc)
                dve.wait_ge(s["y"], 1)
                norm_vector(nc, dve, link, k, s, y)


def mask_heads(nc, k, q_heads, q_T):
    for h in range(8):
        last = nc.scalar.activation(q_heads[:, 1, h, :], q_T[:, 1, :], ACT.Copy, scale=k.head_mask[:, h:h + 1])
    return last


def layer1_cross_attention(nc, k, d):
    with ExitStack() as ctx:
        sb = lambda n, sh, dt=F32: ctx.enter_context(nc.sbuf_tensor(n, sh, dt))
        TILES = S // KP
        w, bqk, rows_of, rs, mask_i = k.c1_weights
        q_T = sb("c1_qT", [128, C2, TOKENS])
        q_heads = sb("c1_qheads", [128, C2, 8, TOKENS])
        k_T = sb("c1_kT", [128, 2, C2, S])
        v = sb("c1_v", [KP, 2, TILES, H, HD + 1])
        clipped = sb("c1_clipped", [KP, 2, H * T])
        probs = sb("c1_probs", [KP, 2, H * T])
        attend = sb("c1_attend", [KP, 2, KT])
        acc_sb = sb("c1_acc", [128, 4 * T])
        sums = sb("c1_sums", [T, 4, H])
        out = sb("c1_out", [T, 2, D])
        ctx_T = sb("c1_ctxT", [128, C2, TOKENS])
        delta = sb("c1_delta", [TP, TT, D])
        ps = ctx.enter_context(nc.psum_tensor("c1_ps", [128, 8, 512], F32))
        s = k.sems("c1", "experts l0 l1 q q_sb q_heads zero attend scored "
                   "clip exp pv link acc_sb turned rows merged ctx_out y rs var2 std2 " + NORM_SEMS)
        loaded = [s["l0"], s["l1"]]
        y = ps[0:TP, 0:2, :].rearrange("p b (t n) -> p (b t) n", n=D)

        def sequences(engine, tile, later=()):
            def sequence(b, parity):
                for i in range(TILES):
                    tile(b, parity, i)
                    for after, work in later:
                        if i == after and not (isinstance(b, int) and b == 0):
                            work(b - 1, 1 - parity)
            sequence(0, 0)
            sequence(1, 1)
            with engine.Fori(1, B // 2) as r:
                sequence(2 * r, 0)
                sequence(2 * r + 1, 1)
            for _, work in later:
                work(B - 1, 1)

        def since(engine, sem, n, lag):
            if isinstance(n, int) and n < lag:
                return
            engine.wait_ge(sem, n + (1 - lag))

        def acc(parity):
            return ps[:, 6 + parity, 0:4 * T]

        def turned(parity):
            return ps[0:T, parity, :].rearrange("p (h e) -> p h e", e=32)

        with nc.Block() as block:

            @block.sync
            def _(sp):
                def load(b, parity):
                    if not (isinstance(b, int) and b < 2):
                        sp.wait_ge(s["pv"], b * TILES - TILES)
                    sp.dma_start(k_T[:, parity], k.k1_T.rearrange("(c p) n -> p c n", p=128)[
                        :, :, bass.ds(b * S, S)]).then_inc(loaded[parity], 16)
                    sp.dma_start(v[:, parity].rearrange("p t h e -> p t (h e)"), k.v1.rearrange(
                        "(t p) n -> p t n", p=KP)[:, bass.ds(b * TILES, TILES), :]).then_inc(loaded[parity], 16)
                load(0, 0)
                load(1, 1)
                load_experts(sp, k, d, s["experts"])
                with sp.Fori(1, B // 2) as r:
                    load(2 * r, 0)
                    load(2 * r + 1, 1)
                sp.wait_ge(s["experts"], 16 * EXPERT_LOADS)

            @block.tensor
            def _(pe):
                for o in range(C2):
                    for c in range(C2):
                        last = nc.tensor.matmul(ps[:, 2 + o, 0:TOKENS], w[:, 0, c, o * 128:(o + 1) * 128],
                                                k.x_T[:, c, :], start=(c == 0), stop=(c == C2 - 1))
                last.then_inc(s["q"], 1)
                pe.wait_ge(s["zero"], 1)

                def product(b, parity, i):
                    n = b * TILES + i
                    since(pe, s["exp"], n, 0)
                    if i == 0:
                        since(pe, s["acc_sb"], b, 2)
                    for n in range(4):
                        for g in range(4):
                            h = 4 * n + g
                            last = nc.tensor.matmul(acc(parity)[32 * g:32 * g + HD + 1, n * T:(n + 1) * T],
                                                    v[:, parity, i, h, :], probs[:, i % 2, h * T:(h + 1) * T],
                                                    start=(i == 0 and n == 0), stop=True, skip_group_check=True)
                    last.then_inc(s["pv"], 1)

                def tile(b, parity, i):
                    n = b * TILES + i
                    if i == 0:
                        pe.wait_ge(loaded[parity], 32 + (b - parity) * 16)
                        if isinstance(b, int) and b == 0:
                            pe.wait_ge(s["q_heads"], C2)
                    since(pe, s["clip"], n, 2)
                    for c in range(C2):
                        last = nc.tensor.matmul(
                            ps[0:KP, 2 + 2 * (i % 2) + c, 0:TOKENS].rearrange("p (h t) -> p h t", h=8),
                            k_T[:, parity, c, i * KP:(i + 1) * KP], q_heads[:, c, :, bass.ds(b * T, T)],
                            start=True, stop=True)
                    last.then_inc(s["scored"], 1)
                    if i >= 1:
                        product(b, parity, i - 1)
                    if i == TILES - 1:
                        product(b, parity, i)

                def turn(b, parity):
                    pe.wait_ge(s["acc_sb"], b + 1)
                    since(pe, s["ctx_out"], b, 2)
                    for n in range(4):
                        last = nc.tensor.matmul(ps[0:T, parity, n * 128:(n + 1) * 128],
                                                acc_sb[:, n * T:(n + 1) * T], k.ident[:], start=True, stop=True)
                    last.then_inc(s["turned"], 1)

                def merge(b, parity):
                    pe.wait_ge(s["rows"], b + 1)
                    for c in range(C2):
                        last = nc.tensor.matmul(ps[:, parity, c * T:(c + 1) * T],
                                                out[:, parity, c * 128:(c + 1) * 128], k.ident[0:T, 0:T],
                                                start=True, stop=True)
                    last.then_inc(s["merged"], 1)

                sequences(pe, tile, ((1, turn), (5, merge)))
                pe.wait_ge(s["ctx_out"], B)
                for t in range(TT):
                    for c in range(C2):
                        last = nc.tensor.matmul(y[:, t, :], ctx_T[:, c, t * TP:(t + 1) * TP], w[:, 1, c, :],
                                                start=(c == 0), stop=(c == C2 - 1))
                last.then_inc(s["y"], 1)
                norm_tensor(nc, pe, k, s, ps[:, 2:4, 0:TOKENS])

            @block.scalar
            def _(act):
                act.wait_ge(s["q"], 1)
                act.wait_ge(s["rs"], 1)
                for c in range(C2):
                    nc.scalar.activation(q_T[:, c, :], ps[:, 2 + c, 0:TOKENS], ACT.Identity, scale=0.25,
                                         bias=bqk[:, 0, c:c + 1]).then_inc(s["q_sb"], 1)
                act.wait_ge(s["q_sb"], C2)
                mask_heads(nc, k, q_heads, q_T).then_inc(s["q_heads"], 1)
                act.wait_ge(s["attend"], 2)

                def tile(b, parity, i):
                    n = b * TILES + i
                    since(act, s["clip"], n, 0)
                    since(act, s["pv"], n, 2)
                    at = bass.ds(n, 1)
                    nc.scalar.activation(probs[:, i % 2], clipped[:, i % 2], ACT.Exp,
                                         scale=attend[:, 0, at], bias=attend[:, 1, at]).then_inc(s["exp"], 1)

                def merge(b, parity):
                    act.wait_ge(s["merged"], b + 1)
                    nc.scalar.activation(ctx_T[:, :, bass.ds(b * T, T)],
                                         ps[:, parity, 0:C2 * T].rearrange("p (c t) -> p c t", c=C2),
                                         ACT.Copy).then_inc(s["ctx_out"], 1)

                sequences(act, tile, ((6, merge),))
                act.wait_ge(s["var2"], 1)
                nc.scalar.activation(k.std[:], k.mv[:, :, 1], ACT.Sqrt, bias=EPS).then_inc(s["std2"], 1)
                norm_scalar(nc, act, k, s, ps[:, 2:4, 0:TOKENS])

            @block.vector
            def _(dve):
                nc.vector.memset(ps[:, 6:8, :], 0.0).then_inc(s["zero"], 1)
                nc.vector.tensor_scalar(bqk[:, 0, :], bqk[:, 0, :], 0.25, None, ALU.mult).then_inc(s["rs"], 1)
                nc.vector.tensor_scalar(rs[:], rs[:], 0.0, 0.3, ALU.max, ALU.min).then_inc(s["rs"], 1)
                nc.vector.tensor_scalar(attend[:, 0, :], mask_i[:], 0.5, None, ALU.is_gt).then_inc(s["attend"], 1)
                dve.wait_ge(s["attend"], 1)
                nc.vector.tensor_scalar(attend[:, 1, :], attend[:, 0, :], 50.0, -50.0, ALU.mult, ALU.add)\
                    .then_inc(s["attend"], 1)
                dve.wait_ge(s["q_sb"], C2)
                nc.vector.tensor_tensor(q_heads[:, 0], bcast(q_T[:, 0:1, :], [128, 8, TOKENS]),
                                        bcast(k.head_mask[:].unsqueeze(2), [128, 8, TOKENS]), ALU.mult)\
                    .then_inc(s["q_heads"], 1)

                def tile(b, parity, i):
                    n = b * TILES + i
                    since(dve, s["scored"], n, 0)
                    since(dve, s["exp"], n, 2)
                    nc.vector.tensor_scalar(clipped[:, i % 2].rearrange("p (c n) -> p c n", c=C2),
                                            ps[0:KP, 2 + 2 * (i % 2):4 + 2 * (i % 2), 0:TOKENS], -50.0, 50.0,
                                            ALU.max, ALU.min).then_inc(s["clip"], 1)
                    if i == TILES - 1:
                        dve.wait_ge(s["pv"], b * TILES + TILES)
                        since(dve, s["turned"], b, 1)
                        nc.vector.tensor_copy(acc_sb[:], acc(parity)).then_inc(s["acc_sb"], 1)

                def normalise(b, parity):
                    dve.wait_ge(s["turned"], b + 1)
                    n = [0]

                    def link(ins):
                        n[0] += 1
                        ins.then_inc(s["link"], 1)
                        dve.wait_ge(s["link"], b * 5 + n[0])
                    total = turned(parity)[:, :, HD]
                    link(nc.vector.reciprocal(sums[:, 0, :], total))
                    link(nc.vector.tensor_tensor(sums[:, 1, :], sums[:, 0, :], total, ALU.mult))
                    link(nc.vector.tensor_scalar(sums[:, 2, :], sums[:, 1, :], 1e-8, None, ALU.add))
                    link(nc.vector.reciprocal(sums[:, 3, :], sums[:, 2, :]))
                    link(nc.vector.tensor_tensor(sums[:, 1, :], sums[:, 0, :], sums[:, 3, :], ALU.mult))
                    since(dve, s["merged"], b, 2)
                    nc.vector.tensor_tensor(
                        out[:, parity].rearrange("p (h e) -> p h e", e=HD), turned(parity)[:, :, 0:HD],
                        bcast(sums[:, 1, :].unsqueeze(2), [T, H, HD]), ALU.mult).then_inc(s["rows"], 1)

                sequences(dve, tile, ((2, normalise),))
                dve.wait_ge(s["y"], 1)
                n0 = B * 5
                n = [n0]

                def link(ins):
                    n[0] += 1
                    ins.then_inc(s["link"], 1)
                    dve.wait_ge(s["link"], n[0])

                row = lambda name: bcast(rows_of[name][0:TP, :].unsqueeze(1), [TP, TT, D])
                link(nc.vector.tensor_tensor(delta[:], y, row("bo"), ALU.add))
                link(nc.vector.tensor_scalar(delta[:], delta[:], rs[:, 0:1], None, ALU.mult))
                for t in range(TT):
                    last = nc.vector.bn_stats(k.stats[:, t, :], delta[:, t, :])
                link(last)
                for t in range(TT):
                    last = nc.vector.bn_aggr(k.mv[:, t, :], k.stats[:, t, :])
                last.then_inc(s["var2"], 1)
                dve.wait_ge(s["std2"], 1)
                link(nc.vector.reciprocal(k.rstd[:], k.std[:]))
                for t in range(TT):
                    last = nc.vector.tensor_scalar(delta[:, t, :], delta[:, t, :], k.mv[:, t, 0:1],
                                                   k.rstd[:, t:t + 1], ALU.subtract, ALU.mult)
                link(last)
                link(nc.vector.tensor_tensor(delta[:], delta[:], row("gamma"), ALU.mult))
                link(nc.vector.tensor_tensor(delta[:], delta[:], row("beta"), ALU.add))
                link(nc.vector.tensor_copy(k.res[:], k.x_tok[:]))
                norm_vector(nc, dve, link, k, s, delta[:])


EC = E * F // 128
SC = -(-FS // 128)


def size(n):
    return min(128, FS - (n - EC) * 128) if n >= EC else 128


def attention_weights(nc, cross, own, k):
    sb = lambda ctx, n, sh, dt=F32: ctx.enter_context(nc.sbuf_tensor(n, sh, dt))
    k.c1_weights = (sb(cross, "c1_w", [128, 2, C2, D]), sb(cross, "c1_bqk", [128, 2, C2]),
                    {n: sb(cross, f"c1_{n}", [KP, D]) for n in ("bo", "gamma", "beta")},
                    sb(cross, "c1_rs", [TP, 1]), sb(cross, "c1_maski", [KP, KT], I32))
    k.a1_weights = (sb(own, "a1_w", [128, 3, C2, D]), sb(own, "a1_wo", [128, C2, D]),
                    sb(own, "a1_bqk", [128, 2, C2]), sb(own, "a1_bv", [TP, D]), sb(own, "a1_bo", [TP, D]))


def load_attention(sp, k, d, loaded):
    w, wo, bqk, bv, bo = k.a1_weights
    for i in range(3):
        sp.dma_start(w[:, i], d["a1_Wqkv"][i].rearrange("(c p) n -> p c n", p=128)).then_inc(loaded, 16)
    sp.dma_start(wo[:], d["a1_Wo"].rearrange("(c p) n -> p c n", p=128)).then_inc(loaded, 16)
    sp.dma_start(bqk[:], d["a1_bqk"]).then_inc(loaded, 16)
    sp.dma_start(bv[:], d["a1_bv"].partition_broadcast(TP)).then_inc(loaded, 16)
    sp.dma_start(bo[:], d["a1_bo"].partition_broadcast(TP)).then_inc(loaded, 16)
    w, bqk, rows_of, rs, mask_i = k.c1_weights
    for i in range(2):
        sp.dma_start(w[:, i], d["c1_W"][3 * i].rearrange("(c p) n -> p c n", p=128)).then_inc(loaded, 16)
    sp.dma_start(bqk[:], d["c1_bqk"]).then_inc(loaded, 16)
    for n in rows_of:
        sp.dma_start(rows_of[n][:], d[f"c1_{n}"].partition_broadcast(KP)).then_inc(loaded, 16)
    sp.dma_start(rs[:], d["c1_scale"].partition_broadcast(TP)).then_inc(loaded, 16)
    sp.dma_start(mask_i[:], d["mask"]).then_inc(loaded, 16)
    return 7 + 5 + len(rows_of)


def expert_weights(nc, ctx, k):
    sb = lambda n, sh: ctx.enter_context(nc.sbuf_tensor(n, sh, F32))
    k.experts = (sb("f1_wr", [128, C2, E]), sb("f1_wgu", [128, 2, C2, E * F]), sb("f1_sgu", [128, 2, C2, FS]),
                 sb("f1_wd", [128, EC + SC, D]))


def load_experts(sp, k, d, loaded):
    wr, wgu, sgu, wd = k.experts
    sp.dma_start(wr[:], d["f1_wr"].rearrange("(c p) n -> p c n", p=128)).then_inc(loaded, 16)
    for i in range(2):
        sp.dma_start(wgu[:, i], d["f1_Wgu"][i].rearrange("(c p) n -> p c n", p=128)).then_inc(loaded, 16)
        sp.dma_start(sgu[:, i], d["f1_Sgu"][i].rearrange("(c p) n -> p c n", p=128)).then_inc(loaded, 16)
    sp.dma_start(wd[:, 0:EC, :], d["f1_Wd"].rearrange("(c p) n -> p c n", p=128)).then_inc(loaded, 16)
    for n in range(EC, EC + SC):
        at = (n - EC) * 128
        sp.dma_start(wd[0:size(n), n, :], d["f1_Sd"][at:at + size(n), :]).then_inc(loaded, 16)


EXPERT_LOADS = 6 + SC


def layer1_experts(nc, k, d):
    with ExitStack() as ctx:
        sb = lambda n, sh, dt=F32: ctx.enter_context(nc.sbuf_tensor(n, sh, dt))
        wr, wgu, sgu, wd = k.experts
        gates = sb("f1_gates", [TP, TT, E])
        gates_T = sb("f1_gatesT", [E, TOKENS])
        select = sb("f1_select", [E, E * F])
        silu = sb("f1_silu", [128, 2, TOKENS])
        mid = sb("f1_mid", [128, TOKENS])
        inner = sb("f1_inner", [128, 2, TOKENS])
        ps = ctx.enter_context(nc.psum_tensor("f1_ps", [128, 8, 512], F32))
        s = k.sems("f1", "logits shifted exp gates gT gT_sb sel select up silu mid inner down link "
                   "out " + NORM_SEMS)
        logits = ps[0:TP, 0, 0:TT * E].rearrange("p (t e) -> p t e", e=E)
        y = ps[0:TP, 6:8, :].rearrange("p b (t n) -> p (b t) n", n=D)
        with nc.Block() as block:

            @block.sync
            def _(sp):
                sp.wait_ge(s["x_ready"], 1)
                sp.dma_start(d["out"].rearrange("(t p) n -> p t n", p=TP), k.x_tok[:]).then_inc(s["out"], 16)
                sp.wait_ge(s["out"], 16)

            @block.gpsimd
            def _(pool):
                nc.gpsimd.memset(select[:], 1.0).then_inc(s["sel"], 1)
                pool.wait_ge(s["sel"], 1)
                nc.gpsimd.affine_select(out=select[:], in_=select[:], compare_op=ALU.is_ge, fill=0.0, base=0,
                                        pattern=[[1, E * F]], channel_multiplier=-F).then_inc(s["sel"], 1)
                pool.wait_ge(s["sel"], 2)
                nc.gpsimd.affine_select(out=select[:], in_=select[:], compare_op=ALU.is_ge, fill=0.0, base=F - 1,
                                        pattern=[[-1, E * F]], channel_multiplier=F).then_inc(s["select"], 1)

            @block.tensor
            def _(pe):
                for t in range(TT):
                    for c in range(C2):
                        last = nc.tensor.matmul(logits[:, t, :], k.x_T[:, c, t * TP:(t + 1) * TP], wr[:, c, :],
                                                start=(c == 0), stop=(c == C2 - 1))
                last.then_inc(s["logits"], 1)

                def up(n):
                    if n < 2:
                        pe.wait_ge(s["shifted"], 1)
                    else:
                        pe.wait_ge(s["inner"], n - 1)
                    of = sgu if n >= EC else wgu
                    at = (n - EC if n >= EC else n) * 128
                    for i in range(2):
                        for c in range(C2):
                            last = nc.tensor.matmul(ps[0:size(n), 2 * i + n % 2, 0:TOKENS],
                                                    of[:, i, c, at:at + size(n)], k.x_T[:, c, :],
                                                    start=(c == 0), stop=(c == C2 - 1))
                    if n < EC:
                        if n == 0:
                            pe.wait_ge(s["gates"], 1)
                            for t in range(TT):
                                tr = nc.tensor.transpose(ps[0:E, 5, t * TP:(t + 1) * TP], gates[:, t, :],
                                                         k.ident[0:TP, 0:TP])
                            tr.then_inc(s["gT"], 1)
                            pe.wait_ge(s["gT_sb"], 1)
                            pe.wait_ge(s["select"], 1)
                        last = nc.tensor.matmul(ps[:, 4 + n % 2, 0:TOKENS], select[:, at:at + 128], gates_T[:],
                                                start=True, stop=True)
                    last.then_inc(s["up"], 1)

                def down(n):
                    pe.wait_ge(s["inner"], n + 1)
                    for t in range(TT):
                        last = nc.tensor.matmul(y[:, t, :], inner[0:size(n), n % 2, t * TP:(t + 1) * TP],
                                                wd[0:size(n), n, :], start=(n == 0 and t % 2 == 0), stop=True,
                                                skip_group_check=True)
                    last.then_inc(s["down"], 1)

                for n in range(EC + SC):
                    up(n)
                    if n >= 1:
                        down(n - 1)
                down(EC + SC - 1)

            @block.scalar
            def _(act):
                act.wait_ge(s["shifted"], 1)
                nc.scalar.activation(k.route[:, :, 8:16], k.route[:, :, 0:8], ACT.Exp).then_inc(s["exp"], 1)
                act.wait_ge(s["gT"], 1)
                nc.scalar.activation(gates_T[:], ps[0:E, 5, 0:TOKENS], ACT.Copy).then_inc(s["gT_sb"], 1)
                for n in range(EC + SC):
                    act.wait_ge(s["up"], n + 1)
                    if n >= 2:
                        act.wait_ge(s["inner"], n - 1)
                    nc.scalar.activation(silu[0:size(n), n % 2, :], ps[0:size(n), n % 2, 0:TOKENS], ACT.Silu)\
                        .then_inc(s["silu"], 1)
                act.wait_ge(s["var_ready"], 1)
                nc.scalar.activation(k.std[:], k.mv[:, :, 1], ACT.Sqrt, bias=EPS).then_inc(s["std_ready"], 1)

            @block.vector
            def _(dve):
                link = linker(dve, s["link"])
                link(nc.vector.tensor_copy(k.res[:], k.x_tok[:]))
                dve.wait_ge(s["logits"], 1)
                route_shift(nc, link, k, logits, s["shifted"])
                dve.wait_ge(s["exp"], 1)
                route_choose(nc, link, k, gates[:], False, s["gates"])
                for n in range(EC + SC):
                    r = size(n)
                    dve.wait_ge(s["silu"], n + 1)
                    if n >= 2:
                        dve.wait_ge(s["down"], n - 1)
                    if 1 <= n < EC:
                        dve.wait_ge(s["inner"], n)
                    to = mid[0:r, :] if n < EC else inner[0:r, n % 2, :]
                    nc.vector.tensor_tensor(to, silu[0:r, n % 2, :], ps[0:r, 2 + n % 2, 0:TOKENS], ALU.mult)\
                        .then_inc(s["mid"] if n < EC else s["inner"], 1)
                    if n < EC:
                        dve.wait_ge(s["mid"], n + 1)
                        nc.vector.tensor_tensor(inner[:, n % 2, :], mid[:], ps[:, 4 + n % 2, 0:TOKENS], ALU.mult)\
                            .then_inc(s["inner"], 1)
                dve.wait_ge(s["down"], EC + SC)
                norm_vector(nc, dve, link, k, s, y)


def program(nc, k, d, phases=99):
    ctx = k.ctx
    sb = lambda n, sh, dt=F32: ctx.enter_context(nc.sbuf_tensor(n, sh, dt))
    k.x_tok = sb("x_tok", [TP, TT, D])
    k.x_T = sb("x_T", [128, C2, TOKENS])
    k.res = sb("res", [TP, TT, D])
    k.sum = sb("sum", [TP, TT, D])
    k.stats = sb("stats", [TP, TT, 6])
    k.mv = sb("mv", [TP, TT, 2])
    k.std = sb("std", [TP, TT])
    k.rstd = sb("rstd", [TP, TT])
    k.shared_w = sb("shared_w", [128, 4 * D])
    k.shared_rows = sb("shared_rows", [KP, D])
    k.kv_w = k.shared_w[:].rearrange("p (c n) -> p c n", c=C2)
    k.kv_bias_rows = k.shared_rows[0:3, :].bitcast(BF16)
    k.ident = sb("ident", [128, 128])
    k.ident_b = sb("ident_b", [128, 128], BF16)
    k.route = sb("route", [TP, TT, 37])
    k.route_at = sb("route_at", [TP, TT, 8], U32)
    k.route_idx = sb("route_idx", [TP, TT, 8])
    k.expert_i = sb("expert_i", [TP, E], I32)
    k.expert = sb("expert", [TP, E])
    k.head_mask = sb("head_mask", [128, 8])
    k.q_parts = nc.dram_tensor("q_parts", (3, D, TOKENS), BF16).ap()
    k.k_parts = nc.dram_tensor("k_parts", (3, D, KEYS), BF16).ap()
    k.k1_T = nc.dram_tensor("k1_T", (D, KEYS), F32).ap()
    k.v1 = nc.dram_tensor("v1", (KEYS, H * (HD + 1)), F32).ap()
    sublayers = [layer0_attention, layer0_context, layer0_query, layer0_cross_attention, layer0_mlp,
                 layer1_attention, layer1_cross_attention, layer1_experts]
    with ExitStack() as cross, ExitStack() as own:
        for n, sublayer in enumerate(sublayers[:phases]):
            if n == 1:
                k.v_steps = cross.enter_context(nc.sbuf_tensor("v_steps", [KP, KT, D], BF16))
                k.v_scale = cross.enter_context(nc.sbuf_tensor("v_scale", [KP, D], F32))
            if n == 2:
                k.kx = cross.enter_context(nc.sbuf_tensor("kx", [128, 3, KEYS], BF16))
                k.kx_loaded = k.sem("kx_loaded")
            if n == 4:
                cross.close()
                attention_weights(nc, ctx, own, k)
            if n == 6:
                own.close()
                expert_weights(nc, ctx, k)
            if n in (4, 7):
                k.renew_sems()
            sublayer(nc, k, d)


def build(nc, arrays, phases=99):
    d = {n: nc.dram_tensor(f"in_{n}", v.shape, mybir.dt.from_np(v.dtype), kind="ExternalInput").ap()
         for n, v in arrays.items()}
    d["out"] = nc.dram_tensor("out", (TOKENS, D), F32, kind="ExternalOutput").ap()
    with ExitStack() as ctx:
        program(nc, Core(nc, ctx), d, phases)


def layout(inputs):
    a = {n: np.asarray(v) for n, v in inputs.items()}
    chunked = lambda b: b.reshape(-1, 128).T
    x = a["x"].reshape(TOKENS, D)
    gu = a["L1_ffn_gate_up_weights"]
    out = {
        "x": x, "x_T": x.T, "ctx_T": a["ctx_2048"].reshape(KEYS, D).T,
        "mask": a["mask_BxS2_ik0"].reshape(KT, KP).T,
        "a0_Wq": a["L0_attn_Wq"], "a0_Wk": a["L0_attn_Wk"], "a0_Wv": a["L0_attn_Wv"], "a0_Wo": a["L0_attn_Wo"],
        "a0_bqk": np.stack([chunked(a["L0_attn_bq"]), chunked(a["L0_attn_bk"])], 1),
        "a0_bv": a["L0_attn_bv"], "a0_bo": a["L0_attn_bo"],
        "c0_Wq": a["L0_xattn_Wq"], "c0_bq": a["L0_xattn_bq"],
        "c0_Wkv": a["L0_xattn_Wkv"], "c0_bkv": a["L0_xattn_bkv"].reshape(1, 2 * D),
        "c0_Wp": a["L0_xattn_Wp"], "c0_bp": a["L0_xattn_bp"],
        "f0_w1": a["L0_ffn_w1"].T, "f0_w3": a["L0_ffn_w3"].T, "f0_w2": a["L0_ffn_w2"].T, "f0_wr": a["L0_ffn_wr"].T,
        "a1_Wqkv": np.stack([a["L1_attn_Wq"], a["L1_attn_Wk"], a["L1_attn_Wv"]]), "a1_Wo": a["L1_attn_Wo"],
        "a1_bqk": np.stack([chunked(a["L1_attn_bq"]), chunked(a["L1_attn_bk"])], 1),
        "a1_bv": a["L1_attn_bv"], "a1_bo": a["L1_attn_bo"],
        "c1_W": np.stack([a["L1_xattn_" + n].T for n in ("Wq", "Wk", "Wv", "Wo")]),
        "c1_bqk": np.stack([chunked(a["L1_xattn_bq"]), chunked(a["L1_xattn_bk"])], 1),
        "c1_bv": a["L1_xattn_bv"], "c1_bo": a["L1_xattn_bo"],
        "c1_gamma": a["L1_xattn_ln_gamma"], "c1_beta": a["L1_xattn_ln_beta"],
        "c1_scale": a["L1_xattn_residual_scale"].reshape(1),
        "f1_wr": a["L1_ffn_gate_weight"].T,
        "f1_Wgu": np.stack([gu[:, :F].reshape(E * F, D).T, gu[:, F:].reshape(E * F, D).T]),
        "f1_Wd": a["L1_ffn_down_weights"].transpose(0, 2, 1).reshape(E * F, D),
        "f1_Sgu": np.stack([a["L1_ffn_shared_gate_up"][:FS].T, a["L1_ffn_shared_gate_up"][FS:].T]),
        "f1_Sd": a["L1_ffn_shared_down"].T,
    }
    return {n: np.ascontiguousarray(v) for n, v in out.items()}


def kernel(**inputs):
    import concourse.bacc as bacc
    from concourse.bass_utils import run_bass_kernel_spmd

    arrays = layout(inputs)
    nc = bacc.Bacc("TRN2", target_bir_lowering=False, num_devices=1)
    build(nc, arrays)
    r = run_bass_kernel_spmd(nc, [{f"in_{n}": v for n, v in arrays.items()}], core_ids=[0])
    return r.results[0]["out"].reshape(B, T, D)
```
